# Optimizing a Trainium2 kernel written in Bass

```python
import numpy as np
import jax
import jax.numpy as jnp

def _softmax(x, axis=-1):
    return jax.nn.softmax(x, axis=axis)

def _gelu(x):
    return jax.nn.gelu(x, approximate=True)

def _silu(x):
    return jax.nn.silu(x)

def _sigmoid(x):
    return jax.nn.sigmoid(x)

def _layernorm(x, axis=-1, eps=1e-05):
    m = jnp.mean(x, axis=axis, keepdims=True)
    v = jnp.var(x, axis=axis, keepdims=True)
    return (x - m) / jnp.sqrt(v + eps)

def _scatter_add(tgt, idx, src, axis=0):
    return tgt.at[idx].add(src)

def _segment_sum(src, seg, n):
    return jax.ops.segment_sum(src, seg, n)
kernel_name = 'mk_adaln_d1_jaxref_r4_ac8eb7'

def setup_inputs(seed: int=0):
    np.random.seed(seed)
    _w = jnp.asarray

    def _L0_attn_setup():
        import jax, jax.numpy as jnp
        import numpy as np
        DIM = 256
        STATE = 64
        HEADS = 8
        EXPAND = 2
        INNER = DIM * EXPAND
        HEAD_DIM = INNER // HEADS
        KERNEL = 4
        B, L = (2, 512)
        EPS = 1e-05

        def _causal_conv(x, conv_w, conv_b):
            x_pad = jnp.pad(x, ((0, 0), (KERNEL - 1, 0), (0, 0)))
            w = conv_w[:, 0, :]
            y = sum((x_pad[:, k:k + x.shape[1], :] * w[:, k] for k in range(KERNEL)))
            return y + conv_b

        def _ssd_scan(x, b, c, dt, a):
            state0 = jnp.zeros((x.shape[0], HEADS, STATE, HEAD_DIM), x.dtype)

            def step(state, inp):
                x_t, b_t, c_t, dt_t = inp
                decay = jnp.exp(dt_t * a)[..., None, None]
                b_bar = dt_t[..., None] * b_t
                state = decay * state + b_bar[..., None] * x_t[:, :, None, :]
                y_t = jnp.einsum('bhn,bhnp->bhp', c_t, state)
                return (state, y_t)
            xs = (x.transpose(1, 0, 2, 3), b.transpose(1, 0, 2, 3), c.transpose(1, 0, 2, 3), dt.transpose(1, 0, 2))
            _, ys = jax.lax.scan(step, state0, xs)
            return ys.transpose(1, 0, 2, 3)
        key = jax.random.key(seed)
        ks = jax.random.split(key, 12)
        s = 0.02
        return {'input_tensor': jax.random.normal(ks[0], (B, L, DIM), jnp.float32), 'Wx': jax.random.normal(ks[1], (INNER, DIM), jnp.float32) * s, 'Wz': jax.random.normal(ks[2], (INNER, DIM), jnp.float32) * s, 'conv_w': jax.random.normal(ks[3], (INNER, 1, KERNEL), jnp.float32) * s, 'conv_b': jnp.zeros((INNER,), jnp.float32), 'Wb': jax.random.normal(ks[4], (HEADS * STATE, INNER), jnp.float32) * s, 'Wc': jax.random.normal(ks[5], (HEADS * STATE, INNER), jnp.float32) * s, 'Wdt': jax.random.normal(ks[6], (HEADS, INNER), jnp.float32) * s, 'b_dt': jnp.zeros((HEADS,), jnp.float32), 'log_a': jnp.log(jnp.full((HEADS,), 0.5, jnp.float32)), 'd_param': jnp.ones((HEADS,), jnp.float32), 'gn_w': jnp.ones((INNER,), jnp.float32), 'gn_b': jnp.zeros((INNER,), jnp.float32), 'Wout': jax.random.normal(ks[7], (DIM, INNER), jnp.float32) * s}
    _L0_attn_in = _L0_attn_setup()

    def _L0_ffn_setup():
        import jax, jax.numpy as jnp
        import numpy as np
        B, S, D, H, F = (4, 1024, 256, 16, 1024)
        CAP = 0.125
        ROPE_BASE = 10000.0

        def rmsnorm(x, g):
            return x * jax.lax.rsqrt(jnp.mean(x * x, -1, keepdims=True) + 1e-06) * g

        def rope(t, pos):
            hd = t.shape[-1]
            inv = 1.0 / ROPE_BASE ** (jnp.arange(0, hd, 2, dtype=jnp.float32) / hd)
            f = pos[:, None, :, None].astype(jnp.float32) * inv
            emb = jnp.concatenate([f, f], axis=-1)
            cos, sin = (jnp.cos(emb), jnp.sin(emb))
            rot = jnp.concatenate([-t[..., hd // 2:], t[..., :hd // 2]], axis=-1)
            return t * cos + rot * sin
        key = jax.random.key(seed)
        ks = jax.random.split(key, 9)
        scale = 0.02
        x = jax.random.normal(ks[0], (B, S, D), jnp.float32)
        causal = jnp.where(jnp.tril(jnp.ones((S, S), bool)), 0.0, -1000000000.0).astype(jnp.float32)
        attention_mask = jnp.broadcast_to(causal[None, None], (B, 1, S, S))
        position_ids = jnp.broadcast_to(jnp.arange(S, dtype=jnp.int32), (B, S))
        return {'x': x, 'attention_mask': attention_mask, 'position_ids': position_ids, 'router_w': jax.random.normal(ks[1], (D, 1), jnp.float32) * scale, 'router_b': jnp.zeros((1,), jnp.float32), 'wq': jax.random.normal(ks[2], (D, D), jnp.float32) * scale, 'wk': jax.random.normal(ks[3], (D, D), jnp.float32) * scale, 'wv': jax.random.normal(ks[4], (D, D), jnp.float32) * scale, 'wo': jax.random.normal(ks[5], (D, D), jnp.float32) * scale, 'w1': jax.random.normal(ks[6], (D, F), jnp.float32) * scale, 'w2': jax.random.normal(ks[7], (F, D), jnp.float32) * scale, 'ln1': jnp.ones((D,), jnp.float32), 'ln2': jnp.ones((D,), jnp.float32)}
    _L0_ffn_in = _L0_ffn_setup()
    _L0_c = _w((lambda *s: np.random.randn(*s).astype(np.float32) * 0.05)(8, 256))
    _L0_wmod = _w((lambda *s: np.random.randn(*s).astype(np.float32) * 0.05)(256, 6 * 256) * 256 ** (-0.5))
    _d = {'L0_attn_input_tensor': _L0_attn_in['input_tensor'], 'L0_attn_Wx': _L0_attn_in['Wx'], 'L0_attn_Wz': _L0_attn_in['Wz'], 'L0_attn_conv_w': _L0_attn_in['conv_w'], 'L0_attn_conv_b': _L0_attn_in['conv_b'], 'L0_attn_Wb': _L0_attn_in['Wb'], 'L0_attn_Wc': _L0_attn_in['Wc'], 'L0_attn_Wdt': _L0_attn_in['Wdt'], 'L0_attn_b_dt': _L0_attn_in['b_dt'], 'L0_attn_log_a': _L0_attn_in['log_a'], 'L0_attn_d_param': _L0_attn_in['d_param'], 'L0_attn_gn_w': _L0_attn_in['gn_w'], 'L0_attn_gn_b': _L0_attn_in['gn_b'], 'L0_attn_Wout': _L0_attn_in['Wout'], 'L0_ffn_attention_mask': _L0_ffn_in['attention_mask'], 'L0_ffn_position_ids': _L0_ffn_in['position_ids'], 'L0_ffn_router_w': _L0_ffn_in['router_w'], 'L0_ffn_router_b': _L0_ffn_in['router_b'], 'L0_ffn_wq': _L0_ffn_in['wq'], 'L0_ffn_wk': _L0_ffn_in['wk'], 'L0_ffn_wv': _L0_ffn_in['wv'], 'L0_ffn_wo': _L0_ffn_in['wo'], 'L0_ffn_w1': _L0_ffn_in['w1'], 'L0_ffn_w2': _L0_ffn_in['w2'], 'L0_ffn_ln1': _L0_ffn_in['ln1'], 'L0_ffn_ln2': _L0_ffn_in['ln2'], 'L0_c': _L0_c, 'L0_wmod': _L0_wmod}
    _x0 = _d['L0_attn_input_tensor']
    _d['L0_attn_input_tensor'] = jax.random.normal(jax.random.fold_in(jax.random.key(seed), 1), (8, 1024, 256), dtype=_x0.dtype)
    del _x0
    return _d

def reference(L0_attn_input_tensor, L0_attn_Wx, L0_attn_Wz, L0_attn_conv_w, L0_attn_conv_b, L0_attn_Wb, L0_attn_Wc, L0_attn_Wdt, L0_attn_b_dt, L0_attn_log_a, L0_attn_d_param, L0_attn_gn_w, L0_attn_gn_b, L0_attn_Wout, L0_ffn_attention_mask, L0_ffn_position_ids, L0_ffn_router_w, L0_ffn_router_b, L0_ffn_wq, L0_ffn_wk, L0_ffn_wv, L0_ffn_wo, L0_ffn_w1, L0_ffn_w2, L0_ffn_ln1, L0_ffn_ln2, L0_c, L0_wmod):

    def _L0_attn_ref(input_tensor, Wx, Wz, conv_w, conv_b, Wb, Wc, Wdt, b_dt, log_a, d_param, gn_w, gn_b, Wout):
        import jax, jax.numpy as jnp
        import numpy as np
        DIM = 256
        STATE = 64
        HEADS = 8
        EXPAND = 2
        INNER = DIM * EXPAND
        HEAD_DIM = INNER // HEADS
        KERNEL = 4
        B, L = (2, 512)
        EPS = 1e-05

        def _causal_conv(x, conv_w, conv_b):
            x_pad = jnp.pad(x, ((0, 0), (KERNEL - 1, 0), (0, 0)))
            w = conv_w[:, 0, :]
            y = sum((x_pad[:, k:k + x.shape[1], :] * w[:, k] for k in range(KERNEL)))
            return y + conv_b

        def _ssd_scan(x, b, c, dt, a):
            state0 = jnp.zeros((x.shape[0], HEADS, STATE, HEAD_DIM), x.dtype)

            def step(state, inp):
                x_t, b_t, c_t, dt_t = inp
                decay = jnp.exp(dt_t * a)[..., None, None]
                b_bar = dt_t[..., None] * b_t
                state = decay * state + b_bar[..., None] * x_t[:, :, None, :]
                y_t = jnp.einsum('bhn,bhnp->bhp', c_t, state)
                return (state, y_t)
            xs = (x.transpose(1, 0, 2, 3), b.transpose(1, 0, 2, 3), c.transpose(1, 0, 2, 3), dt.transpose(1, 0, 2))
            _, ys = jax.lax.scan(step, state0, xs)
            return ys.transpose(1, 0, 2, 3)
        bsz, seq, _ = input_tensor.shape
        x = input_tensor @ Wx.T
        z = input_tensor @ Wz.T
        x = _causal_conv(x, conv_w, conv_b)
        x = jax.nn.silu(x)
        b = (x @ Wb.T).reshape(bsz, seq, HEADS, STATE)
        c = (x @ Wc.T).reshape(bsz, seq, HEADS, STATE)
        dt = jax.nn.softplus(x @ Wdt.T + b_dt)
        xh = x.reshape(bsz, seq, HEADS, HEAD_DIM)
        a = -jnp.exp(log_a)
        y = _ssd_scan(xh, b, c, dt, a)
        y = y + d_param[None, None, :, None] * xh
        yg = y
        mean = yg.mean(axis=(1, 3), keepdims=True)
        var = yg.var(axis=(1, 3), keepdims=True)
        yn = (yg - mean) / jnp.sqrt(var + EPS)
        yn = yn * gn_w.reshape(1, 1, HEADS, HEAD_DIM) + gn_b.reshape(1, 1, HEADS, HEAD_DIM)
        yn = yn.reshape(bsz, seq, INNER)
        out = yn * jax.nn.silu(z)
        return out @ Wout.T

    def _L0_ffn_ref(x, attention_mask, position_ids, router_w, router_b, wq, wk, wv, wo, w1, w2, ln1, ln2):
        import jax, jax.numpy as jnp
        import numpy as np
        B, S, D, H, F = (4, 1024, 256, 16, 1024)
        CAP = 0.125
        ROPE_BASE = 10000.0

        def rmsnorm(x, g):
            return x * jax.lax.rsqrt(jnp.mean(x * x, -1, keepdims=True) + 1e-06) * g

        def rope(t, pos):
            hd = t.shape[-1]
            inv = 1.0 / ROPE_BASE ** (jnp.arange(0, hd, 2, dtype=jnp.float32) / hd)
            f = pos[:, None, :, None].astype(jnp.float32) * inv
            emb = jnp.concatenate([f, f], axis=-1)
            cos, sin = (jnp.cos(emb), jnp.sin(emb))
            rot = jnp.concatenate([-t[..., hd // 2:], t[..., :hd // 2]], axis=-1)
            return t * cos + rot * sin
        b, s, d = x.shape
        hd = d // H
        weights = (x @ router_w)[..., 0] + router_b[0]
        k = int(CAP * s)
        topv, topi = jax.lax.top_k(weights, k)
        thr = topv[:, -1]
        sel_mask = (weights > thr[:, None]).astype(x.dtype)
        kc = k - 1
        sel_idx = jnp.sort(topi[:, :kc], axis=1)
        bidx = jnp.arange(b)[:, None]
        x_sel = x[bidx, sel_idx]
        pos_sel = position_ids[bidx, sel_idx]
        w_sel = weights[bidx, sel_idx]
        m = attention_mask[:, 0]
        m_sel = m[bidx[:, :, None], sel_idx[:, :, None], sel_idx[:, None, :]]
        hn = rmsnorm(x_sel, ln1)

        def heads(t):
            return t.reshape(b, kc, H, hd).transpose(0, 2, 1, 3)
        q = rope(heads(hn @ wq), pos_sel)
        kk = rope(heads(hn @ wk), pos_sel)
        v = heads(hn @ wv)
        sc = jnp.einsum('bhqd,bhkd->bhqk', q, kk) / np.sqrt(hd).astype(np.float32)
        sc = sc + m_sel[:, None]
        a = jax.nn.softmax(sc, axis=-1)
        o = jnp.einsum('bhqk,bhkd->bhqd', a, v).transpose(0, 2, 1, 3).reshape(b, kc, d) @ wo
        x1 = x_sel + o
        x2 = x1 + jax.nn.gelu(rmsnorm(x1, ln2) @ w1) @ w2
        proc = x2 * w_sel[..., None]
        out = jnp.zeros_like(x).at[bidx, sel_idx].set(proc)
        return out + x * (1.0 - sel_mask)[..., None]
    x = L0_attn_input_tensor
    mod = (_silu(L0_c) @ L0_wmod).reshape(L0_c.shape[0], 6, 1, -1)
    sa, ca, ga, sb, cb, gb = (mod[:, 0], mod[:, 1], mod[:, 2], mod[:, 3], mod[:, 4], mod[:, 5])
    ga = (2 * (ga >= 0) - 1) * jnp.maximum(jnp.abs(ga), 0.25)
    gb = (2 * (gb >= 0) - 1) * jnp.maximum(jnp.abs(gb), 0.25)
    h = _layernorm(x, axis=-1) * (1 + ca) + sa
    x = x + ga * _L0_attn_ref(h, L0_attn_Wx, L0_attn_Wz, L0_attn_conv_w, L0_attn_conv_b, L0_attn_Wb, L0_attn_Wc, L0_attn_Wdt, L0_attn_b_dt, L0_attn_log_a, L0_attn_d_param, L0_attn_gn_w, L0_attn_gn_b, L0_attn_Wout)
    h = _layernorm(x, axis=-1) * (1 + cb) + sb
    x = x + gb * _L0_ffn_ref(h, L0_ffn_attention_mask, L0_ffn_position_ids, L0_ffn_router_w, L0_ffn_router_b, L0_ffn_wq, L0_ffn_wk, L0_ffn_wv, L0_ffn_wo, L0_ffn_w1, L0_ffn_w2, L0_ffn_ln1, L0_ffn_ln2)
    return x

_drawn_inputs = setup_inputs


def setup_inputs(seed=0):
    import zlib

    import numpy as np

    out = dict(_drawn_inputs(seed))
    spreads = {'L0_attn_conv_b': (0.0, 0.308),
     'L0_attn_b_dt': (0.0, 0.8),
     'L0_attn_log_a': (-0.6931471824645996, 0.6),
     'L0_attn_d_param': (1.0, 0.6),
     'L0_attn_gn_w': (1.0, 0.6),
     'L0_attn_gn_b': (0.0, 0.8),
     'L0_ffn_ln1': (1.0, 0.6),
     'L0_ffn_ln2': (1.0, 0.6)}
    factors = {'L0_attn_Wx': 8.0,
     'L0_attn_Wz': 2.741,
     'L0_attn_conv_w': 8.0,
     'L0_attn_Wb': 8.0,
     'L0_attn_Wc': 8.0,
     'L0_attn_Wdt': 8.0,
     'L0_attn_Wout': 2.705,
     'L0_ffn_wq': 8.0,
     'L0_ffn_wk': 8.0,
     'L0_ffn_wv': 8.0,
     'L0_ffn_wo': 8.0,
     'L0_ffn_w1': 8.0,
     'L0_ffn_w2': 8.0}
    for name, (base, spread) in spreads.items():
        noise = np.random.default_rng([zlib.crc32(name.encode()), seed]).standard_normal(out[name].shape)
        drawn = base * np.exp(spread * noise) if base else spread * noise
        out[name] = jnp.asarray(drawn.astype(out[name].dtype))
    for name, factor in factors.items():
        out[name] = (out[name] * factor).astype(out[name].dtype)
    return out
```

```python
from contextlib import ExitStack

import concourse.bass as bass
from concourse import mybir
from concourse.alu_op_type import AluOpType as ALU

F32 = mybir.dt.float32
BF16 = mybir.dt.bfloat16
I32 = mybir.dt.int32
U32 = mybir.dt.uint32
ACT = mybir.ActivationFunctionType
AX = mybir.AxisListType

P = 128
NB, L, D = 8, 1024, 256
MB = 4
INNER, HEADS, STATE, TAPS = 512, 8, 64, 4
T = L // P
KD, KC = D // P, INNER // P
HALF = L // 2
G3 = 6
RW = G3 * HEADS
FH, HD, F = 16, 16, 1024
KSEL = L // 8
NSEL = KSEL - 1
FT = F // P
EPS = 1e-5
MASKED = -1e30
ROPE_BASE = 10000.0
PI = 3.141592653589793
ROUND = 12582912.0
TWO_PI = (6.28125, 0.0019352436065673828, 6.35732715934e-08)
SD_MOD, SD_MIX, SD_ALL = 10, 14, 18
SP_ALL = 65
CHAINS = {"A": 2, "V": 13, "D": 14, "S": 3, "G": 16, "R": 29, "O": 16}


PER_BATCH = {}


def at(sem, b, k):
    return b * PER_BATCH[id(sem)] + k


def later(b):
    return not isinstance(b, int) or b > 0


class Chain:

    def __init__(self, sem, name):
        self.sem, self.name, self.k = sem, name, 0

    def __call__(self, eng, b, ins):
        ins.then_inc(self.sem, 1)
        self.k += 1
        eng.wait_ge(self.sem, at(self.sem, b, self.k))

    def end(self):
        assert self.k == CHAINS[self.name], (self.name, self.k)
        self.k = 0


class Ring:

    def __init__(self, banks, filled, drained):
        self.banks, self.filled, self.drained = banks, filled, drained

    def bank(self, q):
        return self.banks[q % 4]

    def full(self, b, q):
        return self.filled[q % 4], at(self.filled[q % 4], b, q // 4 + 1)

    def read(self, b, q):
        return self.drained[q % 4], at(self.drained[q % 4], b, q // 4 + 1)


def adaln_block(nc, x, wxT, wzT, wbT, wcT, wdtT, woT, cols, rows48, mask, pos, rw, rb,
                wqkv, wo, w1, w2, lncols, cT, wmod, out):
    ctx = ExitStack()
    with ctx:
        def sb(name, shape, dt=F32):
            return ctx.enter_context(nc.sbuf_tensor(name, shape, dt))

        def chunk(c):
            return slice((c % 4) * P, (c % 4) * P + P)

        def sig(name, per=1):
            sem = ctx.enter_context(nc.semaphore(name))
            PER_BATCH[id(sem)] = per
            return sem

        mod_d = nc.dram_tensor("mod_scratch", (NB, 6 * D), F32, kind="Internal").ap()
        x1_d = nc.dram_tensor("x1_scratch", (L, D), F32, kind="Internal").ap()

        wx_s = sb("wx_s", [P, KD, INNER])
        wz_s = sb("wz_s", [P, KD, INNER])
        wb_s = sb("wb_s", [P, KC, INNER])
        wc_s = sb("wc_s", [P, KC, INNER])
        wdt_s = sb("wdt_s", [P, KC, RW])
        wo_s = sb("wo_s", [P, KC, D])
        wqkv_s = sb("wqkv_s", [P, KD, 3 * D])
        fwo_s = sb("fwo_s", [P, KD, D])
        w1_s = sb("w1_s", [P, KD, F])
        w2_s = sb("w2_s", [P, FT, D])
        cols_s = sb("cols_s", [P, KC, 8])
        ln_s = sb("ln_s", [P, 2, KD])
        r48_s = sb("r48_s", [RW, 2])
        rw_s = sb("rw_s", [P, D])
        rb_s = sb("rb_s", [P, 1])
        ident = sb("ident", [P, P])
        identb = sb("identb", [P, P], BF16)
        causal = sb("causal", [P, 4, P], BF16)
        ones_b = sb("ones_b", [P, 1], BF16)
        tri = sb("tri", [P, P])
        halfmean = sb("halfmean", [P, P])
        iota_r = sb("iota_r", [P, P])
        tok = sb("tok", [P, T])
        ones4 = sb("ones4", [P, KC, T])
        spare = sb("spare", [P, 4])
        mhalf = sb("mhalf", [P, T])
        gmask = sb("gmask", [RW, 8])
        gneg = sb("gneg", [RW, 1])
        delta = sb("delta", [RW, HEADS])
        selp = sb("selp", [RW, 4, P], BF16)
        reset = sb("reset", [RW, T, P], BF16)
        aneg = sb("aneg", [RW, 1])
        invf = sb("invf", [P, 2, HD // 2])
        phase = sb("phase", [P, 2, 2, HD // 2])
        mcol = sb("mcol", [P, 4, NB])
        mc = sb("mc", [P, 4])
        modrow = sb("modrow", [P, 4, D])
        xr = sb("xr", [P, T, D])
        hT = sb("hT", [P, KD, L])
        xc = sb("xc", [P, KC * (L + TAPS - 1) + 4])
        xT = sb("xT", [P, KC, L])
        zs = sb("zs", [P, KC, L])
        BT = sb("BT", [P, 2, KC, HALF])
        CT = sb("CT", [P, 2, KC, HALF])
        EC = sb("EC", [P, KC * L])
        Lw = sb("Lw", [RW, L], BF16)
        dw = sb("dw", [P, T, 2 * HEADS])
        dec = sb("dec", [P, KC, T])
        st6 = sb("st6", [P, T, 6])
        mv = sb("mv", [P, T, 2])
        rstd = sb("rstd", [P, T])
        Sbd = sb("Sbd", [P, KC, P])
        Sdc = sb("Sdc", [P, KC, P])
        Eg = sb("Eg", [P, 2 * HALF])
        Mt = sb("Mt", [P, 2, 2 * HALF])
        XB = sb("XB", [P, 2, 2, INNER])
        yst = sb("yst", [P, KC, 12])
        ymv = sb("ymv", [P, KC, 2])
        pk = sb("pk", [P, 4, KC])
        gab = sb("gab", [P, 6, KC])
        st6b = sb("st6b", [P, T, 6])
        mvb = sb("mvb", [P, T, 2])
        rstdb = sb("rstdb", [P, T])
        wcol = sb("wcol", [P, T])
        boff = sb("boff", [P, 1])
        moff = sb("moff", [P, 1])
        rank = sb("rank", [P, T])
        self_ = sb("self_", [P, 2])
        xidx = sb("xidx", [P, 1], U32)
        gidx = sb("gidx", [P, 1], U32)
        midx = sb("midx", [P, 1], U32)
        posi = sb("posi", [P, 1], I32)
        posf = sb("posf", [P, 1])
        sm = sb("sm", [P, 16])
        st1 = sb("st1", [P, 6])
        ang = sb("ang", [P, 2, HD // 2])
        trn = sb("trn", [P, 2, HD // 2])
        sc_ = sb("sc_", [P, 2, HD // 2])
        mx = sb("mx", [P, FH])
        den = sb("den", [P, FH])

        xcv = xc[:, 0:KC * (L + TAPS - 1)].rearrange("p (k n) -> p k n", k=KC)
        R8 = xc[0:RW, 0:4 * L].bitcast(BF16).rearrange("p (h n) -> p h n", h=HEADS)
        ECv = EC[:, :].rearrange("p (k n) -> p k n", k=KC)
        CT1 = CT[0:RW, 1, :, :].rearrange("p a b -> p (a b)")
        BT1 = BT[0:RW, 1, :, :].rearrange("p a b -> p (a b)").bitcast(BF16)
        v48, dt48 = CT1[:, 0:L], CT1[:, L:2 * L]
        Rw, lo = BT1[:, 0:L], BT1[:, L:2 * L]
        xin = zs[:, 0:2, :].rearrange("p a n -> p (a n)").rearrange("p (t n) -> p t n", t=T)
        h2 = EC[:, 0:T * D].rearrange("p (t n) -> p t n", t=T)
        wog_s = hT[:, 1, :].rearrange("p (k n) -> p k n", k=KC)
        a48 = hT[0:RW, 0, :]
        b48 = hT[0:RW, 1, :]
        hi = hT[0:RW, 1, 0:HALF].bitcast(BF16)
        mid = hT[0:RW, 1, HALF:L].bitcast(BF16)
        Gt = EC[:, :].bitcast(BF16).rearrange("p (t n) -> p t n", t=T)
        scr = EC[:, 0:2048].rearrange("p (h n) -> p h n", h=FH)
        AT = EC[:, 2048:4096].rearrange("p (h n) -> p h n", h=FH)
        qk = EC[:, 0:512]
        rt = EC[:, 512:1024]
        qkr = EC[:, 2048:3072].rearrange("p (s h n) -> p s h n", s=2, h=FH)
        qT = EC[:, 3072:3584].rearrange("p (m n) -> p m n", m=4)
        kT = EC[:, 3584:4096].rearrange("p (m n) -> p m n", m=4)
        wrow = Eg
        Pm = Mt[:, 0, :].rearrange("p (t n) -> p t n", t=T)
        mrows = Mt[:, 1, :]
        mT = XB[:, 0, :, :].rearrange("p a b -> p (a b)").rearrange("p (t n) -> p t n", t=T)
        gT = XB[:, 1, :, :].rearrange("p a b -> p (a b)").rearrange("p (t n) -> p t n", t=FT)
        xs, hs, hn, vs, ob, x1s, hnT_, oT_ = (xr[:, i, :] for i in range(8))
        hnT = hnT_.rearrange("p (k n) -> p k n", k=KD)
        oT = oT_.rearrange("p (k n) -> p k n", k=KD)
        msel = Sbd[:, 0, :]
        junk = Sdc[:, 0:2, :].rearrange("p a b -> p (a b)")
        junkf = Mt[:, 1, :]

        junkt = XB[:, 1, :, :].rearrange("p a b -> p (a b)")
        junkd = Mt[:, 0, 0:2 * D].rearrange("p (a n) -> p a n", a=2)
        mcin_s = sb("mcin_s", [P, KD, NB])
        mcin = mcin_s[:, :, :]
        wmod_s = BT[:, :, :, :].rearrange("p s k n -> p (s k n)")[:, 0:KD * 6 * D].rearrange("p (k n) -> p k n", k=KD)
        mod8 = CT[0:NB, 1, :, :].rearrange("p a n -> p (a n)")[:, 0:6 * D]
        sgn8, abs8 = EC[0:NB, L:L + D], EC[0:NB, L + D:L + 2 * D]
        dlt6 = EC[0:RW, 0:RW].rearrange("p (g h) -> p g h", g=G3)
        delt3 = sb("delt3", [RW, HEADS])

        ps = [ctx.enter_context(nc.psum_tensor(f"ps{i}", [P, 512], F32)) for i in range(8)]

        wload = ctx.enter_context(nc.semaphore("weights_loaded"))
        fload = ctx.enter_context(nc.semaphore("ffn_weights_loaded"))
        mload = ctx.enter_context(nc.semaphore("mod_inputs_loaded"))
        setup_pool = ctx.enter_context(nc.semaphore("setup_pool"))
        setup_dve = ctx.enter_context(nc.semaphore("setup_dve"))
        setup_act = ctx.enter_context(nc.semaphore("setup_act"))
        setup_pe = ctx.enter_context(nc.semaphore("setup_pe"))
        mod_stored = ctx.enter_context(nc.semaphore("mod_stored"))
        x_loaded = sig("x_loaded", 16)
        xr_loaded = sig("xr_loaded", 16)
        modrow_loaded = sig("modrow_loaded", 16)
        mc_ready = sig("mc_ready")
        var_ready = sig("var_ready")
        rstd_ready = sig("rstd_ready")
        xn_ready = sig("xn_ready", T)
        conv_ready = sig("conv_ready", 8)
        xT_ready = sig("xT_ready", 8)
        u_ready = sig("dt_u_ready")
        l_ready = sig("dt_log_ready", 2)
        dif_ready = sig("dif_ready")
        wexp_ready = sig("wexp_ready")
        rows_ready = sig("decay_rows_ready")
        v_ready = sig("v_ready")
        dec_ready = sig("dec_ready")
        CE_ready = sig("CE_ready", 8)
        cd_filled = sig("cumdiff_filled", 2 * T)
        Eg_ready = sig("decay_ready", 2 * T)
        sc_filled = sig("scores_filled", 2 * T)
        Mt_ready = sig("masked_scores_ready", 2 * T)
        xt_filled = sig("xt_filled", T)
        bt_filled = sig("bt_filled", T - 1)
        Xd_ready = sig("Xd_ready", T)
        Bw_ready = sig("Bw_ready", T - 1)
        y_filled = sig("y_filled", T)
        y_ready = sig("y_ready", T)
        s_filled = sig("s_filled", T - 1)
        S_ready = sig("state_ready", T - 1)
        Sdc_ready = sig("state_decayed", T - 2)
        pk_ready = sig("gn_stats_ready")
        pk_filled = sig("gn_stats_filled")
        gvar_ready = sig("gn_var_ready")
        grstd_ready = sig("gn_rstd_ready")
        wog_ready = sig("wog_ready")
        yn_ready = sig("yn_ready", 8)
        g_ready = sig("gated_ready", 8)
        out_filled = sig("out_filled", 4)
        x1_ready = sig("x1_ready", 4)
        var2_ready = sig("var2_ready", 4)
        rstd2_ready = sig("rstd2_ready", 4)
        hn2_ready = sig("hn2_ready", T)
        h2_ready = sig("h2_ready", T)
        w_ready = sig("w_ready", T)
        wcol_ready = sig("wcol_ready")
        base_ready = sig("base_ready", T)
        x1_stored = sig("x1_stored", 64)
        base_stored = sig("base_stored", 64)
        G_ready = sig("compare_ready", T)
        P_ready = sig("onehot_ready", T)
        gidx_ready = sig("gidx_ready")
        xs_loaded = sig("xs_gathered", 16)
        m_loaded = sig("mask_gathered", 16)
        pos_loaded = sig("pos_gathered", 16)
        fv_ready = sig("ffn_var_ready")
        fr_ready = sig("ffn_rstd_ready")
        fs_ready = sig("ffn_rms1_ready")
        frr_ready = sig("ffn_rms1_inv")
        fs2_ready = sig("ffn_rms2_ready")
        frr2_ready = sig("ffn_rms2_inv")
        hn_ready = sig("ffn_hn_ready")
        mclamp_ready = sig("mask_clamped")
        msel_ready = sig("msel_ready")
        qkz_ready = sig("rope_pad_zero")
        qk_ready = sig("qk_ready")
        ang_ready = sig("angles_ready")
        sin_ready = sig("sin_ready")
        rope_ready = sig("rope_ready")
        scr_ready = sig("scr_ready", 4)
        mx_ready = sig("max_ready")
        prob_ready = sig("prob_ready", FH)
        den_ready = sig("den_ready")
        x1s_ready = sig("x1s_ready")
        hnb_ready = sig("ffn_hn2_ready")
        so_ready = sig("proc_ready")
        scattered = sig("scattered", 16)

        def ring(name, banks, jobs):
            return Ring(banks, [sig(f"{name}_filled{i}", len(range(i, jobs, 4))) for i in range(4)],
                        [sig(f"{name}_drained{i}", len(range(i, jobs, 4))) for i in range(4)])

        proj = ring("proj", ps[0:4], 47)
        ffn = ring("ffn", ps[4:8], 27)
        J_H, J_X, J_Z, J_DT, J_B0, J_V, J_B1, J_EC = 0, 4, 12, 20, 22, 30, 31, 39
        J_BC = (J_B0, J_B1)
        (F_WROW, F_RANK, F_IDX, F_HNT, F_MT, F_MSEL, F_QK, F_V, F_QT, F_KT, F_SC, F_AT, F_AV, F_OT, F_WO,
         F_HNBT, F_W1, F_W2) = 0, 2, 3, 4, 5, 7, 8, 9, 10, 11, 12, 16, 20, 21, 22, 23, 24, 26

        chA, chV, chD, chS, chG, chR, chO = (Chain(sig("chain" + c, CHAINS[c]), c) for c in "AVDSGRO")

        block = ctx.enter_context(nc.Block())

        def kp(w):
            return w.rearrange("(k p) n -> p k n", p=P)

        mixer_loads = ((r48_s[:, :], rows48), (cols_s[:, :, :], cols), (wx_s[:, :, :], kp(wxT)),
                       (wz_s[:, :, :], kp(wzT)), (wdt_s[:, :, :], kp(wdtT)), (wb_s[:, :, :], kp(wbT)),
                       (wc_s[:, :, :], kp(wcT)), (wo_s[:, :, :], kp(woT)), (rw_s[:, :], rw.partition_broadcast(P)),
                       (rb_s[:, :], rb.partition_broadcast(P)))
        ffn_loads = ((wqkv_s[:, :, :], kp(wqkv)), (fwo_s[:, :, :], kp(wo)), (w1_s[:, :, :], kp(w1)),
                     (w2_s[:, :, :], kp(w2)), (ln_s[:, :, :], lncols))

        @block.sync
        def _(sp):

            sp.dma_start(mcin, cT.rearrange("(k p) n -> p k n", p=P)).then_inc(mload, 16)
            sp.dma_start(wmod_s, kp(wmod)).then_inc(mload, 16)
            sp.dma_start(xin[:, :, :], x[0, :, :].rearrange("(t p) n -> p t n", p=P)).then_inc(x_loaded, 16)
            for dst, src in mixer_loads:
                sp.dma_start(dst, src).then_inc(wload, 16)
            for dst, src in ffn_loads:
                sp.dma_start(dst, src).then_inc(fload, 16)
            sp.wait_ge(setup_dve, SD_MOD)
            sp.dma_start(mod_d[:, :], mod8).then_inc(mod_stored, 16)
            sp.wait_ge(mod_stored, 16)

            def loads(b):
                if later(b):
                    sp.wait_ge(so_ready, at(so_ready, b - 1, 1))
                if later(b):
                    sp.wait_ge(scattered, at(scattered, b - 1, 16))
                sp.dma_start(modrow[:, :, :].rearrange("p a n -> p (a n)"),
                             mod_d[bass.ds(b, 1), 2 * D:6 * D].rearrange("a n -> (a n)").partition_broadcast(P)
                             ).then_inc(modrow_loaded, 16)
                sp.dma_start(xr[:, :, :], x[bass.ds(b, 1), :, :].rearrange("a (t p) n -> p (a t) n", p=P)
                             ).then_inc(xr_loaded, 16)

            def prefetch(b):
                sp.wait_ge(g_ready, at(g_ready, b, 8))
                sp.dma_start(xin[:, :, :], x[bass.ds(b + 1, 1), :, :].rearrange("a (t p) n -> p (a t) n", p=P)
                             ).then_inc(x_loaded, 16)

            def stores(b):
                for j in range(4):
                    rows = slice(2 * j, 2 * j + 2)
                    sp.wait_ge(x1_ready, at(x1_ready, b, j + 1))
                    sp.dma_start(x1_d[2 * j * P:2 * (j + 1) * P, :].rearrange("(t p) n -> p t n", p=P),
                                 xr[:, rows, :]).then_inc(x1_stored, 16)
                    sp.wait_ge(base_ready, at(base_ready, b, 2 * j + 2))
                    sp.dma_start(out[bass.ds(b * L + 2 * j * P, 2 * P), :].rearrange("(t p) n -> p t n", p=P),
                                 h2[:, rows, :]).then_inc(base_stored, 16)

            loads(0)
            prefetch(0)
            stores(0)
            with sp.Fori(1, NB - 1) as b:
                loads(b)
                prefetch(b)
                stores(b)
            loads(NB - 1)
            stores(NB - 1)
            sp.wait_ge(x1_stored, at(x1_stored, NB - 1, 64))
            sp.wait_ge(base_stored, at(base_stored, NB - 1, 64))
            sp.wait_ge(scattered, at(scattered, NB - 1, 16))

        @block.gpsimd
        def _(pool):
            g = nc.gpsimd
            n = [0]

            def link(ins):
                ins.then_inc(setup_pool, 1)
                n[0] += 1
                pool.wait_ge(setup_pool, n[0])

            link(g.memset(ident[:, :], 0.0))
            link(g.affine_select(out=ident[:, :], in_=ident[:, :], compare_op=ALU.not_equal, fill=1.0,
                                 base=0, pattern=[[-1, P]], channel_multiplier=1))
            link(g.tensor_copy(identb[:, :], ident[:, :]))
            link(g.memset(tri[:, :], 1.0))
            link(g.affine_select(out=tri[:, :], in_=tri[:, :], compare_op=ALU.is_gt, fill=0.0,
                                 base=0, pattern=[[1, P]], channel_multiplier=-1))
            link(g.memset(causal[:, :, :], 0.0))
            link(g.affine_select(out=causal[:, :, :], in_=causal[:, :, :], compare_op=ALU.is_ge, fill=MASKED,
                                 base=0, pattern=[[0, 4], [1, P]], channel_multiplier=-1))
            link(g.memset(ones_b[:, :], 1.0))
            link(g.memset(halfmean[:, :], 0.0))
            link(g.memset(halfmean[0:64, 0:64], 1.0 / STATE))
            link(g.memset(halfmean[64:128, 64:128], 1.0 / STATE))
            link(g.iota(iota_r[:, :], pattern=[[1, P]], base=0, channel_multiplier=0,
                        allow_small_or_imprecise_dtypes=True))
            link(g.iota(tok[:, :], pattern=[[P, T]], base=0, channel_multiplier=1,
                        allow_small_or_imprecise_dtypes=True))
            link(g.memset(mhalf[:, :], -0.5))
            link(g.memset(ones4[:, :, :], 1.0))
            link(g.memset(spare[:, :], 0.0))
            for i in range(G3 + 2):
                first, last = (i, i) if i < G3 else ((0, 2) if i == G3 else (3, 5))
                link(g.memset(gmask[:, i:i + 1], 1.0))
                link(g.affine_select(out=gmask[:, i:i + 1], in_=gmask[:, i:i + 1], compare_op=ALU.is_ge,
                                     fill=0.0, base=-HEADS * first, pattern=[[0, 1]], channel_multiplier=1))
                link(g.affine_select(out=gmask[:, i:i + 1], in_=gmask[:, i:i + 1], compare_op=ALU.is_ge,
                                     fill=0.0, base=HEADS * last + HEADS - 1, pattern=[[0, 1]],
                                     channel_multiplier=-1))
            link(g.tensor_scalar(gneg[:, :], gmask[:, G3:G3 + 1], -1.0, None, ALU.mult))
            link(g.memset(dlt6, 0.0))
            link(g.affine_select(out=dlt6, in_=dlt6, compare_op=ALU.not_equal, fill=1.0, base=0,
                                 pattern=[[-HEADS, G3], [-1, HEADS]], channel_multiplier=1))
            for i in range(G3):
                link(g.tensor_copy(delta[:, :], dlt6[:, 0, :]) if i == 0 else
                     g.tensor_tensor(delta[:, :], delta[:, :], dlt6[:, i, :], ALU.add))
            link(g.memset(reset[:, :, :], 1.0))
            link(g.memset(reset[:, :, 0:1], 0.0))
            for i in range(HD // 2):
                link(g.memset(invf[:, :, i:i + 1], 1.0 / ROPE_BASE ** (2.0 * i / HD)))
            link(g.memset(phase[:, :, 0, :], 0.0))
            link(g.memset(phase[:, 0, 1, :], 0.25))
            link(g.memset(phase[:, 1, 1, :], PI / 2))
            link(g.memset(Sbd[:, :, :], 0.0))
            link(g.memset(Sdc[:, :, :], 0.0))
            link(g.memset(boff[:, :], 0.0))
            assert n[0] == SP_ALL, n[0]

            def ln_in(b):
                pool.wait_ge(var_ready, at(var_ready, b, 1))
                g.tensor_tensor(rstd[:, :], rstd[:, :], mhalf[:, :], ALU.pow).then_inc(rstd_ready, 1)

            def carry(b):
                pool.wait_ge(*proj.read(b, J_EC + 7))
                g.tensor_tensor(dec[:, :, :], ECv[:, :, P - 1::P], ones4[:, :, :], ALU.mult
                                ).then_inc(dec_ready, 1)
                pool.wait_ge(dec_ready, at(dec_ready, b, 1))
                pool.wait_ge(*proj.read(b, J_B1 + 7))
                for half in range(2):
                    for k in range(KC):
                        s = ECv[:, k, half * HALF:(half + 1) * HALF]
                        g.tensor_tensor(s, s, CT[:, half, k, :], ALU.mult
                                        ).then_inc(CE_ready, 1)
                pool.wait_ge(modrow_loaded, at(modrow_loaded, b, 16))
                pool.wait_ge(v_ready, at(v_ready, b, 1))
                g.tensor_tensor(wog_s[:, :, :], wo_s[:, :, :],
                                modrow[:, 0:1, :].broadcast_to([P, KC, D]), ALU.mult).then_inc(wog_ready, 1)

            def decays(b):
                for c in range(1, T - 1):
                    if c or later(b):
                        pool.wait_ge(S_ready, at(S_ready, b, c))
                    g.tensor_tensor(Sdc[:, :, :], Sbd[:, :, :], dec[:, :, c:c + 1].broadcast_to([P, KC, P]),
                                    ALU.mult).then_inc(Sdc_ready, 1)

            def out_(b):
                pool.wait_ge(gvar_ready, at(gvar_ready, b, 1))
                g.tensor_tensor(gab[:, 1, :], gab[:, 0, :], mhalf[:, 0:KC], ALU.pow).then_inc(grstd_ready, 1)
                for half in range(2):
                    for k in range(KC):
                        s = slice(half * HALF, (half + 1) * HALF)
                        pool.wait_ge(yn_ready, at(yn_ready, b, half * KC + k + 1))
                        g.tensor_tensor(xT[:, k, s], xT[:, k, s], zs[:, k, s], ALU.mult).then_inc(g_ready, 1)
                for j in range(4):
                    pool.wait_ge(var2_ready, at(var2_ready, b, j + 1))
                    q = slice(2 * j, 2 * j + 2)
                    g.tensor_tensor(rstdb[:, q], rstdb[:, q], mhalf[:, q], ALU.pow).then_inc(rstd2_ready, 1)
                    for t in (2 * j, 2 * j + 1):
                        pool.wait_ge(hn2_ready, at(hn2_ready, b, t + 1))
                        chO(pool, b, g.tensor_tensor(h2[:, t, :], h2[:, t, :], modrow[:, 2, :], ALU.mult))
                        g.tensor_tensor(h2[:, t, :], h2[:, t, :], modrow[:, 1, :], ALU.add
                                        ).then_inc(h2_ready, 1)
                    for t in (2 * j, 2 * j + 1):
                        pool.wait_ge(w_ready, at(w_ready, b, t + 1))
                        chO(pool, b, g.tensor_tensor(h2[:, t, :], h2[:, t, :], modrow[:, 3, :], ALU.mult))
                        g.tensor_tensor(h2[:, t, :], h2[:, t, :], xr[:, t, :], ALU.add
                                        ).then_inc(base_ready, 1)
                chO.end()

            def take_waits():
                g.tensor_tensor(spare[:, 0:1], mhalf[:, 0:1], mhalf[:, 1:2], ALU.mult)

            def gather(b):
                pool.wait_ge(gidx_ready, at(gidx_ready, b, 1))
                pool.wait_ge(x1_stored, at(x1_stored, b, 64))
                take_waits()
                g.indirect_dma_start(xs, None, x1_d[:, :], bass.IndirectOffsetOnAxis(ap=xidx[:, 0:1], axis=0)
                                     ).then_inc(xs_loaded, 16)
                g.indirect_dma_start(mrows, None, mask, bass.IndirectOffsetOnAxis(ap=midx[:, 0:1], axis=0)
                                     ).then_inc(m_loaded, 16)
                g.indirect_dma_start(posi[:, :], None, pos, bass.IndirectOffsetOnAxis(ap=midx[:, 0:1], axis=0)
                                     ).then_inc(pos_loaded, 16)
                g.memset(qkr[:, :, :, HD:2 * HD], 0.0).then_inc(qkz_ready, 1)

            def small_pow(b, before, after, col):
                pool.wait_ge(before, at(before, b, 1))
                g.tensor_tensor(sm[:, col + 1:col + 2], sm[:, col:col + 1], mhalf[:, 0:1], ALU.pow
                                ).then_inc(after, 1)

            def scatter(b):
                pool.wait_ge(so_ready, at(so_ready, b, 1))
                pool.wait_ge(base_stored, at(base_stored, b, 64))
                take_waits()
                g.indirect_dma_start(out, bass.IndirectOffsetOnAxis(ap=gidx[0:NSEL, 0:1], axis=0),
                                     x1s[0:NSEL, :], None).then_inc(scattered, 16)

            def ffn_all(b):
                gather(b)
                small_pow(b, fv_ready, fr_ready, 0)
                small_pow(b, fs_ready, frr_ready, 2)
                small_pow(b, fs2_ready, frr2_ready, 4)
                scatter(b)

            def rest(b):
                carry(b)
                decays(b)
                out_(b)

            ln_in(0)
            rest(0)
            with pool.Fori(1, NB) as b:
                ln_in(b)
                ffn_all(b - 1)
                rest(b)
            ffn_all(NB - 1)

        @block.scalar
        def _(act):
            a = nc.scalar
            act.wait_ge(mload, 16 * 2)
            a.activation(mcin, mcin, ACT.Silu).then_inc(setup_act, 1)
            for j in range(3):
                act.wait_ge(setup_pe, j + 1)
                a.activation(mod8[:, j * 512:(j + 1) * 512], ps[j][0:NB, :], ACT.Copy).then_inc(setup_act, 1)
            act.wait_ge(setup_pe, 4)
            a.activation(mcol[:, :, :], ps[3][:, 0:4 * NB].rearrange("p (a n) -> p a n", a=4), ACT.Copy
                         ).then_inc(setup_act, 1)
            act.wait_ge(wload, 16 * len(mixer_loads))
            a.activation(aneg[:, :], r48_s[:, 1:2], ACT.Exp).then_inc(setup_act, 1)
            act.wait_ge(mod_stored, 16)

            def ln_in(b):
                act.wait_ge(mc_ready, at(mc_ready, b, 1))
                for half in range(2):
                    for k in range(KD):
                        q = J_H + half * KD + k
                        act.wait_ge(*proj.full(b, q))
                        bank = proj.bank(q)
                        act_in = a.activation(hT[:, k, half * HALF:(half + 1) * HALF], bank[:, :], ACT.Identity,
                                              bias=mc[:, k:k + 1], scale=mc[:, 2 + k:3 + k])
                        act_in.then_inc(proj.drained[q % 4], 1)

            def x_copies(b):
                for half in range(2):
                    for m in range(KC):
                        q = J_X + half * KC + m
                        act.wait_ge(*proj.full(b, q))
                        bank = proj.bank(q)
                        o = TAPS - 1 + half * HALF
                        ins = a.activation(xcv[:, m, o:o + HALF], bank[:, :], ACT.Copy)
                        ins.then_inc(proj.drained[q % 4], 1)

            def x_silu(b):
                for half in range(2):
                    for m in range(KC):
                        s = xT[:, m, half * HALF:(half + 1) * HALF]
                        act.wait_ge(conv_ready, at(conv_ready, b, half * KC + m + 1))
                        a.activation(s, s, ACT.Silu).then_inc(xT_ready, 1)

            def z_half(b, half):
                for m in range(KC):
                    act.wait_ge(*proj.full(b, J_Z + half * KC + m))
                    bank = proj.bank(J_Z + half * KC + m)
                    ins = a.activation(zs[:, m, half * HALF:(half + 1) * HALF], bank[:, :], ACT.Silu)
                    ins.then_inc(proj.drained[(J_Z + half * KC + m) % 4], 1)

            def softplus(b):
                act.wait_ge(u_ready, at(u_ready, b, 1))
                a.activation(a48, a48, ACT.Exp, scale=-1.0).then_inc(l_ready, 1)
                act.wait_ge(l_ready, at(l_ready, b, 1))
                a.activation(b48, a48, ACT.Ln, bias=1.0).then_inc(l_ready, 1)

            def c_half(b, half):
                for m in range(KC):
                    act.wait_ge(*proj.full(b, J_BC[half] + KC + m))
                    bank = proj.bank(J_BC[half] + KC + m)
                    ins = a.activation(CT[:, half, m, :], bank[:, :], ACT.Copy)
                    ins.then_inc(proj.drained[(J_BC[half] + KC + m) % 4], 1)

            def w_exp(b):
                act.wait_ge(dif_ready, at(dif_ready, b, 1))
                a.activation(a48, a48, ACT.Exp).then_inc(wexp_ready, 1)

            def ec(b):
                for half in range(2):
                    for k in range(KC):
                        act.wait_ge(*proj.full(b, J_EC + half * KC + k))
                        bank = proj.bank(J_EC + half * KC + k)
                        ins = a.activation(ECv[:, k, half * HALF:(half + 1) * HALF], bank[:, :], ACT.Exp)
                        ins.then_inc(proj.drained[(J_EC + half * KC + k) % 4], 1)

            def scan(b):
                for c in range(T):
                    for s in range(2):
                        act.wait_ge(cd_filled, at(cd_filled, b, 2 * c + s + 1))
                        if c or later(b):
                            act.wait_ge(Mt_ready, at(Mt_ready, b, 2 * (c - 1) + s + 1 if c else 0))
                        a.activation(Eg[:, s * HALF:(s + 1) * HALF], ps[s][:, :], ACT.Exp
                                     ).then_inc(Eg_ready, 1)

            def ffn_wrow(b):
                for j in range(2):
                    act.wait_ge(*ffn.full(b, F_WROW + j))
                    bank = ffn.bank(F_WROW + j)
                    ins = a.activation(wrow[:, j * HALF:(j + 1) * HALF], bank[:, :], ACT.Copy)
                    ins.then_inc(ffn.drained[(F_WROW + j) % 4], 1)

            def ffn_hnT(b):
                act.wait_ge(*ffn.full(b, F_HNT))
                bank = ffn.bank(F_HNT)
                ins = a.activation(hnT_, bank[:, 0:D], ACT.Copy)
                ins.then_inc(ffn.drained[F_HNT % 4], 1)
                for j in range(2):
                    act.wait_ge(*ffn.full(b, F_MT + j))
                    bank = ffn.bank(F_MT + j)
                    ins = a.activation(mT[:, 4 * j:4 * j + 4, :].rearrange("p t n -> p (t n)"), bank[:, :], ACT.Copy)
                    ins.then_inc(ffn.drained[(F_MT + j) % 4], 1)

            def ffn_v(b):
                act.wait_ge(*ffn.full(b, F_V))
                bank = ffn.bank(F_V)
                ins = a.activation(vs, bank[:, 0:D], ACT.Copy)
                ins.then_inc(ffn.drained[F_V % 4], 1)
                act.wait_ge(ang_ready, at(ang_ready, b, 1))
                a.activation(sc_[:, :, :], ang[:, :, :], ACT.Sin).then_inc(sin_ready, 1)

            def ffn_qT(b):
                for j, dst in ((F_QT, qT), (F_KT, kT)):
                    act.wait_ge(*ffn.full(b, j))
                    bank = ffn.bank(j)
                    ins = a.activation(dst.rearrange("p m n -> p (m n)"), bank[:, :], ACT.Copy)
                    ins.then_inc(ffn.drained[j % 4], 1)

            def ffn_softmax(b):
                act.wait_ge(mx_ready, at(mx_ready, b, 1))
                for h in range(FH):
                    a.activation(scr[:, h, 0:NSEL], scr[:, h, 0:NSEL], ACT.Exp, bias=mx[:, h:h + 1],
                                 accum_out=den[:, h:h + 1]).then_inc(prob_ready, 1)

            def ffn_AT(b):
                for j in range(4):
                    act.wait_ge(*ffn.full(b, F_AT + j))
                    bank = ffn.bank(F_AT + j)
                    ins = a.activation(AT[0:NSEL, 4 * j:4 * j + 4, :].rearrange("p t n -> p (t n)"),
                                       bank[0:NSEL, :], ACT.Copy)
                    ins.then_inc(ffn.drained[(F_AT + j) % 4], 1)

            def ffn_oT(b):
                act.wait_ge(*ffn.full(b, F_OT))
                bank = ffn.bank(F_OT)
                ins = a.activation(oT_, bank[:, 0:D], ACT.Copy)
                ins.then_inc(ffn.drained[F_OT % 4], 1)

            def ffn_hnbT(b):
                act.wait_ge(*ffn.full(b, F_HNBT))
                bank = ffn.bank(F_HNBT)
                ins = a.activation(hnT_, bank[:, 0:D], ACT.Copy)
                ins.then_inc(ffn.drained[F_HNBT % 4], 1)

            def ffn_gelu(b):
                for j in range(2):
                    act.wait_ge(*ffn.full(b, F_W1 + j))
                    bank = ffn.bank(F_W1 + j)
                    ins = a.activation(gT[:, 4 * j:4 * j + 4, :].rearrange("p t n -> p (t n)"), bank[:, :],
                                       ACT.Gelu_apprx_tanh)
                    ins.then_inc(ffn.drained[(F_W1 + j) % 4], 1)

            def batch(b, f):
                ln_in(b)
                if f is not None:
                    ffn_wrow(f)
                x_copies(b)
                x_silu(b)
                z_half(b, 0)
                if f is not None:
                    ffn_hnT(f)
                z_half(b, 1)
                if f is not None:
                    ffn_v(f)
                softplus(b)
                if f is not None:
                    ffn_qT(f)
                w_exp(b)
                if f is not None:
                    ffn_softmax(f)
                c_half(b, 0)
                if f is not None:
                    ffn_AT(f)
                    ffn_oT(f)
                    ffn_hnbT(f)
                    ffn_gelu(f)
                act.wait_ge(*proj.read(b, J_V))
                c_half(b, 1)
                ec(b)
                scan(b)

            batch(0, None)
            with act.Fori(1, NB) as b:
                batch(b, b - 1)
            f = NB - 1
            ffn_wrow(f)
            ffn_hnT(f)
            ffn_v(f)
            ffn_qT(f)
            ffn_softmax(f)
            ffn_AT(f)
            ffn_oT(f)
            ffn_hnbT(f)
            ffn_gelu(f)

        @block.vector
        def _(dve):
            v = nc.vector
            n = [0]

            def link(ins):
                ins.then_inc(setup_dve, 1)
                n[0] += 1
                dve.wait_ge(setup_dve, n[0])

            dve.wait_ge(setup_act, 4)
            for i in (1, 4):
                s = mod8[:, i * D:(i + 1) * D]
                link(v.tensor_scalar(s, s, 1.0, None, ALU.add))
            for i in (2, 5):
                s = mod8[:, i * D:(i + 1) * D]
                link(v.tensor_scalar(sgn8, s, 0.0, 2.0, ALU.is_ge, ALU.mult))
                link(v.scalar_tensor_tensor(abs8, s, -1.0, s, ALU.mult, ALU.max))
                link(v.tensor_scalar(abs8, abs8, 0.25, None, ALU.max))
                link(v.scalar_tensor_tensor(s, sgn8, -1.0, abs8, ALU.add, ALU.mult))
            assert n[0] == SD_MOD, n[0]
            dve.wait_ge(setup_pool, SP_ALL)
            dve.wait_ge(setup_act, 6)
            link(v.tensor_scalar(aneg[:, :], aneg[:, :], -1.0, None, ALU.mult))
            link(v.tensor_scalar(delt3[:, :], delta[:, :], gmask[:, G3:G3 + 1], None, ALU.mult))
            for hh in range(2):
                link(v.tensor_copy(selp[:, :, 64 * hh:64 * hh + 64],
                                   delt3[:, hh::2].unsqueeze(2).broadcast_to([RW, 4, 64])))
            assert n[0] == SD_MIX
            dve.wait_ge(wload, 16 * len(mixer_loads))

            def fold_ln():
              dve.wait_ge(fload, 16 * len(ffn_loads))
              for k in range(KD):
                link(v.tensor_scalar(wqkv_s[:, k, :], wqkv_s[:, k, :], ln_s[:, 0, k:k + 1], None, ALU.mult))
                link(v.tensor_scalar(w1_s[:, k, :], w1_s[:, k, :], ln_s[:, 1, k:k + 1], None, ALU.mult))
              assert n[0] == SD_ALL

            def take_waits():
                v.tensor_copy(spare[:, 1:2], mhalf[:, 0:1])

            def ln_in(b):
                dve.wait_ge(x_loaded, at(x_loaded, b, 16))
                if later(b):
                    dve.wait_ge(*proj.read(b - 1, J_H + (4) - 1))
                v.tensor_copy(mc[:, :], mcol[:, :, bass.ds(b, 1)].rearrange("p a n -> p (a n)")
                              ).then_inc(mc_ready, 1)
                for t in range(T):
                    ins = v.bn_stats(st6[:, t, :], xin[:, t, :])
                chA(dve, b, ins)
                take_waits()
                for t in range(T):
                    ins = v.bn_aggr(mv[:, t, :], st6[:, t, :])
                chA(dve, b, ins)
                v.tensor_scalar(rstd[:, :], mv[:, :, 1], EPS, None, ALU.add).then_inc(var_ready, 1)
                dve.wait_ge(rstd_ready, at(rstd_ready, b, 1))
                for t in range(T):
                    v.tensor_scalar(xin[:, t, :], xin[:, t, :], mv[:, t, 0:1], rstd[:, t:t + 1],
                                    ALU.subtract, ALU.mult).then_inc(xn_ready, 1)
                chA.end()

            def conv(b):
                if later(b):
                    dve.wait_ge(cd_filled, at(cd_filled, b - 1, 2 * T))
                chV(dve, b, v.memset(xcv[:, :, 0:TAPS - 1], 0.0))
                for half in range(2):
                    for m2 in range(2):
                        pair = (2 * m2, 2 * m2 + 1)
                        dve.wait_ge(*proj.read(b, J_X + (half * KC + pair[1] + 1) - 1))
                        for tap in range(TAPS):
                            for m in pair:
                                dst = xT[:, m, half * HALF:(half + 1) * HALF]
                                src = xcv[:, m, half * HALF + tap:half * HALF + tap + HALF]
                                if tap == 0:
                                    ins = v.tensor_scalar(dst, src, cols_s[:, m, 0:1], cols_s[:, m, 4:5],
                                                          ALU.mult, ALU.add)
                                else:
                                    ins = v.scalar_tensor_tensor(dst, src, cols_s[:, m, tap:tap + 1], dst,
                                                                 ALU.mult, ALU.add)
                                if tap == TAPS - 1:
                                    ins.then_inc(conv_ready, 1)
                                elif m == pair[1]:
                                    chV(dve, b, ins)
                chV.end()

            def softplus_in(b):
                for half in range(2):
                    q = J_DT + half
                    dve.wait_ge(*proj.full(b, q))
                    bank = proj.bank(q)
                    s = slice(half * HALF, (half + 1) * HALF)
                    ins = v.tensor_scalar(v48[:, s], bank[0:RW, :], r48_s[:, 0:1], None, ALU.add)
                    ins.then_inc(proj.drained[q % 4], 1)
                for half in range(2):
                    dve.wait_ge(*proj.read(b, J_DT + half))
                v.scalar_tensor_tensor(a48, v48, -1.0, v48, ALU.mult, ALU.max).then_inc(u_ready, 1)

            def decay_rows(b):
                dve.wait_ge(l_ready, at(l_ready, b, 2))
                chD(dve, b, v.scalar_tensor_tensor(dt48, v48, 0.0, b48, ALU.max, ALU.add))
                chD(dve, b, v.tensor_scalar(a48, dt48, aneg[:, :], None, ALU.mult))
                chD(dve, b, v.tensor_tensor_scan(v48, reset[:, :, :].rearrange("p t n -> p (t n)"), a48, 0.0,
                                                 ALU.mult, ALU.add))
                chD(dve, b, v.tensor_copy(hi, v48))
                chD(dve, b, v.tensor_tensor(a48, v48, hi, ALU.subtract))
                chD(dve, b, v.tensor_copy(mid, a48))
                chD(dve, b, v.tensor_tensor(lo, a48, mid, ALU.subtract))
                cv = v48.rearrange("p (t n) -> p t n", t=T)
                v.tensor_tensor(a48.rearrange("p (t n) -> p t n", t=T), cv[:, :, P - 1:P].broadcast_to([RW, T, P]),
                                cv, ALU.subtract).then_inc(dif_ready, 1)
                chD(dve, b, v.tensor_scalar(Lw[:, :], hi, gmask[:, 0:1], gmask[:, 7:8], ALU.mult, ALU.add))
                chD(dve, b, v.scalar_tensor_tensor(Lw[:, :], mid, gmask[:, 1:2], Lw[:, :], ALU.mult, ALU.add))
                chD(dve, b, v.scalar_tensor_tensor(Lw[:, :], lo, gmask[:, 2:3], Lw[:, :], ALU.mult, ALU.add))
                chD(dve, b, v.tensor_scalar(Rw, hi, gmask[:, 3:4], gneg[:, :], ALU.mult, ALU.add))
                chD(dve, b, v.scalar_tensor_tensor(Rw, mid, gmask[:, 4:5], Rw, ALU.mult, ALU.add))
                chD(dve, b, v.scalar_tensor_tensor(Rw, lo, gmask[:, 5:6], Rw, ALU.mult, ALU.add))
                for i in range(HEADS):
                    h = 2 * (i % 4) + i // 4
                    ins = v.tensor_scalar(R8[:, i, :], Rw, delta[:, h:h + 1], None, ALU.mult)
                ins.then_inc(rows_ready, 1)
                dve.wait_ge(wexp_ready, at(wexp_ready, b, 1))
                chD(dve, b, v.tensor_scalar(v48, dt48, gmask[:, 0:1], None, ALU.mult))
                v.scalar_tensor_tensor(v48, a48, gmask[:, 1:2], v48, ALU.mult, ALU.add).then_inc(v_ready, 1)
                chD.end()

            def b_half(b, half):
                for m in range(KC):
                    dve.wait_ge(*proj.full(b, J_BC[half] + m))
                    bank = proj.bank(J_BC[half] + m)
                    ins = v.tensor_copy(BT[:, half, m, :], bank[:, :])
                    ins.then_inc(proj.drained[(J_BC[half] + m) % 4], 1)

            def dw_copy(b):
                dve.wait_ge(*proj.full(b, J_V))
                bank = proj.bank(J_V)
                ins = v.tensor_copy(dw[:, :, :],
                                    bank[:, 0:T * RW].rearrange("p (t n) -> p t n", t=T)[:, :, 0:2 * HEADS])
                ins.then_inc(proj.drained[J_V % 4], 1)

            def scan(b):
                def weigh(c):
                    dve.wait_ge(*proj.read(b, J_V))
                    if c == 0:
                        if later(b):
                            dve.wait_ge(so_ready, at(so_ready, b - 1, 1))
                    dve.wait_ge(xt_filled, at(xt_filled, b, c + 1))
                    if c >= 2:
                        dve.wait_ge(y_filled, at(y_filled, b, c - 1))
                    if c >= 2:
                        dve.wait_ge(s_filled, at(s_filled, b, c - 1))
                    v.tensor_tensor(XB[:, c % 2, 0, :].rearrange("p (h n) -> p h n", h=HEADS),
                                    ps[6][:, :].rearrange("p (h n) -> p h n", h=HEADS),
                                    dw[:, c, 0:HEADS].unsqueeze(2).broadcast_to([P, HEADS, STATE]), ALU.mult
                                    ).then_inc(Xd_ready, 1)
                    if c < T - 1:
                        dve.wait_ge(bt_filled, at(bt_filled, b, c + 1))
                        v.tensor_tensor(XB[:, c % 2, 1, :].rearrange("p (h n) -> p h n", h=HEADS),
                                        ps[7][:, :].rearrange("p (h n) -> p h n", h=HEADS),
                                        dw[:, c, HEADS:2 * HEADS].unsqueeze(2).broadcast_to([P, HEADS, STATE]),
                                        ALU.mult).then_inc(Bw_ready, 1)

                def masked(c):
                    for s in range(2):
                        dve.wait_ge(sc_filled, at(sc_filled, b, 2 * c + s + 1))
                        dve.wait_ge(Eg_ready, at(Eg_ready, b, 2 * c + s + 1))
                        v.tensor_tensor(Mt[:, c % 2, s * HALF:(s + 1) * HALF], ps[2 + s][:, :],
                                        Eg[:, s * HALF:(s + 1) * HALF], ALU.mult).then_inc(Mt_ready, 1)

                def state(c):
                    dve.wait_ge(s_filled, at(s_filled, b, c + 1))
                    if c:
                        if c or later(b):
                            dve.wait_ge(Sdc_ready, at(Sdc_ready, b, c))
                        dve.wait_ge(y_filled, at(y_filled, b, c + 1))
                    for hh in range(2):
                        q = slice(64 * hh, 64 * hh + 64)
                        src = ps[5][q, :].rearrange("p (k n) -> p k n", k=KC)[:, :, q]
                        if c:
                            ins = v.tensor_tensor(Sbd[q, :, q], src, Sdc[q, :, q], ALU.add)
                        else:
                            ins = v.tensor_copy(Sbd[q, :, q], src)
                    ins.then_inc(S_ready, 1)

                def skip(c):
                    dve.wait_ge(y_filled, at(y_filled, b, c + 1))
                    for k in range(KC):
                        s = xT[:, k, c * P:(c + 1) * P]
                        ins = v.scalar_tensor_tensor(s, s, cols_s[:, k, 5:6], ps[4][:, k * P:(k + 1) * P],
                                                     ALU.mult, ALU.add)
                    ins.then_inc(y_ready, 1)

                if later(b):
                    dve.wait_ge(so_ready, at(so_ready, b - 1, 1))
                v.memset(Sbd[0:64, 0, 64:128], 0.0)
                chS(dve, b, v.memset(Sbd[64:128, 0, 0:64], 0.0))
                weigh(0)
                masked(0)
                for c in range(T):
                    if c + 1 < T:
                        weigh(c + 1)
                    if c < T - 1:
                        state(c)
                    skip(c)
                    if c + 1 < T:
                        masked(c + 1)
                    if c % 4 == 3:
                        dve.wait_ge(y_ready, at(y_ready, b, c + 1))
                        for k in range(KC):
                            ins = v.bn_stats(yst[:, k, 6 * (c // 4):6 * (c // 4) + 6],
                                             xT[:, k, (c - 3) * P:(c + 1) * P])
                        chS(dve, b, ins)
                chS.end()

            def out_(b):
                take_waits()
                for k in range(KC):
                    ins = v.bn_aggr(ymv[:, k, :], yst[:, k, :])
                chG(dve, b, ins)
                v.tensor_copy(pk[:, 0, :], ymv[:, :, 0])
                chG(dve, b, v.tensor_tensor(pk[:, 1, :], ymv[:, :, 0], ymv[:, :, 0], ALU.mult))
                v.tensor_tensor(pk[:, 1, :], pk[:, 1, :], ymv[:, :, 1], ALU.add).then_inc(pk_ready, 1)
                dve.wait_ge(pk_filled, at(pk_filled, b, 1))
                chG(dve, b, v.tensor_copy(pk[:, 2:4, :], ps[4][:, 0:2 * KC].rearrange("p (a n) -> p a n", a=2)))
                chG(dve, b, v.tensor_tensor(gab[:, 0, :], pk[:, 2, :], pk[:, 2, :], ALU.mult))
                chG(dve, b, v.tensor_tensor(gab[:, 0, :], pk[:, 3, :], gab[:, 0, :], ALU.subtract))
                v.tensor_scalar(gab[:, 0, :], gab[:, 0, :], EPS, None, ALU.add).then_inc(gvar_ready, 1)
                dve.wait_ge(grstd_ready, at(grstd_ready, b, 1))
                chG(dve, b, v.tensor_tensor(gab[:, 2, :], gab[:, 1, :], cols_s[:, :, 6], ALU.mult))
                chG(dve, b, v.tensor_tensor(gab[:, 3, :], pk[:, 2, :], gab[:, 2, :], ALU.mult))
                chG(dve, b, v.tensor_tensor(gab[:, 3, :], cols_s[:, :, 7], gab[:, 3, :], ALU.subtract))
                for half in range(2):
                    for k in range(KC):
                        s = xT[:, k, half * HALF:(half + 1) * HALF]
                        v.tensor_scalar(s, s, gab[:, 2, k:k + 1], gab[:, 3, k:k + 1], ALU.mult, ALU.add
                                        ).then_inc(yn_ready, 1)
                dve.wait_ge(xr_loaded, at(xr_loaded, b, 16))
                dve.wait_ge(v_ready, at(v_ready, b, 1))
                for j in range(4):
                    q = slice(2 * j, 2 * j + 2)
                    dve.wait_ge(out_filled, at(out_filled, b, j + 1))
                    v.tensor_tensor(xr[:, q, :], xr[:, q, :], ps[j][:, :].rearrange("p (t n) -> p t n", t=2),
                                    ALU.add).then_inc(x1_ready, 1)
                    dve.wait_ge(x1_ready, at(x1_ready, b, j + 1))
                    for t in (2 * j, 2 * j + 1):
                        ins = v.bn_stats(st6b[:, t, :], xr[:, t, :])
                    chG(dve, b, ins)
                    take_waits()
                    for t in (2 * j, 2 * j + 1):
                        ins = v.bn_aggr(mvb[:, t, :], st6b[:, t, :])
                    chG(dve, b, ins)
                    v.tensor_scalar(rstdb[:, q], mvb[:, q, 1], EPS, None, ALU.add).then_inc(var2_ready, 1)
                    dve.wait_ge(rstd2_ready, at(rstd2_ready, b, j + 1))
                    for t in (2 * j, 2 * j + 1):
                        v.tensor_scalar(h2[:, t, :], xr[:, t, :], mvb[:, t, 0:1], rstdb[:, t:t + 1],
                                        ALU.subtract, ALU.mult).then_inc(hn2_ready, 1)
                    for t in (2 * j, 2 * j + 1):
                        dve.wait_ge(h2_ready, at(h2_ready, b, t + 1))
                        v.tensor_tensor_reduce(out=junkd[:, t % 2, :], in0=h2[:, t, :], in1=rw_s[:, :], scale=1.0,
                                               scalar=0.0, op0=ALU.mult, op1=ALU.add,
                                               accum_out=wcol[:, t:t + 1]).then_inc(w_ready, 1)
                dve.wait_ge(w_ready, at(w_ready, b, T))
                v.tensor_scalar(wcol[:, :], wcol[:, :], rb_s[:, :], None, ALU.add).then_inc(wcol_ready, 1)
                chG.end()

            def ffn_rank(b):
                dve.wait_ge(*ffn.read(b, F_WROW + 1))
                dve.wait_ge(base_stored, at(base_stored, b, 64))
                for t in range(T):
                    ins = v.scalar_tensor_tensor(Pm[:, t, :], wrow[:, t * P:(t + 1) * P], wcol[:, t:t + 1],
                                                 tri[:, :], ALU.is_equal, ALU.mult)
                chR(dve, b, ins)
                for t in range(T):
                    lo_, hi_ = t * P, (t + 1) * P
                    wj = wcol[:, t:t + 1]
                    if t:
                        v.tensor_scalar(Gt[:, t, 0:lo_], wrow[:, 0:lo_], wj, None, ALU.is_lt)
                    if t < T - 1:
                        v.tensor_scalar(Gt[:, t, hi_:L], wrow[:, hi_:L], wj, None, ALU.is_le)
                    v.scalar_tensor_tensor(Gt[:, t, lo_:hi_], wrow[:, lo_:hi_], wj, Pm[:, t, :],
                                           ALU.is_lt, ALU.add).then_inc(G_ready, 1)

            def ffn_pick(b):
                dve.wait_ge(*ffn.full(b, F_RANK))
                bank = ffn.bank(F_RANK)
                ins = v.tensor_copy(rank[:, :], bank[:, 0:T])
                ins.then_inc(ffn.drained[F_RANK % 4], 1)
                dve.wait_ge(*ffn.read(b, F_RANK))
                for t in range(T):
                    v.tensor_scalar(Pm[:, t, :], iota_r[:, :], rank[:, t:t + 1], None, ALU.is_equal
                                    ).then_inc(P_ready, 1)
                v.tensor_scalar(moff[:, :], boff[:, :], float((MB - 1) * L), None, ALU.min)
                dve.wait_ge(*ffn.full(b, F_IDX))
                bank = ffn.bank(F_IDX)
                ins = v.tensor_copy(self_[:, 0:1], bank[:, 0:1])
                ins.then_inc(ffn.drained[F_IDX % 4], 1)
                dve.wait_ge(*ffn.read(b, F_IDX))
                v.tensor_copy(xidx[:, :], self_[:, 0:1])
                v.tensor_scalar(gidx[:, :], self_[:, 0:1], boff[:, :], None, ALU.add)
                v.tensor_scalar(midx[:, :], self_[:, 0:1], moff[:, :], None, ALU.add).then_inc(gidx_ready, 1)
                dve.wait_ge(gidx_ready, at(gidx_ready, b, 1))
                chR(dve, b, v.tensor_scalar(boff[:, :], boff[:, :], float(L), None, ALU.add))

            def ffn_norm(b):
                dve.wait_ge(xs_loaded, at(xs_loaded, b, 16))
                chR(dve, b, v.bn_stats(st1[:, :], xs))
                take_waits()
                chR(dve, b, v.bn_aggr(sm[:, 8:10], st1[:, :]))
                v.tensor_scalar(sm[:, 0:1], sm[:, 9:10], EPS, None, ALU.add).then_inc(fv_ready, 1)
                dve.wait_ge(m_loaded, at(m_loaded, b, 16))
                v.tensor_scalar(mrows, mrows, -3e38, None, ALU.max).then_inc(mclamp_ready, 1)
                dve.wait_ge(fr_ready, at(fr_ready, b, 1))
                chR(dve, b, v.tensor_scalar(hs, xs, sm[:, 8:9], sm[:, 1:2], ALU.subtract, ALU.mult))
                chR(dve, b, v.tensor_tensor(hs, hs, modrow[:, 2, :], ALU.mult))
                chR(dve, b, v.tensor_tensor(hs, hs, modrow[:, 1, :], ALU.add))
                chR(dve, b, v.tensor_tensor_reduce(out=junk, in0=hs, in1=hs, scale=1.0, scalar=0.0, op0=ALU.mult,
                                                   op1=ALU.add, accum_out=sm[:, 10:11]))
                v.tensor_scalar(sm[:, 2:3], sm[:, 10:11], 1.0 / D, 1e-6, ALU.mult, ALU.add).then_inc(fs_ready, 1)
                chR(dve, b, v.tensor_tensor_reduce(out=junk, in0=hs, in1=rw_s[:, :], scale=1.0, scalar=0.0,
                                                   op0=ALU.mult, op1=ALU.add, accum_out=sm[:, 11:12]))
                chR(dve, b, v.tensor_scalar(sm[:, 11:12], sm[:, 11:12], rb_s[:, :], None, ALU.add))
                dve.wait_ge(frr_ready, at(frr_ready, b, 1))
                v.tensor_scalar(hn, hs, sm[:, 3:4], None, ALU.mult).then_inc(hn_ready, 1)
                chR(dve, b, v.tensor_scalar(junkt, wrow[:, :], sm[:, 11:12], None, ALU.is_ge, ALU.add,
                                            accum_out=sm[:, 12:13]))
                chR(dve, b, v.tensor_scalar(sm[:, 13:14], sm[:, 12:13], KSEL - 0.5, None, ALU.is_ge))
                dve.wait_ge(pos_loaded, at(pos_loaded, b, 16))
                chR(dve, b, v.tensor_copy(posf[:, :], posi[:, :]))
                chR(dve, b, v.tensor_scalar(ang[:, :, :], invf[:, :, :], posf[:, :], None, ALU.mult))
                chR(dve, b, v.scalar_tensor_tensor(trn[:, :, :], ang[:, :, :], 1.0 / (2 * PI), phase[:, 0, :, :],
                                                   ALU.mult, ALU.add))
                chR(dve, b, v.tensor_scalar(trn[:, :, :], trn[:, :, :], ROUND, None, ALU.add))
                chR(dve, b, v.tensor_scalar(trn[:, :, :], trn[:, :, :], -ROUND, None, ALU.add))
                for part in TWO_PI:
                    chR(dve, b, v.scalar_tensor_tensor(ang[:, :, :], trn[:, :, :], -part, ang[:, :, :],
                                                       ALU.mult, ALU.add))
                chR(dve, b, v.tensor_tensor(ang[:, :, :], ang[:, :, :], phase[:, 1, :, :], ALU.add))
                v.tensor_scalar(ang[:, :, :], ang[:, :, :], -3.1415925, 3.1415925, ALU.max, ALU.min
                                ).then_inc(ang_ready, 1)

            def ffn_rope(b):
                dve.wait_ge(*ffn.full(b, F_MSEL))
                bank = ffn.bank(F_MSEL)
                ins = v.tensor_copy(msel, bank[:, 0:P])
                ins.then_inc(ffn.drained[F_MSEL % 4], 1)
                dve.wait_ge(*ffn.read(b, F_MSEL))
                dve.wait_ge(*ffn.full(b, F_QK))
                bank = ffn.bank(F_QK)
                ins = v.tensor_copy(qk, bank[:, :])
                ins.then_inc(ffn.drained[F_QK % 4], 1)
                dve.wait_ge(*ffn.read(b, F_QK))
                dve.wait_ge(sin_ready, at(sin_ready, b, 1))
                dve.wait_ge(qkz_ready, at(qkz_ready, b, 1))
                q4 = qk.rearrange("p (h a n) -> p h a n", a=2, n=HD // 2)
                r4 = rt.rearrange("p (h a n) -> p h a n", a=2, n=HD // 2)
                sinb = sc_[:, 0:1, :].broadcast_to([P, 2 * FH, HD // 2])
                cosb = sc_[:, 1:2, :].broadcast_to([P, 2 * FH, HD // 2])
                v.scalar_tensor_tensor(r4[:, :, 0, :], q4[:, :, 1, :], -1.0, sinb, ALU.mult, ALU.mult)
                chR(dve, b, v.tensor_tensor(r4[:, :, 1, :], q4[:, :, 0, :], sinb, ALU.mult))
                v.tensor_tensor(q4[:, :, 0, :], q4[:, :, 0, :], cosb, ALU.mult)
                chR(dve, b, v.tensor_tensor(q4[:, :, 1, :], q4[:, :, 1, :], cosb, ALU.mult))
                v.tensor_tensor(qkr[:, :, :, 0:HD].rearrange("p s h n -> p (s h) n"),
                                qk.rearrange("p (h n) -> p h n", n=HD),
                                rt.rearrange("p (h n) -> p h n", n=HD), ALU.add).then_inc(rope_ready, 1)

            def ffn_scores(b):
                for r in range(4):
                    q = F_SC + r
                    dve.wait_ge(*ffn.full(b, q))
                    bank = ffn.bank(q)
                    ins = v.scalar_tensor_tensor(scr[:, 4 * r:4 * r + 4, 0:NSEL],
                                                 bank[:, :].rearrange("p (m n) -> p m n", m=4)[:, :, 0:NSEL],
                                                 float(HD) ** -0.5,
                                                 msel[:, 0:NSEL].unsqueeze(1).broadcast_to([P, 4, NSEL]),
                                                 ALU.mult, ALU.add)
                    ins.then_inc(ffn.drained[q % 4], 1)
                dve.wait_ge(*ffn.read(b, F_SC + 3))
                chR(dve, b, v.tensor_reduce(mx[:, :], scr[:, :, 0:NSEL], AX.X, ALU.max))
                v.tensor_scalar(mx[:, :], mx[:, :], -1.0, None, ALU.mult).then_inc(mx_ready, 1)

            def ffn_o(b):
                dve.wait_ge(prob_ready, at(prob_ready, b, FH))
                chR(dve, b, v.reciprocal(den[:, :], den[:, :]))
                q = F_AV
                dve.wait_ge(*ffn.full(b, q))
                bank = ffn.bank(q)
                ins = v.tensor_tensor(ob.rearrange("p (m r n) -> p r m n", m=4, r=4),
                                      bank[:, 0:D].rearrange("p (m r n) -> p r m n", m=4, r=4),
                                      den[:, :].rearrange("p (r m) -> p r m", r=4).unsqueeze(3)
                                      .broadcast_to([P, 4, 4, HD]), ALU.mult)
                ins.then_inc(ffn.drained[q % 4], 1)

            def ffn_x1(b):
                q = F_WO
                dve.wait_ge(*ffn.full(b, q))
                bank = ffn.bank(q)
                ins = v.tensor_tensor(x1s, hs, bank[:, 0:D], ALU.add)
                ins.then_inc(ffn.drained[q % 4], 1)
                dve.wait_ge(*ffn.read(b, q))
                chR(dve, b, v.tensor_tensor_reduce(out=junk, in0=x1s, in1=x1s, scale=1.0, scalar=0.0, op0=ALU.mult,
                                                   op1=ALU.add, accum_out=sm[:, 10:11]))
                v.tensor_scalar(sm[:, 4:5], sm[:, 10:11], 1.0 / D, 1e-6, ALU.mult, ALU.add).then_inc(fs2_ready, 1)
                dve.wait_ge(frr2_ready, at(frr2_ready, b, 1))
                v.tensor_scalar(hn, x1s, sm[:, 5:6], None, ALU.mult).then_inc(hnb_ready, 1)

            def ffn_end(b):
                q = F_W2
                dve.wait_ge(*ffn.full(b, q))
                bank = ffn.bank(q)
                ins = v.tensor_tensor(x1s, x1s, bank[:, 0:D], ALU.add)
                ins.then_inc(ffn.drained[q % 4], 1)
                dve.wait_ge(*ffn.read(b, q))
                chR(dve, b, v.tensor_scalar(x1s, x1s, sm[:, 11:12], None, ALU.mult))
                chR(dve, b, v.scalar_tensor_tensor(x1s, hs, sm[:, 13:14], x1s, ALU.mult, ALU.add))
                chR(dve, b, v.tensor_tensor(x1s, x1s, modrow[:, 3, :], ALU.mult))
                v.tensor_tensor(x1s, x1s, xs, ALU.add).then_inc(so_ready, 1)
                chR.end()

            def batch(b, f):
                ln_in(b)
                if f is not None:
                    ffn_rank(f)
                conv(b)
                if f is not None:
                    ffn_pick(f)
                    ffn_norm(f)
                softplus_in(b)
                if f is not None:
                    ffn_rope(f)
                decay_rows(b)
                if f is not None:
                    ffn_scores(f)
                b_half(b, 0)
                if f is not None:
                    ffn_o(f)
                    ffn_x1(f)
                    ffn_end(f)
                dw_copy(b)
                b_half(b, 1)
                scan(b)
                out_(b)

            batch(0, None)
            fold_ln()
            with dve.Fori(1, NB) as b:
                batch(b, b - 1)
            f = NB - 1
            ffn_rank(f)
            ffn_pick(f)
            ffn_norm(f)
            ffn_rope(f)
            ffn_scores(f)
            ffn_o(f)
            ffn_x1(f)
            ffn_end(f)

        @block.tensor
        def _(pe):
            t_ = nc.tensor
            pe.wait_ge(mload, 32)
            pe.wait_ge(setup_act, 1)
            for j in range(3):
                for k in range(KD):
                    ins = t_.matmul(ps[j][0:NB, :], mcin[:, k, :], wmod_s[:, k, j * 512:(j + 1) * 512],
                                    start=k == 0, stop=k == KD - 1)
                ins.then_inc(setup_pe, 1)
            pe.wait_ge(setup_dve, SD_MOD)
            pe.wait_ge(setup_pool, SP_ALL)
            for j in range(4):
                ins = t_.transpose(ps[3][:, j * NB:(j + 1) * NB], mod8[:, j * P:(j + 1) * P], ident[0:NB, 0:NB])
            ins.then_inc(setup_pe, 1)
            pe.wait_ge(wload, 16 * len(mixer_loads))
            pe.wait_ge(setup_dve, SD_MIX)
            pe.wait_ge(setup_act, 5)

            def ln_in(b):
                for half in range(2):
                    for k in range(KD):
                        q = J_H + half * KD + k
                        if later(b):
                            pe.wait_ge(x1_ready, at(x1_ready, b - 1, 4))
                        if q >= 4:
                            pe.wait_ge(*proj.read(b, q - 4))
                        bank = proj.bank(q)
                        pe.wait_ge(xn_ready, at(xn_ready, b, 4 * half + 4))
                        for i in range(4):
                            ins = t_.transpose(bank[:, i * P:(i + 1) * P],
                                               xin[:, 4 * half + i, k * P:(k + 1) * P], ident[:, :])
                        ins.then_inc(proj.filled[q % 4], 1)

            def project(b, q, w, m, rhs, nk, half):
                if q >= 4:
                    pe.wait_ge(*proj.read(b, q - 4))
                bank = proj.bank(q)
                for k in range(nk):
                    ins = t_.matmul(bank[:, :], w[:, k, m * P:(m + 1) * P],
                                    rhs[:, k, half * HALF:(half + 1) * HALF], start=k == 0, stop=k == nk - 1)
                ins.then_inc(proj.filled[q % 4], 1)

            def x_proj(b):
                for half in range(2):
                    pe.wait_ge(*proj.read(b, J_H + (2 * half + 2) - 1))
                    for m in range(KC):
                        project(b, J_X + half * KC + m, wx_s, m, hT, KD, half)

            def z_proj(b, half):
                for m in range(KC):
                    project(b, J_Z + half * KC + m, wz_s, m, hT, KD, half)

            def dt_proj(b):
                for half in range(2):
                    pe.wait_ge(xT_ready, at(xT_ready, b, 4 * half + 4))
                    q = J_DT + half
                    if q >= 4:
                        pe.wait_ge(*proj.read(b, q - 4))
                    bank = proj.bank(q)
                    for k in range(KC):
                        ins = t_.matmul(bank[0:RW, :], wdt_s[:, k, :], xT[:, k, half * HALF:(half + 1) * HALF],
                                        start=k == 0, stop=k == KC - 1)
                    ins.then_inc(proj.filled[q % 4], 1)

            def bc_proj(b, half, ms):
                for m in ms:
                    project(b, J_BC[half] + m, wb_s if m < KC else wc_s, m % KC, xT, KC, half)

            def decay_jobs(b):
                q = J_V
                if q >= 4:
                    pe.wait_ge(*proj.read(b, q - 4))
                bank = proj.bank(q)
                pe.wait_ge(v_ready, at(v_ready, b, 1))
                t_.matmul(bank[:, 0:1], identb[:, :], ones_b[:, :], start=True, stop=True)
                for t in range(T):
                    ins = t_.transpose(bank[:, t * RW:(t + 1) * RW], v48[:, t * P:(t + 1) * P], ident[0:RW, 0:RW])
                ins.then_inc(proj.filled[q % 4], 1)

            def carry_rows(b):
                pe.wait_ge(rows_ready, at(rows_ready, b, 1))
                for half in range(2):
                    for k in range(KC):
                        q = J_EC + half * KC + k
                        if q >= 4:
                            pe.wait_ge(*proj.read(b, q - 4))
                        bank = proj.bank(q)
                        ins = t_.matmul(bank[:, :], selp[:, k, :], Lw[:, half * HALF:(half + 1) * HALF],
                                        start=True, stop=True)
                        ins.then_inc(proj.filled[q % 4], 1)

            def scan(b):
                def turn(c):
                    if c or later(b):
                        pe.wait_ge(Xd_ready, at(Xd_ready, b, c))
                    for k in range(KC):
                        ins = t_.transpose(ps[6][:, k * P:(k + 1) * P], xT[:, k, c * P:(c + 1) * P], ident[:, :])
                    ins.then_inc(xt_filled, 1)
                    if c < T - 1:
                        if c or later(b):
                            pe.wait_ge(Bw_ready, at(Bw_ready, b, c))
                        for k in range(KC):
                            ins = t_.transpose(ps[7][:, k * P:(k + 1) * P], BT[:, c // 4, k, chunk(c)],
                                               ident[:, :])
                        ins.then_inc(bt_filled, 1)

                def cumdiff(c):
                    for s in range(2):
                        if c or later(b):
                            pe.wait_ge(Eg_ready, at(Eg_ready, b, 2 * (c - 1) + s + 1 if c else 0))
                        t_.matmul(ps[s][:, :], identb[:, :], causal[:, :, :].rearrange("p a n -> p (a n)"),
                                  start=True, stop=False)
                        t_.matmul(ps[s][:, :], Lw[:, c * P:(c + 1) * P], R8[:, 4 * s:4 * s + 4, c * P:(c + 1) * P],
                                  start=False, stop=True).then_inc(cd_filled, 1)

                def scores(c):
                    for s in range(2):
                        if c or later(b):
                            pe.wait_ge(Mt_ready, at(Mt_ready, b, 2 * (c - 1) + s + 1 if c else 0))
                        r = slice(64 * s, 64 * s + 64)
                        for k in range(KC):
                            ins = t_.matmul(ps[2 + s][:, k * P:(k + 1) * P], BT[r, c // 4, k, chunk(c)],
                                            CT[r, c // 4, k, chunk(c)], start=True, stop=True)
                        ins.then_inc(sc_filled, 1)

                def state(c):
                    pe.wait_ge(Bw_ready, at(Bw_ready, b, c + 1))
                    pe.wait_ge(Xd_ready, at(Xd_ready, b, c + 1))
                    if c or later(b):
                        pe.wait_ge(S_ready, at(S_ready, b, c))
                    for k in range(KC):
                        ins = t_.matmul(ps[5][:, k * P:(k + 1) * P], XB[:, c % 2, 1, k * P:(k + 1) * P],
                                        XB[:, c % 2, 0, k * P:(k + 1) * P], start=True, stop=True)
                    ins.then_inc(s_filled, 1)

                def output(c):
                    if c or later(b):
                        pe.wait_ge(y_ready, at(y_ready, b, c))
                    pe.wait_ge(Mt_ready, at(Mt_ready, b, 2 * c + 2))
                    if c:
                        if c or later(b):
                            pe.wait_ge(S_ready, at(S_ready, b, c))
                        pe.wait_ge(CE_ready, at(CE_ready, b, 4 * (c // 4) + 4))
                    for k in range(KC):
                        o = slice(k * P, (k + 1) * P)
                        for hh in range(2):
                            r = slice(64 * hh, 64 * hh + 64)
                            h = 2 * k + hh
                            ins = t_.matmul(ps[4][r, o], XB[:, c % 2, 0, h * 64:(h + 1) * 64],
                                            Mt[:, c % 2, hh * HALF + k * P:hh * HALF + (k + 1) * P],
                                            start=True, stop=True)
                        if c:
                            ins = t_.matmul(ps[4][:, o], Sbd[:, k, :], ECv[:, k, c * P:(c + 1) * P],
                                            start=False, stop=True, skip_group_check=True)
                    ins.then_inc(y_filled, 1)

                for i in range(4):
                    pe.wait_ge(proj.drained[i], at(proj.drained[i], b + 1, 0))
                if later(b):
                    for i in range(4):
                        pe.wait_ge(ffn.drained[i], at(ffn.drained[i], b - 1 + 1, 0))
                pe.wait_ge(*proj.read(b, J_B1 + 3))
                pe.wait_ge(*proj.read(b, J_B1 + 7))
                turn(0)
                cumdiff(0)
                scores(0)
                for c in range(T):
                    if c + 1 < T:
                        turn(c + 1)
                        cumdiff(c + 1)
                    if c < T - 1:
                        state(c)
                    output(c)
                    if c + 1 < T:
                        scores(c + 1)

            def out_(b):
                pe.wait_ge(pk_ready, at(pk_ready, b, 1))
                t_.matmul(ps[4][:, 0:2 * KC], halfmean[:, :], pk[:, 0:2, :].rearrange("p a n -> p (a n)"),
                          start=True, stop=True).then_inc(pk_filled, 1)
                pe.wait_ge(wog_ready, at(wog_ready, b, 1))
                for j in range(4):
                    pe.wait_ge(g_ready, at(g_ready, b, 4 * (j // 2) + 4))
                    for i in range(2):
                        t = 2 * j + i
                        for k in range(KC):
                            ins = t_.matmul(ps[j][:, i * D:(i + 1) * D], xT[:, k, t * P:(t + 1) * P],
                                            wog_s[:, k, :], start=k == 0, stop=k == KC - 1)
                    ins.then_inc(out_filled, 1)

            def ffn_wrow(b):
                pe.wait_ge(wcol_ready, at(wcol_ready, b, 1))
                for j in range(2):
                    if F_WROW + j >= 4:
                        pe.wait_ge(*ffn.read(b, F_WROW + j - 4))
                    bank = ffn.bank(F_WROW + j)
                    for i in range(4):
                        ins = t_.transpose(bank[:, i * P:(i + 1) * P],
                                           wcol[:, 4 * j + i:4 * j + i + 1].broadcast_to([P, P]), ident[:, :])
                    ins.then_inc(ffn.filled[(F_WROW + j) % 4], 1)

            def ffn_rank(b):
                if F_RANK >= 4:
                    pe.wait_ge(*ffn.read(b, F_RANK - 4))
                bank = ffn.bank(F_RANK)
                pe.wait_ge(G_ready, at(G_ready, b, T))
                for s in range(T):
                    for t in range(T):
                        ins = t_.matmul(bank[:, s:s + 1], Gt[:, t, s * P:(s + 1) * P], ones_b[:, :],
                                        start=t == 0, stop=t == T - 1)
                ins.then_inc(ffn.filled[F_RANK % 4], 1)

            def ffn_idx(b):
                if F_IDX >= 4:
                    pe.wait_ge(*ffn.read(b, F_IDX - 4))
                bank = ffn.bank(F_IDX)
                pe.wait_ge(P_ready, at(P_ready, b, T))
                for t in range(T):
                    ins = t_.matmul(bank[:, 0:1], Pm[:, t, :], tok[:, t:t + 1], start=t == 0, stop=t == T - 1)
                ins.then_inc(ffn.filled[F_IDX % 4], 1)

            def ffn_turn(b, q, src):
                if q >= 4:
                    pe.wait_ge(*ffn.read(b, q - 4))
                bank = ffn.bank(q)
                for k in range(KD):
                    ins = t_.transpose(bank[:, k * P:(k + 1) * P], src[:, k * P:(k + 1) * P], ident[:, :])
                ins.then_inc(ffn.filled[q % 4], 1)

            def ffn_mask(b):
                pe.wait_ge(mclamp_ready, at(mclamp_ready, b, 1))
                for j in range(2):
                    if F_MT + j >= 4:
                        pe.wait_ge(*ffn.read(b, F_MT + j - 4))
                    bank = ffn.bank(F_MT + j)
                    for i in range(4):
                        t = 4 * j + i
                        ins = t_.transpose(bank[:, i * P:(i + 1) * P], mrows[:, t * P:(t + 1) * P], ident[:, :])
                    ins.then_inc(ffn.filled[(F_MT + j) % 4], 1)

            def ffn_msel(b):
                if F_MSEL >= 4:
                    pe.wait_ge(*ffn.read(b, F_MSEL - 4))
                bank = ffn.bank(F_MSEL)
                pe.wait_ge(*ffn.read(b, F_MT + 1))
                for t in range(T):
                    ins = t_.matmul(bank[:, 0:P], mT[:, t, :], Pm[:, t, :], start=t == 0, stop=t == T - 1)
                ins.then_inc(ffn.filled[F_MSEL % 4], 1)

            def ffn_qkv(b):
                pe.wait_ge(*ffn.read(b, F_HNT))
                for q, o, w in ((F_QK, 0, 2 * D), (F_V, 2 * D, D)):
                    if q >= 4:
                        pe.wait_ge(*ffn.read(b, q - 4))
                    bank = ffn.bank(q)
                    for k in range(KD):
                        ins = t_.matmul(bank[:, 0:w], hnT[:, k, :], wqkv_s[:, k, o:o + w],
                                        start=k == 0, stop=k == KD - 1)
                    ins.then_inc(ffn.filled[q % 4], 1)

            def ffn_qT(b):
                pe.wait_ge(rope_ready, at(rope_ready, b, 1))
                for s in range(2):
                    if F_QT + s >= 4:
                        pe.wait_ge(*ffn.read(b, F_QT + s - 4))
                    bank = ffn.bank(F_QT + s)
                    for m in range(4):
                        ins = t_.transpose(bank[:, m * P:(m + 1) * P],
                                           qkr[:, s, 4 * m:4 * m + 4, :].rearrange("p h n -> p (h n)"), ident[:, :])
                    ins.then_inc(ffn.filled[(F_QT + s) % 4], 1)

            def ffn_scores(b):
                pe.wait_ge(*ffn.read(b, F_KT))
                for r in range(4):
                    if F_SC + r >= 4:
                        pe.wait_ge(*ffn.read(b, F_SC + r - 4))
                    bank = ffn.bank(F_SC + r)
                    s = slice(32 * r, 32 * r + 32)
                    for m in range(4):
                        ins = t_.matmul(bank[:, m * P:m * P + NSEL], qT[s, m, :], kT[s, m, 0:NSEL],
                                        start=True, stop=True)
                    ins.then_inc(ffn.filled[(F_SC + r) % 4], 1)

            def ffn_AT(b):
                for r in range(4):
                    if F_AT + r >= 4:
                        pe.wait_ge(*ffn.read(b, F_AT + r - 4))
                    bank = ffn.bank(F_AT + r)
                    pe.wait_ge(prob_ready, at(prob_ready, b, 4 * r + 4))
                    for m in range(4):
                        ins = t_.transpose(bank[0:NSEL, m * P:(m + 1) * P], scr[:, 4 * r + m, 0:NSEL], ident[:, :])
                    ins.then_inc(ffn.filled[(F_AT + r) % 4], 1)

            def ffn_av(b):
                if F_AV >= 4:
                    pe.wait_ge(*ffn.read(b, F_AV - 4))
                bank = ffn.bank(F_AV)
                pe.wait_ge(*ffn.read(b, F_AT + 3))
                pe.wait_ge(*ffn.read(b, F_V))
                for r in range(4):
                    for m in range(4):
                        o = (4 * m + r) * HD
                        ins = t_.matmul(bank[:, o:o + HD], AT[0:NSEL, 4 * r + m, :], vs[0:NSEL, o:o + HD],
                                        start=True, stop=True)
                ins.then_inc(ffn.filled[F_AV % 4], 1)

            def ffn_wo(b):
                if F_WO >= 4:
                    pe.wait_ge(*ffn.read(b, F_WO - 4))
                bank = ffn.bank(F_WO)
                pe.wait_ge(*ffn.read(b, F_OT))
                for k in range(KD):
                    ins = t_.matmul(bank[:, 0:D], oT[:, k, :], fwo_s[:, k, :], start=k == 0, stop=k == KD - 1)
                ins.then_inc(ffn.filled[F_WO % 4], 1)

            def ffn_w1(b):
                pe.wait_ge(*ffn.read(b, F_HNBT))
                for j in range(2):
                    if F_W1 + j >= 4:
                        pe.wait_ge(*ffn.read(b, F_W1 + j - 4))
                    bank = ffn.bank(F_W1 + j)
                    for i in range(4):
                        f = 4 * j + i
                        for k in range(KD):
                            ins = t_.matmul(bank[:, i * P:(i + 1) * P], w1_s[:, k, f * P:(f + 1) * P], hnT[:, k, :],
                                            start=k == 0, stop=k == KD - 1)
                    ins.then_inc(ffn.filled[(F_W1 + j) % 4], 1)

            def ffn_w2(b):
                if F_W2 >= 4:
                    pe.wait_ge(*ffn.read(b, F_W2 - 4))
                bank = ffn.bank(F_W2)
                pe.wait_ge(*ffn.read(b, F_W1 + 1))
                for f in range(FT):
                    ins = t_.matmul(bank[:, 0:D], gT[:, f, :], w2_s[:, f, :], start=f == 0, stop=f == FT - 1)
                ins.then_inc(ffn.filled[F_W2 % 4], 1)

            def batch(b, f):
                ln_in(b)
                if f is not None:
                    ffn_wrow(f)
                x_proj(b)
                if f is not None:
                    ffn_rank(f)
                    ffn_idx(f)
                z_proj(b, 0)
                if f is not None:
                    pe.wait_ge(hn_ready, at(hn_ready, f, 1))
                    ffn_turn(f, F_HNT, hn)
                    ffn_mask(f)
                z_proj(b, 1)
                if f is not None:
                    ffn_msel(f)
                    ffn_qkv(f)
                dt_proj(b)
                if f is not None:
                    ffn_qT(f)
                    ffn_scores(f)
                bc_proj(b, 0, range(0, 8))
                if f is not None:
                    ffn_AT(f)
                    ffn_av(f)
                    pe.wait_ge(*ffn.read(f, F_AV))
                    ffn_turn(f, F_OT, ob)
                    ffn_wo(f)
                    pe.wait_ge(hnb_ready, at(hnb_ready, f, 1))
                    ffn_turn(f, F_HNBT, hn)
                    ffn_w1(f)
                    ffn_w2(f)
                decay_jobs(b)
                bc_proj(b, 1, range(0, 8))
                carry_rows(b)
                scan(b)
                out_(b)

            batch(0, None)
            pe.wait_ge(fload, 16 * len(ffn_loads))
            pe.wait_ge(setup_dve, SD_ALL)
            with pe.Fori(1, NB) as b:
                batch(b, b - 1)
            f = NB - 1
            ffn_wrow(f)
            ffn_rank(f)
            ffn_idx(f)
            pe.wait_ge(hn_ready, at(hn_ready, f, 1))
            ffn_turn(f, F_HNT, hn)
            ffn_mask(f)
            ffn_msel(f)
            ffn_qkv(f)
            ffn_qT(f)
            ffn_scores(f)
            ffn_AT(f)
            ffn_av(f)
            pe.wait_ge(*ffn.read(f, F_AV))
            ffn_turn(f, F_OT, ob)
            ffn_wo(f)
            pe.wait_ge(hnb_ready, at(hnb_ready, f, 1))
            ffn_turn(f, F_HNBT, hn)
            ffn_w1(f)
            ffn_w2(f)


def kernel(**inputs):
    import concourse.bacc as bacc
    import numpy as np
    from concourse.bass_utils import run_bass_kernel_spmd

    def arr(name):
        return np.asarray(inputs[name])

    def by_partition(w):
        return np.ascontiguousarray(w.reshape(-1, P, w.shape[-1]).transpose(1, 0, 2))

    rep = INNER // HEADS
    columns = np.concatenate([
        arr("L0_attn_conv_w")[:, 0, :], arr("L0_attn_conv_b")[:, None],
        np.repeat(arr("L0_attn_d_param"), rep)[:, None], arr("L0_attn_gn_w")[:, None],
        arr("L0_attn_gn_b")[:, None]], axis=1)
    lncols = np.stack([arr("L0_ffn_ln1").reshape(KD, P).T, arr("L0_ffn_ln2").reshape(KD, P).T], axis=1)
    arrays = {
        "x": arr("L0_attn_input_tensor"),
        "wxT": arr("L0_attn_Wx").T, "wzT": arr("L0_attn_Wz").T, "wbT": arr("L0_attn_Wb").T,
        "wcT": arr("L0_attn_Wc").T, "wdtT": np.tile(arr("L0_attn_Wdt").T, (1, G3)), "woT": arr("L0_attn_Wout").T,
        "cols": by_partition(columns),
        "rows48": np.tile(np.stack([arr("L0_attn_b_dt"), arr("L0_attn_log_a")], axis=1), (G3, 1)),
        "mask": arr("L0_ffn_attention_mask").reshape(MB * L, L),
        "pos": arr("L0_ffn_position_ids").reshape(MB * L, 1),
        "rw": arr("L0_ffn_router_w").reshape(D), "rb": arr("L0_ffn_router_b"),
        "wqkv": np.concatenate([arr("L0_ffn_wq"), arr("L0_ffn_wk"), arr("L0_ffn_wv")], axis=1),
        "wo": arr("L0_ffn_wo"), "w1": arr("L0_ffn_w1"), "w2": arr("L0_ffn_w2"), "lncols": lncols,
        "cT": arr("L0_c").T, "wmod": arr("L0_wmod"),
    }
    nc = bacc.Bacc("TRN2", target_bir_lowering=False, num_devices=1)
    aps = {}
    for name, a in arrays.items():
        arrays[name] = a = np.ascontiguousarray(a)
        aps[name] = nc.dram_tensor(name, a.shape, mybir.dt.from_np(a.dtype), kind="ExternalInput").ap()
    out = nc.dram_tensor("out", (NB * L, D), F32, kind="ExternalOutput").ap()
    adaln_block(nc, out=out, **aps)
    result = run_bass_kernel_spmd(nc, [arrays], core_ids=[0])
    return result.results[0]["out"].reshape(NB, L, D)
```

```python
from contextlib import ExitStack

import concourse.bass as bass
from concourse import mybir
from concourse.alu_op_type import AluOpType as ALU

F32 = mybir.dt.float32
BF16 = mybir.dt.bfloat16
I32 = mybir.dt.int32
U32 = mybir.dt.uint32
ACT = mybir.ActivationFunctionType
AX = mybir.AxisListType

P = 128
NB, L, D = 8, 1024, 256
MB = 4
INNER, HEADS, STATE, TAPS = 512, 8, 64, 4
T = L // P
KD, KC = D // P, INNER // P
HALF = L // 2
G3 = 6
RW = G3 * HEADS
FH, HD, F = 16, 16, 1024
KSEL = L // 8
NSEL = KSEL - 1
FT = F // P
EPS = 1e-5
MASKED = -1e30
ROPE_BASE = 10000.0
PI = 3.141592653589793
ROUND = 12582912.0
TWO_PI = (6.28125, 0.0019352436065673828, 6.35732715934e-08)
SD_MOD, SD_MIX, SD_ALL = 10, 14, 18
SP_ALL = 66
CHAINS = {"A": 2, "V": 13, "D": 14, "S": 3, "G": 17, "R": 29, "O": 8}


PER_BATCH = {}


def at(sem, b, k):
    return b * PER_BATCH[id(sem)] + k


def later(b):
    return not isinstance(b, int) or b > 0


class Chain:

    def __init__(self, sem, name):
        self.sem, self.name, self.k = sem, name, 0

    def __call__(self, eng, b, ins):
        ins.then_inc(self.sem, 1)
        self.k += 1
        eng.wait_ge(self.sem, at(self.sem, b, self.k))

    def end(self):
        assert self.k == CHAINS[self.name], (self.name, self.k)
        self.k = 0


class Ring:

    def __init__(self, banks, filled, drained):
        self.banks, self.filled, self.drained = banks, filled, drained

    def bank(self, q):
        return self.banks[q % 4]

    def full(self, b, q):
        return self.filled[q % 4], at(self.filled[q % 4], b, q // 4 + 1)

    def read(self, b, q):
        return self.drained[q % 4], at(self.drained[q % 4], b, q // 4 + 1)


def adaln_block(nc, x, wxT, wzT, wbT, wcT, wdtT, woT, cols, rows48, mask, pos, rw, rb,
                wqkv, wo, w1, w2, lncols, cT, wmod, out):
    ctx = ExitStack()
    with ctx:
        def sb(name, shape, dt=F32):
            return ctx.enter_context(nc.sbuf_tensor(name, shape, dt))

        def chunk(c):
            return slice((c % 4) * P, (c % 4) * P + P)

        def sig(name, per=1):
            sem = ctx.enter_context(nc.semaphore(name))
            PER_BATCH[id(sem)] = per
            return sem

        mod_d = nc.dram_tensor("mod_scratch", (NB, 6 * D), F32, kind="Internal").ap()
        x1_d = nc.dram_tensor("x1_scratch", (L, D), F32, kind="Internal").ap()

        wx_s = sb("wx_s", [P, KD, INNER])
        wz_s = sb("wz_s", [P, KD, INNER])
        wb_s = sb("wb_s", [P, KC, INNER])
        wc_s = sb("wc_s", [P, KC, INNER])
        wdt_s = sb("wdt_s", [P, KC, RW])
        wo_s = sb("wo_s", [P, KC, D])
        wqkv_s = sb("wqkv_s", [P, KD, 3 * D])
        fwo_s = sb("fwo_s", [P, KD, D])
        w1_s = sb("w1_s", [P, KD, F])
        w2_s = sb("w2_s", [P, FT, D])
        cols_s = sb("cols_s", [P, KC, 8])
        ln_s = sb("ln_s", [P, 2, KD])
        r48_s = sb("r48_s", [RW, 2])
        rw_s = sb("rw_s", [P, D])
        rb_s = sb("rb_s", [P, 1])
        ident = sb("ident", [P, P])
        identb = sb("identb", [P, P], BF16)
        causal = sb("causal", [P, 4, P], BF16)
        ones_b = sb("ones_b", [P, 1], BF16)
        tri = sb("tri", [P, P])
        halfmean = sb("halfmean", [P, P])
        iota_r = sb("iota_r", [P, P])
        tok = sb("tok", [P, T])
        ones4 = sb("ones4", [P, KC, T])
        spare = sb("spare", [P, 4])
        mhalf = sb("mhalf", [P, T])
        gmask = sb("gmask", [RW, 8])
        gneg = sb("gneg", [RW, 1])
        delta = sb("delta", [RW, HEADS])
        selp = sb("selp", [RW, 4, P], BF16)
        reset = sb("reset", [RW, T, P], BF16)
        zero48 = sb("zero48", [RW, 1])
        aneg = sb("aneg", [RW, 1])
        invf = sb("invf", [P, 2, HD // 2])
        phase = sb("phase", [P, 2, 2, HD // 2])
        mcol = sb("mcol", [P, 4, NB])
        mc = sb("mc", [P, 4])
        modrow = sb("modrow", [P, 4, D])
        xr = sb("xr", [P, T, D])
        hT = sb("hT", [P, KD, L])
        xc = sb("xc", [P, KC * (L + TAPS - 1) + 4])
        xT = sb("xT", [P, KC, L])
        zs = sb("zs", [P, KC, L])
        BT = sb("BT", [P, 2, KC, HALF])
        CT = sb("CT", [P, 2, KC, HALF])
        EC = sb("EC", [P, KC * L])
        Lw = sb("Lw", [RW, L], BF16)
        dw = sb("dw", [P, T, 2 * HEADS])
        dec = sb("dec", [P, KC, T])
        st6 = sb("st6", [P, T, 6])
        mv = sb("mv", [P, T, 2])
        rstd = sb("rstd", [P, T])
        Sbd = sb("Sbd", [P, KC, P])
        Sdc = sb("Sdc", [P, KC, P])
        Eg = sb("Eg", [P, 2 * HALF])
        Mt = sb("Mt", [P, 2, 2 * HALF])
        XB = sb("XB", [P, 2, 2, INNER])
        yst = sb("yst", [P, KC, 12])
        ymv = sb("ymv", [P, KC, 2])
        pk = sb("pk", [P, 4, KC])
        gab = sb("gab", [P, 6, KC])
        st6b = sb("st6b", [P, T, 6])
        mvb = sb("mvb", [P, T, 2])
        rstdb = sb("rstdb", [P, T])
        wcol = sb("wcol", [P, T])
        c0 = sb("c0", [P, 1])
        boff = sb("boff", [P, 1])
        moff = sb("moff", [P, 1])
        rank = sb("rank", [P, T])
        self_ = sb("self_", [P, 2])
        xidx = sb("xidx", [P, 1], U32)
        gidx = sb("gidx", [P, 1], U32)
        midx = sb("midx", [P, 1], U32)
        posi = sb("posi", [P, 1], I32)
        posf = sb("posf", [P, 1])
        sm = sb("sm", [P, 16])
        st1 = sb("st1", [P, 6])
        ang = sb("ang", [P, 2, HD // 2])
        trn = sb("trn", [P, 2, HD // 2])
        sc_ = sb("sc_", [P, 2, HD // 2])
        mx = sb("mx", [P, FH])
        den = sb("den", [P, FH])

        xcv = xc[:, 0:KC * (L + TAPS - 1)].rearrange("p (k n) -> p k n", k=KC)
        R8 = xc[0:RW, 0:4 * L].bitcast(BF16).rearrange("p (h n) -> p h n", h=HEADS)
        ECv = EC[:, :].rearrange("p (k n) -> p k n", k=KC)
        v48, dt48 = xc[0:RW, 0:L], xc[0:RW, L:2 * L]
        lo = xc[0:RW, 2 * L:2 * L + HALF].bitcast(BF16)
        Rw = Sdc[0:RW, :, :].rearrange("p a b -> p (a b)").bitcast(BF16)
        xin = BT[:, 0, :, :].rearrange("p a n -> p (a n)").rearrange("p (t n) -> p t n", t=T)
        h2 = EC[:, 0:T * D].rearrange("p (t n) -> p t n", t=T)
        wog_s = CT[:, 0, 0:2, :].rearrange("p a n -> p (a n)").rearrange("p (k n) -> p k n", k=KC)
        rwc, cg, sg = CT[:, 1, 0, 0:D], CT[:, 1, 0, D:2 * D], CT[:, 1, 1, 0:D]
        a48 = hT[0:RW, 0, :]
        b48 = hT[0:RW, 1, :]
        hi = hT[0:RW, 1, 0:HALF].bitcast(BF16)
        mid = hT[0:RW, 1, HALF:L].bitcast(BF16)
        Gt = EC[:, :].bitcast(BF16).rearrange("p (t n) -> p t n", t=T)
        scr = EC[:, 0:2048].rearrange("p (h n) -> p h n", h=FH)
        AT = EC[:, 2048:4096].rearrange("p (h n) -> p h n", h=FH)
        qk = EC[:, 0:512]
        rt = EC[:, 512:1024]
        qkr = EC[:, 2048:3072].rearrange("p (s h n) -> p s h n", s=2, h=FH)
        qT = EC[:, 3072:3584].rearrange("p (m n) -> p m n", m=4)
        kT = EC[:, 3584:4096].rearrange("p (m n) -> p m n", m=4)
        wrow = Eg
        Pm = Mt[:, 0, :].rearrange("p (t n) -> p t n", t=T)
        mrows = Mt[:, 1, :]
        mT = XB[:, 0, :, :].rearrange("p a b -> p (a b)").rearrange("p (t n) -> p t n", t=T)
        gT = XB[:, 1, :, :].rearrange("p a b -> p (a b)").rearrange("p (t n) -> p t n", t=FT)
        xs, hs, hn, vs, ob, x1s, hnT_, oT_ = (xr[:, i, :] for i in range(8))
        hnT = hnT_.rearrange("p (k n) -> p k n", k=KD)
        oT = oT_.rearrange("p (k n) -> p k n", k=KD)
        msel = Sbd[:, 0, :]
        junk = oT_
        junkf = Mt[:, 1, :]

        junkt = XB[:, 1, :, :].rearrange("p a b -> p (a b)")
        junkd = Mt[:, 0, 0:2 * D].rearrange("p (a n) -> p a n", a=2)
        mcin_s = sb("mcin_s", [P, KD, NB])
        mcin = mcin_s[:, :, :]
        wmod_s = xT[:, 0:3, :].rearrange("p k n -> p (k n)")[:, 0:KD * 6 * D].rearrange("p (k n) -> p k n", k=KD)
        mod8 = CT[0:NB, 1, :, :].rearrange("p a n -> p (a n)")[:, 0:6 * D]
        sgn8, abs8 = EC[0:NB, L:L + D], EC[0:NB, L + D:L + 2 * D]
        dlt6 = EC[0:RW, 0:RW].rearrange("p (g h) -> p g h", g=G3)
        delt3 = sb("delt3", [RW, HEADS])

        ps = [ctx.enter_context(nc.psum_tensor(f"ps{i}", [P, 512], F32)) for i in range(8)]

        wload = ctx.enter_context(nc.semaphore("weights_loaded"))
        fload = ctx.enter_context(nc.semaphore("ffn_weights_loaded"))
        mload = ctx.enter_context(nc.semaphore("mod_inputs_loaded"))
        setup_pool = ctx.enter_context(nc.semaphore("setup_pool"))
        setup_dve = ctx.enter_context(nc.semaphore("setup_dve"))
        setup_act = ctx.enter_context(nc.semaphore("setup_act"))
        setup_pe = ctx.enter_context(nc.semaphore("setup_pe"))
        mod_stored = ctx.enter_context(nc.semaphore("mod_stored"))
        x_loaded = sig("x_loaded", 16)
        xr_loaded = sig("xr_loaded", 16)
        modrow_loaded = sig("modrow_loaded", 16)
        mc_ready = sig("mc_ready")
        var_ready = sig("var_ready")
        rstd_ready = sig("rstd_ready")
        xn_ready = sig("xn_ready", T)
        conv_ready = sig("conv_ready", 8)
        xT_ready = sig("xT_ready", 8)
        u_ready = sig("dt_u_ready")
        l_ready = sig("dt_log_ready", 2)
        dif_ready = sig("dif_ready")
        wexp_ready = sig("wexp_ready")
        rows_ready = sig("decay_rows_ready")
        v_ready = sig("v_ready")
        dec_ready = sig("dec_ready")
        CE_ready = sig("CE_ready", 8)
        cd_filled = sig("cumdiff_filled", 2 * T)
        Eg_ready = sig("decay_ready", 2 * T)
        sc_filled = sig("scores_filled", 2 * T)
        Mt_ready = sig("masked_scores_ready", 2 * T)
        xt_filled = sig("xt_filled", T)
        bt_filled = sig("bt_filled", T - 1)
        Xd_ready = sig("Xd_ready", T)
        Bw_ready = sig("Bw_ready", T - 1)
        y_filled = sig("y_filled", T)
        y_ready = sig("y_ready", T)
        s_filled = sig("s_filled", T - 1)
        S_ready = sig("state_ready", T - 1)
        Sdc_ready = sig("state_decayed", T - 2)
        pk_ready = sig("gn_stats_ready")
        pk_filled = sig("gn_stats_filled")
        gvar_ready = sig("gn_var_ready")
        grstd_ready = sig("gn_rstd_ready")
        wog_ready = sig("wog_ready")
        yn_ready = sig("yn_ready", 8)
        g_ready = sig("gated_ready", 4)
        out_filled = sig("out_filled", 4)
        x1_ready = sig("x1_ready", 4)
        var2_ready = sig("var2_ready", 4)
        rstd2_ready = sig("rstd2_ready", 4)
        hn2_ready = sig("hn2_ready", T)
        w_ready = sig("w_ready", T)
        rows2_ready = sig("folded_rows_ready")
        c0_ready = sig("router_constant_ready")
        gd_ready = sig("gated_by_dve_ready", 4)
        wcol_ready = sig("wcol_ready")
        base_ready = sig("base_ready", 4)
        x1_stored = sig("x1_stored", 64)
        base_stored = sig("base_stored", 64)
        G_ready = sig("compare_ready", T)
        P_ready = sig("onehot_ready", T)
        gidx_ready = sig("gidx_ready")
        xs_loaded = sig("xs_gathered", 16)
        m_loaded = sig("mask_gathered", 16)
        pos_loaded = sig("pos_gathered", 16)
        fv_ready = sig("ffn_var_ready")
        fr_ready = sig("ffn_rstd_ready")
        fs_ready = sig("ffn_rms1_ready")
        frr_ready = sig("ffn_rms1_inv")
        fs2_ready = sig("ffn_rms2_ready")
        frr2_ready = sig("ffn_rms2_inv")
        hn_ready = sig("ffn_hn_ready")
        mclamp_ready = sig("mask_clamped")
        msel_ready = sig("msel_ready")
        qkz_ready = sig("rope_pad_zero")
        qk_ready = sig("qk_ready")
        ang_ready = sig("angles_ready")
        sin_ready = sig("sin_ready")
        rope_ready = sig("rope_ready")
        scr_ready = sig("scr_ready", 4)
        mx_ready = sig("max_ready")
        prob_ready = sig("prob_ready", FH)
        den_ready = sig("den_ready")
        x1s_ready = sig("x1s_ready")
        hnb_ready = sig("ffn_hn2_ready")
        so_ready = sig("proc_ready")
        scattered = sig("scattered", 16)

        def ring(name, banks, jobs):
            return Ring(banks, [sig(f"{name}_filled{i}", len(range(i, jobs, 4))) for i in range(4)],
                        [sig(f"{name}_drained{i}", len(range(i, jobs, 4))) for i in range(4)])

        proj = ring("proj", ps[0:4], 47)
        ffn = ring("ffn", ps[4:8], 27)
        J_H, J_X, J_Z, J_DT, J_V, J_EC = 0, 4, 12, 28, 36, 39
        J_BC = ((20, 21, 22, 23, 24, 25, 26, 27), (30, 31, 32, 33, 34, 35, 37, 38))
        (F_WROW, F_RANK, F_IDX, F_HNT, F_MT, F_MSEL, F_QK, F_V, F_QT, F_KT, F_SC, F_AT, F_AV, F_OT, F_WO,
         F_HNBT, F_W1, F_W2) = 0, 2, 3, 4, 5, 7, 8, 9, 10, 11, 12, 16, 20, 21, 22, 23, 24, 26

        chA, chV, chD, chS, chG, chR, chO = (Chain(sig("chain" + c, CHAINS[c]), c) for c in "AVDSGRO")

        block = ctx.enter_context(nc.Block())

        def kp(w):
            return w.rearrange("(k p) n -> p k n", p=P)

        mixer_loads = ((r48_s[:, :], rows48), (cols_s[:, :, :], cols), (wx_s[:, :, :], kp(wxT)),
                       (wz_s[:, :, :], kp(wzT)), (wdt_s[:, :, :], kp(wdtT)), (wb_s[:, :, :], kp(wbT)),
                       (wc_s[:, :, :], kp(wcT)), (wo_s[:, :, :], kp(woT)), (rw_s[:, :], rw.partition_broadcast(P)),
                       (rb_s[:, :], rb.partition_broadcast(P)))
        ffn_loads = ((wqkv_s[:, :, :], kp(wqkv)), (fwo_s[:, :, :], kp(wo)), (w1_s[:, :, :], kp(w1)),
                     (w2_s[:, :, :], kp(w2)), (ln_s[:, :, :], lncols))

        @block.sync
        def _(sp):

            sp.dma_start(mcin, cT.rearrange("(k p) n -> p k n", p=P)).then_inc(mload, 16)
            sp.dma_start(wmod_s, kp(wmod)).then_inc(mload, 16)
            sp.dma_start(xin[:, :, :], x[0, :, :].rearrange("(t p) n -> p t n", p=P)).then_inc(x_loaded, 16)
            for dst, src in mixer_loads:
                sp.dma_start(dst, src).then_inc(wload, 16)
            for dst, src in ffn_loads:
                sp.dma_start(dst, src).then_inc(fload, 16)
            sp.wait_ge(setup_dve, SD_MOD)
            sp.dma_start(mod_d[:, :], mod8).then_inc(mod_stored, 16)
            sp.wait_ge(mod_stored, 16)

            def loads(b):
                if later(b):
                    sp.wait_ge(so_ready, at(so_ready, b - 1, 1))
                if later(b):
                    sp.wait_ge(scattered, at(scattered, b - 1, 16))
                sp.dma_start(modrow[:, :, :].rearrange("p a n -> p (a n)"),
                             mod_d[bass.ds(b, 1), 2 * D:6 * D].rearrange("a n -> (a n)").partition_broadcast(P)
                             ).then_inc(modrow_loaded, 16)
                sp.dma_start(xr[:, :, :], x[bass.ds(b, 1), :, :].rearrange("a (t p) n -> p (a t) n", p=P)
                             ).then_inc(xr_loaded, 16)

            def prefetch(b):
                sp.wait_ge(sc_filled, at(sc_filled, b, 8))
                sp.wait_ge(bt_filled, at(bt_filled, b, 4))
                sp.dma_start(xin[:, :, :], x[bass.ds(b + 1, 1), :, :].rearrange("a (t p) n -> p (a t) n", p=P)
                             ).then_inc(x_loaded, 16)

            def stores(b):
                for j in range(4):
                    rows = slice(2 * j, 2 * j + 2)
                    sp.wait_ge(x1_ready, at(x1_ready, b, j + 1))
                    sp.dma_start(x1_d[2 * j * P:2 * (j + 1) * P, :].rearrange("(t p) n -> p t n", p=P),
                                 xr[:, rows, :]).then_inc(x1_stored, 16)
                    sp.wait_ge(base_ready, at(base_ready, b, j + 1))
                    sp.dma_start(out[bass.ds(b * L + 2 * j * P, 2 * P), :].rearrange("(t p) n -> p t n", p=P),
                                 h2[:, rows, :]).then_inc(base_stored, 16)

            loads(0)
            prefetch(0)
            stores(0)
            with sp.Fori(1, NB - 1) as b:
                loads(b)
                prefetch(b)
                stores(b)
            loads(NB - 1)
            stores(NB - 1)
            sp.wait_ge(x1_stored, at(x1_stored, NB - 1, 64))
            sp.wait_ge(base_stored, at(base_stored, NB - 1, 64))
            sp.wait_ge(scattered, at(scattered, NB - 1, 16))

        @block.gpsimd
        def _(pool):
            g = nc.gpsimd
            n = [0]

            def link(ins):
                ins.then_inc(setup_pool, 1)
                n[0] += 1
                pool.wait_ge(setup_pool, n[0])

            link(g.memset(ident[:, :], 0.0))
            link(g.affine_select(out=ident[:, :], in_=ident[:, :], compare_op=ALU.not_equal, fill=1.0,
                                 base=0, pattern=[[-1, P]], channel_multiplier=1))
            link(g.tensor_copy(identb[:, :], ident[:, :]))
            link(g.memset(tri[:, :], 1.0))
            link(g.affine_select(out=tri[:, :], in_=tri[:, :], compare_op=ALU.is_gt, fill=0.0,
                                 base=0, pattern=[[1, P]], channel_multiplier=-1))
            link(g.memset(causal[:, :, :], 0.0))
            link(g.affine_select(out=causal[:, :, :], in_=causal[:, :, :], compare_op=ALU.is_ge, fill=MASKED,
                                 base=0, pattern=[[0, 4], [1, P]], channel_multiplier=-1))
            link(g.memset(ones_b[:, :], 1.0))
            link(g.memset(halfmean[:, :], 0.0))
            link(g.memset(halfmean[0:64, 0:64], 1.0 / STATE))
            link(g.memset(halfmean[64:128, 64:128], 1.0 / STATE))
            link(g.iota(iota_r[:, :], pattern=[[1, P]], base=0, channel_multiplier=0,
                        allow_small_or_imprecise_dtypes=True))
            link(g.iota(tok[:, :], pattern=[[P, T]], base=0, channel_multiplier=1,
                        allow_small_or_imprecise_dtypes=True))
            link(g.memset(mhalf[:, :], -0.5))
            link(g.memset(ones4[:, :, :], 1.0))
            link(g.memset(spare[:, :], 0.0))
            for i in range(G3 + 2):
                first, last = (i, i) if i < G3 else ((0, 2) if i == G3 else (3, 5))
                link(g.memset(gmask[:, i:i + 1], 1.0))
                link(g.affine_select(out=gmask[:, i:i + 1], in_=gmask[:, i:i + 1], compare_op=ALU.is_ge,
                                     fill=0.0, base=-HEADS * first, pattern=[[0, 1]], channel_multiplier=1))
                link(g.affine_select(out=gmask[:, i:i + 1], in_=gmask[:, i:i + 1], compare_op=ALU.is_ge,
                                     fill=0.0, base=HEADS * last + HEADS - 1, pattern=[[0, 1]],
                                     channel_multiplier=-1))
            link(g.tensor_scalar(gneg[:, :], gmask[:, G3:G3 + 1], -1.0, None, ALU.mult))
            link(g.memset(dlt6, 0.0))
            link(g.affine_select(out=dlt6, in_=dlt6, compare_op=ALU.not_equal, fill=1.0, base=0,
                                 pattern=[[-HEADS, G3], [-1, HEADS]], channel_multiplier=1))
            for i in range(G3):
                link(g.tensor_copy(delta[:, :], dlt6[:, 0, :]) if i == 0 else
                     g.tensor_tensor(delta[:, :], delta[:, :], dlt6[:, i, :], ALU.add))
            link(g.memset(reset[:, :, :], 1.0))
            link(g.memset(reset[:, :, 0:1], 0.0))
            for i in range(HD // 2):
                link(g.memset(invf[:, :, i:i + 1], 1.0 / ROPE_BASE ** (2.0 * i / HD)))
            link(g.memset(phase[:, :, 0, :], 0.0))
            link(g.memset(phase[:, 0, 1, :], 0.25))
            link(g.memset(phase[:, 1, 1, :], PI / 2))
            link(g.memset(Sbd[:, :, :], 0.0))
            link(g.memset(Sdc[:, :, :], 0.0))
            link(g.memset(boff[:, :], 0.0))
            link(g.memset(zero48[:, :], 0.0))
            assert n[0] == SP_ALL, n[0]

            def ln_in(b):
                pool.wait_ge(var_ready, at(var_ready, b, 1))
                g.tensor_tensor(rstd[:, :], rstd[:, :], mhalf[:, :], ALU.pow).then_inc(rstd_ready, 1)

            def carry(b):
                pool.wait_ge(*proj.read(b, J_EC + 7))
                g.tensor_tensor(dec[:, :, :], ECv[:, :, P - 1::P], ones4[:, :, :], ALU.mult).then_inc(dec_ready, 1)
                pool.wait_ge(dec_ready, at(dec_ready, b, 1))
                pool.wait_ge(*proj.read(b, J_BC[1][7]))
                for half in range(2):
                    for k in range(KC):
                        s = ECv[:, k, half * HALF:(half + 1) * HALF]
                        g.tensor_tensor(s, s, CT[:, half, k, :], ALU.mult).then_inc(CE_ready, 1)

            def decays(b):
                for c in range(1, T - 1):
                    pool.wait_ge(S_ready, at(S_ready, b, c))
                    g.tensor_tensor(Sdc[:, :, :], Sbd[:, :, :], dec[:, :, c:c + 1].broadcast_to([P, KC, P]),
                                    ALU.mult).then_inc(Sdc_ready, 1)
                    if c == 5:
                        pool.wait_ge(modrow_loaded, at(modrow_loaded, b, 16))
                        pool.wait_ge(sc_filled, at(sc_filled, b, 8))
                        g.tensor_tensor(wog_s, wo_s[:, :, :], modrow[:, 0:1, :].broadcast_to([P, KC, D]),
                                        ALU.mult).then_inc(wog_ready, 1)

            def fold_rows(b):
                pool.wait_ge(sc_filled, at(sc_filled, b, 16))
                g.tensor_tensor(rwc, modrow[:, 2, :], rw_s[:, :], ALU.mult)
                g.tensor_tensor(cg, modrow[:, 2, :], modrow[:, 3, :], ALU.mult)
                g.tensor_tensor(sg, modrow[:, 1, :], modrow[:, 3, :], ALU.mult).then_inc(rows2_ready, 1)

            def out_(b):
                fold_rows(b)
                pool.wait_ge(gvar_ready, at(gvar_ready, b, 1))
                g.tensor_tensor(gab[:, 1, :], gab[:, 0, :], mhalf[:, 0:KC], ALU.pow).then_inc(grstd_ready, 1)
                for half in range(2):
                    for k in range(2):
                        s = slice(half * HALF, (half + 1) * HALF)
                        pool.wait_ge(yn_ready, at(yn_ready, b, half * KC + k + 1))
                        g.tensor_tensor(xT[:, k, s], xT[:, k, s], zs[:, k, s], ALU.mult).then_inc(g_ready, 1)
                for j in range(4):
                    pool.wait_ge(var2_ready, at(var2_ready, b, j + 1))
                    q = slice(2 * j, 2 * j + 2)
                    g.tensor_tensor(rstdb[:, q], rstdb[:, q], mhalf[:, q], ALU.pow).then_inc(rstd2_ready, 1)
                    if j:
                        base(b, j - 1)
                base(b, 3)
                chO.end()

            def base(b, j):
                q = slice(2 * j, 2 * j + 2)
                pool.wait_ge(w_ready, at(w_ready, b, 2 * j + 2))
                for i, row in enumerate((cg, sg)):
                    chO(pool, b, g.tensor_tensor(h2[:, q, :], h2[:, q, :],
                                                 row.unsqueeze(1).broadcast_to([P, 2, D]),
                                                 ALU.add if i else ALU.mult))
                g.tensor_tensor(h2[:, q, :], h2[:, q, :], xr[:, q, :], ALU.add).then_inc(base_ready, 1)

            def take_waits():
                g.tensor_tensor(spare[:, 0:1], mhalf[:, 0:1], mhalf[:, 1:2], ALU.mult)

            def gather(b):
                pool.wait_ge(gidx_ready, at(gidx_ready, b, 1))
                pool.wait_ge(x1_stored, at(x1_stored, b, 64))
                take_waits()
                g.indirect_dma_start(xs, None, x1_d[:, :], bass.IndirectOffsetOnAxis(ap=xidx[:, 0:1], axis=0)
                                     ).then_inc(xs_loaded, 16)
                g.indirect_dma_start(mrows, None, mask, bass.IndirectOffsetOnAxis(ap=midx[:, 0:1], axis=0)
                                     ).then_inc(m_loaded, 16)
                g.indirect_dma_start(posi[:, :], None, pos, bass.IndirectOffsetOnAxis(ap=midx[:, 0:1], axis=0)
                                     ).then_inc(pos_loaded, 16)
                g.memset(qkr[:, :, :, HD:2 * HD], 0.0).then_inc(qkz_ready, 1)

            def small_pow(b, before, after, col):
                pool.wait_ge(before, at(before, b, 1))
                g.tensor_tensor(sm[:, col + 1:col + 2], sm[:, col:col + 1], mhalf[:, 0:1], ALU.pow
                                ).then_inc(after, 1)

            def scatter(b):
                pool.wait_ge(so_ready, at(so_ready, b, 1))
                pool.wait_ge(base_stored, at(base_stored, b, 64))
                take_waits()
                g.indirect_dma_start(out, bass.IndirectOffsetOnAxis(ap=gidx[0:NSEL, 0:1], axis=0),
                                     x1s[0:NSEL, :], None).then_inc(scattered, 16)

            def ffn_all(b):
                gather(b)
                small_pow(b, fv_ready, fr_ready, 0)
                small_pow(b, fs_ready, frr_ready, 2)
                small_pow(b, fs2_ready, frr2_ready, 4)
                scatter(b)

            def rest(b, last=False):
                carry(b)
                decays(b)
                if not last:
                    ln_in(b + 1)
                out_(b)

            ln_in(0)
            rest(0)
            with pool.Fori(1, NB - 1) as b:
                ffn_all(b - 1)
                rest(b)
            ffn_all(NB - 2)
            rest(NB - 1, last=True)
            ffn_all(NB - 1)

        @block.scalar
        def _(act):
            a = nc.scalar
            act.wait_ge(mload, 16 * 2)
            a.activation(mcin, mcin, ACT.Silu).then_inc(setup_act, 1)
            for j in range(3):
                act.wait_ge(setup_pe, j + 1)
                a.activation(mod8[:, j * 512:(j + 1) * 512], ps[j][0:NB, :], ACT.Copy).then_inc(setup_act, 1)
            act.wait_ge(setup_pe, 4)
            a.activation(mcol[:, :, :], ps[3][:, 0:4 * NB].rearrange("p (a n) -> p a n", a=4), ACT.Copy
                         ).then_inc(setup_act, 1)
            act.wait_ge(wload, 16 * len(mixer_loads))
            a.activation(aneg[:, :], r48_s[:, 1:2], ACT.Exp).then_inc(setup_act, 1)
            act.wait_ge(mod_stored, 16)
            act.wait_ge(setup_pool, SP_ALL)

            def ln_in(b):
                act.wait_ge(mc_ready, at(mc_ready, b, 1))
                for half in range(2):
                    for k in range(KD):
                        q = J_H + half * KD + k
                        act.wait_ge(*proj.full(b, q))
                        bank = proj.bank(q)
                        act_in = a.activation(hT[:, k, half * HALF:(half + 1) * HALF], bank[:, :], ACT.Identity,
                                              bias=mc[:, k:k + 1], scale=mc[:, 2 + k:3 + k])
                        act_in.then_inc(proj.drained[q % 4], 1)

            def x_copies(b):
                for half in range(2):
                    for m in range(KC):
                        q = J_X + half * KC + m
                        act.wait_ge(*proj.full(b, q))
                        bank = proj.bank(q)
                        o = TAPS - 1 + half * HALF
                        ins = a.activation(xcv[:, m, o:o + HALF], bank[:, :], ACT.Copy)
                        ins.then_inc(proj.drained[q % 4], 1)

            def x_silu(b, half, pair):
                for m in (2 * pair, 2 * pair + 1):
                    s = xT[:, m, half * HALF:(half + 1) * HALF]
                    act.wait_ge(conv_ready, at(conv_ready, b, half * KC + m + 1))
                    a.activation(s, s, ACT.Silu).then_inc(xT_ready, 1)

            def z_silu(b, half, pair):
                for m in (2 * pair, 2 * pair + 1):
                    q = J_Z + half * KC + m
                    act.wait_ge(*proj.full(b, q))
                    a.activation(zs[:, m, half * HALF:(half + 1) * HALF], proj.bank(q)[:, :], ACT.Silu
                                 ).then_inc(proj.drained[q % 4], 1)

            def softplus(b):
                act.wait_ge(u_ready, at(u_ready, b, 1))
                a.activation(a48, a48, ACT.Exp, scale=-1.0).then_inc(l_ready, 1)
                act.wait_ge(l_ready, at(l_ready, b, 1))
                a.activation(b48, a48, ACT.Ln, bias=1.0).then_inc(l_ready, 1)

            def bc_copies(b, half, ms):
                for m in ms:
                    q = J_BC[half][m]
                    act.wait_ge(*proj.full(b, q))
                    a.activation((BT if m < KC else CT)[:, half, m % KC, :], proj.bank(q)[:, :], ACT.Copy
                                 ).then_inc(proj.drained[q % 4], 1)

            def w_exp(b):
                act.wait_ge(dif_ready, at(dif_ready, b, 1))
                a.activation(a48, a48, ACT.Exp).then_inc(wexp_ready, 1)

            def right_rows(b):
                act.wait_ge(v_ready, at(v_ready, b, 1))
                for i in range(HEADS):
                    h = 2 * (i % 4) + i // 4
                    ins = a.activation(R8[:, i, :], Rw, ACT.Identity, bias=zero48[:, :], scale=delta[:, h:h + 1])
                ins.then_inc(rows_ready, 1)

            def ec(b, half):
                for k in range(KC):
                    q = J_EC + half * KC + k
                    act.wait_ge(*proj.full(b, q))
                    a.activation(ECv[:, k, half * HALF:(half + 1) * HALF], proj.bank(q)[:, :], ACT.Exp
                                 ).then_inc(proj.drained[q % 4], 1)

            def scan(b):
                for c in range(T):
                    for s in range(2):
                        act.wait_ge(cd_filled, at(cd_filled, b, 2 * c + s + 1))
                        if c or later(b):
                            act.wait_ge(Mt_ready, at(Mt_ready, b, 2 * (c - 1) + s + 1 if c else 0))
                        a.activation(Eg[:, s * HALF:(s + 1) * HALF], ps[s][:, :], ACT.Exp
                                     ).then_inc(Eg_ready, 1)

            def ffn_wrow(b):
                for j in range(2):
                    act.wait_ge(*ffn.full(b, F_WROW + j))
                    bank = ffn.bank(F_WROW + j)
                    ins = a.activation(wrow[:, j * HALF:(j + 1) * HALF], bank[:, :], ACT.Copy)
                    ins.then_inc(ffn.drained[(F_WROW + j) % 4], 1)

            def ffn_hnT(b):
                act.wait_ge(*ffn.full(b, F_HNT))
                bank = ffn.bank(F_HNT)
                ins = a.activation(hnT_, bank[:, 0:D], ACT.Copy)
                ins.then_inc(ffn.drained[F_HNT % 4], 1)
                for j in range(2):
                    act.wait_ge(*ffn.full(b, F_MT + j))
                    bank = ffn.bank(F_MT + j)
                    ins = a.activation(mT[:, 4 * j:4 * j + 4, :].rearrange("p t n -> p (t n)"), bank[:, :], ACT.Copy)
                    ins.then_inc(ffn.drained[(F_MT + j) % 4], 1)

            def ffn_v(b):
                act.wait_ge(*ffn.full(b, F_V))
                bank = ffn.bank(F_V)
                ins = a.activation(vs, bank[:, 0:D], ACT.Copy)
                ins.then_inc(ffn.drained[F_V % 4], 1)
                act.wait_ge(ang_ready, at(ang_ready, b, 1))
                a.activation(sc_[:, :, :], ang[:, :, :], ACT.Sin).then_inc(sin_ready, 1)

            def ffn_qT(b):
                for j, dst in ((F_QT, qT), (F_KT, kT)):
                    act.wait_ge(*ffn.full(b, j))
                    bank = ffn.bank(j)
                    ins = a.activation(dst.rearrange("p m n -> p (m n)"), bank[:, :], ACT.Copy)
                    ins.then_inc(ffn.drained[j % 4], 1)

            def ffn_softmax(b):
                act.wait_ge(mx_ready, at(mx_ready, b, 1))
                for h in range(FH):
                    a.activation(scr[:, h, 0:NSEL], scr[:, h, 0:NSEL], ACT.Exp, bias=mx[:, h:h + 1],
                                 accum_out=den[:, h:h + 1]).then_inc(prob_ready, 1)

            def ffn_AT(b):
                for j in range(4):
                    act.wait_ge(*ffn.full(b, F_AT + j))
                    bank = ffn.bank(F_AT + j)
                    ins = a.activation(AT[0:NSEL, 4 * j:4 * j + 4, :].rearrange("p t n -> p (t n)"),
                                       bank[0:NSEL, :], ACT.Copy)
                    ins.then_inc(ffn.drained[(F_AT + j) % 4], 1)

            def ffn_oT(b):
                act.wait_ge(*ffn.full(b, F_OT))
                bank = ffn.bank(F_OT)
                ins = a.activation(oT_, bank[:, 0:D], ACT.Copy)
                ins.then_inc(ffn.drained[F_OT % 4], 1)

            def ffn_hnbT(b):
                act.wait_ge(*ffn.full(b, F_HNBT))
                bank = ffn.bank(F_HNBT)
                ins = a.activation(hnT_, bank[:, 0:D], ACT.Copy)
                ins.then_inc(ffn.drained[F_HNBT % 4], 1)

            def ffn_gelu(b):
                for j in range(2):
                    act.wait_ge(*ffn.full(b, F_W1 + j))
                    bank = ffn.bank(F_W1 + j)
                    ins = a.activation(gT[:, 4 * j:4 * j + 4, :].rearrange("p t n -> p (t n)"), bank[:, :],
                                       ACT.Gelu_apprx_tanh)
                    ins.then_inc(ffn.drained[(F_W1 + j) % 4], 1)

            def batch(b, f):
                ln_in(b)
                x_copies(b)
                z_silu(b, 0, 0)
                z_silu(b, 0, 1)
                if f is not None:
                    ffn_wrow(f)
                z_silu(b, 1, 0)
                x_silu(b, 0, 0)
                z_silu(b, 1, 1)
                x_silu(b, 0, 1)
                bc_copies(b, 0, (0, 1, 2, 3, 4))
                x_silu(b, 1, 0)
                bc_copies(b, 0, (5, 6))
                x_silu(b, 1, 1)
                bc_copies(b, 0, (7,))
                softplus(b)
                if f is not None:
                    ffn_hnT(f)
                bc_copies(b, 1, (0,))
                w_exp(b)
                if f is not None:
                    ffn_v(f)
                bc_copies(b, 1, (1,))
                if f is not None:
                    ffn_qT(f)
                bc_copies(b, 1, (2,))
                right_rows(b)
                if f is not None:
                    ffn_softmax(f)
                bc_copies(b, 1, (3, 4))
                if f is not None:
                    ffn_AT(f)
                bc_copies(b, 1, (5,))
                if f is not None:
                    ffn_oT(f)
                bc_copies(b, 1, (6, 7))
                if f is not None:
                    ffn_hnbT(f)
                ec(b, 0)
                if f is not None:
                    ffn_gelu(f)
                ec(b, 1)
                scan(b)

            batch(0, None)
            with act.Fori(1, NB) as b:
                batch(b, b - 1)
            f = NB - 1
            ffn_wrow(f)
            ffn_hnT(f)
            ffn_v(f)
            ffn_qT(f)
            ffn_softmax(f)
            ffn_AT(f)
            ffn_oT(f)
            ffn_hnbT(f)
            ffn_gelu(f)

        @block.vector
        def _(dve):
            v = nc.vector
            n = [0]

            def link(ins):
                ins.then_inc(setup_dve, 1)
                n[0] += 1
                dve.wait_ge(setup_dve, n[0])

            dve.wait_ge(setup_act, 4)
            for i in (1, 4):
                s = mod8[:, i * D:(i + 1) * D]
                link(v.tensor_scalar(s, s, 1.0, None, ALU.add))
            for i in (2, 5):
                s = mod8[:, i * D:(i + 1) * D]
                link(v.tensor_scalar(sgn8, s, 0.0, 2.0, ALU.is_ge, ALU.mult))
                link(v.scalar_tensor_tensor(abs8, s, -1.0, s, ALU.mult, ALU.max))
                link(v.tensor_scalar(abs8, abs8, 0.25, None, ALU.max))
                link(v.scalar_tensor_tensor(s, sgn8, -1.0, abs8, ALU.add, ALU.mult))
            assert n[0] == SD_MOD, n[0]
            dve.wait_ge(setup_pool, SP_ALL)
            dve.wait_ge(setup_act, 6)
            link(v.tensor_scalar(aneg[:, :], aneg[:, :], -1.0, None, ALU.mult))
            link(v.tensor_scalar(delt3[:, :], delta[:, :], gmask[:, G3:G3 + 1], None, ALU.mult))
            for hh in range(2):
                link(v.tensor_copy(selp[:, :, 64 * hh:64 * hh + 64],
                                   delt3[:, hh::2].unsqueeze(2).broadcast_to([RW, 4, 64])))
            assert n[0] == SD_MIX
            dve.wait_ge(wload, 16 * len(mixer_loads))

            def fold_ln():
                dve.wait_ge(fload, 16 * len(ffn_loads))
                for k in range(KD):
                    link(v.tensor_scalar(wqkv_s[:, k, :], wqkv_s[:, k, :], ln_s[:, 0, k:k + 1], None, ALU.mult))
                    link(v.tensor_scalar(w1_s[:, k, :], w1_s[:, k, :], ln_s[:, 1, k:k + 1], None, ALU.mult))
                assert n[0] == SD_ALL

            def take_waits():
                v.tensor_copy(spare[:, 1:2], mhalf[:, 0:1])

            def ln_stats(b):
                dve.wait_ge(x_loaded, at(x_loaded, b, 16))
                if later(b):
                    dve.wait_ge(*proj.read(b - 1, J_H + 3))
                v.tensor_copy(mc[:, :], mcol[:, :, bass.ds(b, 1)].rearrange("p a n -> p (a n)")
                              ).then_inc(mc_ready, 1)
                for t in range(T):
                    ins = v.bn_stats(st6[:, t, :], xin[:, t, :])
                chA(dve, b, ins)
                take_waits()
                for t in range(T):
                    ins = v.bn_aggr(mv[:, t, :], st6[:, t, :])
                chA(dve, b, ins)
                v.tensor_scalar(rstd[:, :], mv[:, :, 1], EPS, None, ALU.add).then_inc(var_ready, 1)
                chA.end()

            def ln_apply(b):
                dve.wait_ge(rstd_ready, at(rstd_ready, b, 1))
                for t in range(T):
                    v.tensor_scalar(xin[:, t, :], xin[:, t, :], mv[:, t, 0:1], rstd[:, t:t + 1],
                                    ALU.subtract, ALU.mult).then_inc(xn_ready, 1)

            def conv(b, half, m2):
                pair = (2 * m2, 2 * m2 + 1)
                for tap in range(TAPS):
                    for m in pair:
                        dst = xT[:, m, half * HALF:(half + 1) * HALF]
                        src = xcv[:, m, half * HALF + tap:half * HALF + tap + HALF]
                        if tap == 0:
                            ins = v.tensor_scalar(dst, src, cols_s[:, m, 0:1], cols_s[:, m, 4:5],
                                                  ALU.mult, ALU.add)
                        else:
                            ins = v.scalar_tensor_tensor(dst, src, cols_s[:, m, tap:tap + 1], dst,
                                                         ALU.mult, ALU.add)
                        if tap == TAPS - 1:
                            ins.then_inc(conv_ready, 1)
                        elif m == pair[1]:
                            chV(dve, b, ins)

            def conv_first_half(b):
                if later(b):
                    dve.wait_ge(out_filled, at(out_filled, b - 1, 4))
                    dve.wait_ge(cd_filled, at(cd_filled, b - 1, 2 * T))
                dve.wait_ge(*proj.read(b, J_X + 7))
                chV(dve, b, v.memset(xcv[:, :, 0:TAPS - 1], 0.0))
                conv(b, 0, 0)
                conv(b, 0, 1)

            def softplus_in(b):
                for half in range(2):
                    q = J_DT + half
                    dve.wait_ge(*proj.full(b, q))
                    bank = proj.bank(q)
                    s = slice(half * HALF, (half + 1) * HALF)
                    ins = v.tensor_scalar(v48[:, s], bank[0:RW, :], r48_s[:, 0:1], None, ALU.add)
                    ins.then_inc(proj.drained[q % 4], 1)
                for half in range(2):
                    dve.wait_ge(*proj.read(b, J_DT + half))
                v.scalar_tensor_tensor(a48, v48, -1.0, v48, ALU.mult, ALU.max).then_inc(u_ready, 1)

            def decay_rows(b):
                dve.wait_ge(l_ready, at(l_ready, b, 2))
                chD(dve, b, v.scalar_tensor_tensor(dt48, v48, 0.0, b48, ALU.max, ALU.add))
                chD(dve, b, v.tensor_scalar(a48, dt48, aneg[:, :], None, ALU.mult))
                chD(dve, b, v.tensor_tensor_scan(v48, reset[:, :, :].rearrange("p t n -> p (t n)"), a48, 0.0,
                                                 ALU.mult, ALU.add))
                chD(dve, b, v.tensor_copy(hi, v48))
                chD(dve, b, v.tensor_tensor(a48, v48, hi, ALU.subtract))
                chD(dve, b, v.tensor_copy(mid, a48))
                chD(dve, b, v.tensor_tensor(lo, a48, mid, ALU.subtract))
                cv = v48.rearrange("p (t n) -> p t n", t=T)
                v.tensor_tensor(a48.rearrange("p (t n) -> p t n", t=T), cv[:, :, P - 1:P].broadcast_to([RW, T, P]),
                                cv, ALU.subtract).then_inc(dif_ready, 1)

            def decay_operands(b):
                chD(dve, b, v.tensor_scalar(Lw[:, :], hi, gmask[:, 0:1], gmask[:, 7:8], ALU.mult, ALU.add))
                chD(dve, b, v.scalar_tensor_tensor(Lw[:, :], mid, gmask[:, 1:2], Lw[:, :], ALU.mult, ALU.add))
                chD(dve, b, v.scalar_tensor_tensor(Lw[:, :], lo, gmask[:, 2:3], Lw[:, :], ALU.mult, ALU.add))
                chD(dve, b, v.tensor_scalar(Rw, hi, gmask[:, 3:4], gneg[:, :], ALU.mult, ALU.add))
                chD(dve, b, v.scalar_tensor_tensor(Rw, mid, gmask[:, 4:5], Rw, ALU.mult, ALU.add))
                chD(dve, b, v.scalar_tensor_tensor(Rw, lo, gmask[:, 5:6], Rw, ALU.mult, ALU.add))
                chD(dve, b, v.tensor_scalar(v48, dt48, gmask[:, 0:1], None, ALU.mult))
                dve.wait_ge(wexp_ready, at(wexp_ready, b, 1))
                v.scalar_tensor_tensor(a48, a48, gmask[:, 1:2], v48, ALU.mult, ALU.add).then_inc(v_ready, 1)
                chD.end()

            def dw_copy(b):
                dve.wait_ge(*proj.full(b, J_V))
                bank = proj.bank(J_V)
                ins = v.tensor_copy(dw[:, :, :],
                                    bank[:, 0:T * RW].rearrange("p (t n) -> p t n", t=T)[:, :, 0:2 * HEADS])
                ins.then_inc(proj.drained[J_V % 4], 1)

            def scan(b, last):
                def weigh(c):
                    dve.wait_ge(*proj.read(b, J_V))
                    if c == 0:
                        if later(b):
                            dve.wait_ge(so_ready, at(so_ready, b - 1, 1))
                    dve.wait_ge(xt_filled, at(xt_filled, b, c + 1))
                    if c >= 2:
                        dve.wait_ge(y_filled, at(y_filled, b, c - 1))
                    if c >= 2:
                        dve.wait_ge(s_filled, at(s_filled, b, c - 1))
                    v.tensor_tensor(XB[:, c % 2, 0, :].rearrange("p (h n) -> p h n", h=HEADS),
                                    ps[6][:, :].rearrange("p (h n) -> p h n", h=HEADS),
                                    dw[:, c, 0:HEADS].unsqueeze(2).broadcast_to([P, HEADS, STATE]), ALU.mult
                                    ).then_inc(Xd_ready, 1)
                    if c < T - 1:
                        dve.wait_ge(bt_filled, at(bt_filled, b, c + 1))
                        v.tensor_tensor(XB[:, c % 2, 1, :].rearrange("p (h n) -> p h n", h=HEADS),
                                        ps[7][:, :].rearrange("p (h n) -> p h n", h=HEADS),
                                        dw[:, c, HEADS:2 * HEADS].unsqueeze(2).broadcast_to([P, HEADS, STATE]),
                                        ALU.mult).then_inc(Bw_ready, 1)

                def masked(c):
                    for s in range(2):
                        dve.wait_ge(sc_filled, at(sc_filled, b, 2 * c + s + 1))
                        dve.wait_ge(Eg_ready, at(Eg_ready, b, 2 * c + s + 1))
                        v.tensor_tensor(Mt[:, c % 2, s * HALF:(s + 1) * HALF], ps[2 + s][:, :],
                                        Eg[:, s * HALF:(s + 1) * HALF], ALU.mult).then_inc(Mt_ready, 1)

                def state(c):
                    dve.wait_ge(s_filled, at(s_filled, b, c + 1))
                    if c:
                        if c or later(b):
                            dve.wait_ge(Sdc_ready, at(Sdc_ready, b, c))
                        dve.wait_ge(y_filled, at(y_filled, b, c + 1))
                    for hh in range(2):
                        q = slice(64 * hh, 64 * hh + 64)
                        src = ps[5][q, :].rearrange("p (k n) -> p k n", k=KC)[:, :, q]
                        if c:
                            ins = v.tensor_tensor(Sbd[q, :, q], src, Sdc[q, :, q], ALU.add)
                        else:
                            ins = v.tensor_copy(Sbd[q, :, q], src)
                    ins.then_inc(S_ready, 1)

                def skip(c):
                    dve.wait_ge(y_filled, at(y_filled, b, c + 1))
                    for k in range(KC):
                        s = xT[:, k, c * P:(c + 1) * P]
                        ins = v.scalar_tensor_tensor(s, s, cols_s[:, k, 5:6], ps[4][:, k * P:(k + 1) * P],
                                                     ALU.mult, ALU.add)
                    ins.then_inc(y_ready, 1)

                if later(b):
                    dve.wait_ge(so_ready, at(so_ready, b - 1, 1))
                v.memset(Sbd[0:64, 0, 64:128], 0.0)
                chS(dve, b, v.memset(Sbd[64:128, 0, 0:64], 0.0))
                weigh(0)
                masked(0)
                for c in range(T):
                    if c + 1 < T:
                        weigh(c + 1)
                    if c < T - 1:
                        state(c)
                    skip(c)
                    if c + 1 < T:
                        masked(c + 1)
                    if c % 4 == 3:
                        dve.wait_ge(y_ready, at(y_ready, b, c + 1))
                        for k in range(KC):
                            ins = v.bn_stats(yst[:, k, 6 * (c // 4):6 * (c // 4) + 6],
                                             xT[:, k, (c - 3) * P:(c + 1) * P])
                        chS(dve, b, ins)
                    if c == 5 and not last:
                        ln_stats(b + 1)
                    if c == 6 and not last:
                        ln_apply(b + 1)
                chS.end()

            def out_(b):
                take_waits()
                for k in range(KC):
                    ins = v.bn_aggr(ymv[:, k, :], yst[:, k, :])
                chG(dve, b, ins)
                v.tensor_copy(pk[:, 0, :], ymv[:, :, 0])
                chG(dve, b, v.tensor_tensor(pk[:, 1, :], ymv[:, :, 0], ymv[:, :, 0], ALU.mult))
                v.tensor_tensor(pk[:, 1, :], pk[:, 1, :], ymv[:, :, 1], ALU.add).then_inc(pk_ready, 1)
                dve.wait_ge(pk_filled, at(pk_filled, b, 1))
                chG(dve, b, v.tensor_copy(pk[:, 2:4, :], ps[4][:, 0:2 * KC].rearrange("p (a n) -> p a n", a=2)))
                chG(dve, b, v.tensor_tensor(gab[:, 0, :], pk[:, 2, :], pk[:, 2, :], ALU.mult))
                chG(dve, b, v.tensor_tensor(gab[:, 0, :], pk[:, 3, :], gab[:, 0, :], ALU.subtract))
                v.tensor_scalar(gab[:, 0, :], gab[:, 0, :], EPS, None, ALU.add).then_inc(gvar_ready, 1)
                dve.wait_ge(grstd_ready, at(grstd_ready, b, 1))
                chG(dve, b, v.tensor_tensor(gab[:, 2, :], gab[:, 1, :], cols_s[:, :, 6], ALU.mult))
                chG(dve, b, v.tensor_tensor(gab[:, 3, :], pk[:, 2, :], gab[:, 2, :], ALU.mult))
                chG(dve, b, v.tensor_tensor(gab[:, 3, :], cols_s[:, :, 7], gab[:, 3, :], ALU.subtract))
                for half in range(2):
                    for k in range(KC):
                        s = xT[:, k, half * HALF:(half + 1) * HALF]
                        v.tensor_scalar(s, s, gab[:, 2, k:k + 1], gab[:, 3, k:k + 1], ALU.mult, ALU.add
                                        ).then_inc(yn_ready, 1)
                    for k in (2, 3):
                        s = xT[:, k, half * HALF:(half + 1) * HALF]
                        dve.wait_ge(yn_ready, at(yn_ready, b, half * KC + k + 1))
                        v.tensor_tensor(s, s, zs[:, k, half * HALF:(half + 1) * HALF], ALU.mult
                                        ).then_inc(gd_ready, 1)
                dve.wait_ge(modrow_loaded, at(modrow_loaded, b, 16))
                chG(dve, b, v.tensor_tensor_reduce(out=junkd[:, 0, :], in0=modrow[:, 1, :], in1=rw_s[:, :], scale=1.0,
                                                   scalar=0.0, op0=ALU.mult, op1=ALU.add, accum_out=c0[:, :]))
                v.tensor_scalar(c0[:, :], c0[:, :], rb_s[:, :], None, ALU.add).then_inc(c0_ready, 1)
                dve.wait_ge(xr_loaded, at(xr_loaded, b, 16))
                dve.wait_ge(rows2_ready, at(rows2_ready, b, 1))
                for step in range(6):
                    if step < 4:
                        residual(b, step)
                    if 1 <= step < 5:
                        second_norm(b, step - 1)
                    if step >= 2:
                        router(b, step - 2)
                dve.wait_ge(w_ready, at(w_ready, b, T))
                dve.wait_ge(c0_ready, at(c0_ready, b, 1))
                v.tensor_scalar(wcol[:, :], wcol[:, :], c0[:, :], None, ALU.add).then_inc(wcol_ready, 1)
                chG.end()

            def residual(b, j):
                q = slice(2 * j, 2 * j + 2)
                dve.wait_ge(out_filled, at(out_filled, b, j + 1))
                v.tensor_tensor(xr[:, q, :], xr[:, q, :], ps[4 + j][:, :].rearrange("p (t n) -> p t n", t=2),
                                ALU.add).then_inc(x1_ready, 1)
                dve.wait_ge(x1_ready, at(x1_ready, b, j + 1))
                for t in (2 * j, 2 * j + 1):
                    ins = v.bn_stats(st6b[:, t, :], xr[:, t, :])
                chG(dve, b, ins)
                take_waits()
                for t in (2 * j, 2 * j + 1):
                    ins = v.bn_aggr(mvb[:, t, :], st6b[:, t, :])
                chG(dve, b, ins)
                v.tensor_scalar(rstdb[:, q], mvb[:, q, 1], EPS, None, ALU.add).then_inc(var2_ready, 1)

            def second_norm(b, j):
                dve.wait_ge(rstd2_ready, at(rstd2_ready, b, j + 1))
                for t in (2 * j, 2 * j + 1):
                    v.tensor_scalar(h2[:, t, :], xr[:, t, :], mvb[:, t, 0:1], rstdb[:, t:t + 1],
                                    ALU.subtract, ALU.mult).then_inc(hn2_ready, 1)

            def router(b, j):
                dve.wait_ge(hn2_ready, at(hn2_ready, b, 2 * j + 2))
                if j:
                    dve.wait_ge(w_ready, at(w_ready, b, 2 * j))
                for t in (2 * j, 2 * j + 1):
                    v.tensor_tensor_reduce(out=junkd[:, t % 2, :], in0=h2[:, t, :], in1=rwc, scale=1.0,
                                           scalar=0.0, op0=ALU.mult, op1=ALU.add,
                                           accum_out=wcol[:, t:t + 1]).then_inc(w_ready, 1)

            def ffn_rank(b):
                dve.wait_ge(*ffn.read(b, F_WROW + 1))
                for t in range(T):
                    ins = v.scalar_tensor_tensor(Pm[:, t, :], wrow[:, t * P:(t + 1) * P], wcol[:, t:t + 1],
                                                 tri[:, :], ALU.is_equal, ALU.mult)
                chR(dve, b, ins)
                for t in (4, 5, 6, 7, 0, 1, 2, 3):
                    if t == 0:
                        dve.wait_ge(base_stored, at(base_stored, b, 64))
                    lo_, hi_ = t * P, (t + 1) * P
                    wj = wcol[:, t:t + 1]
                    if t:
                        v.tensor_scalar(Gt[:, t, 0:lo_], wrow[:, 0:lo_], wj, None, ALU.is_lt)
                    if t < T - 1:
                        v.tensor_scalar(Gt[:, t, hi_:L], wrow[:, hi_:L], wj, None, ALU.is_le)
                    v.scalar_tensor_tensor(Gt[:, t, lo_:hi_], wrow[:, lo_:hi_], wj, Pm[:, t, :],
                                           ALU.is_lt, ALU.add).then_inc(G_ready, 1)

            def ffn_onehot(b):
                dve.wait_ge(*ffn.full(b, F_RANK))
                bank = ffn.bank(F_RANK)
                ins = v.tensor_copy(rank[:, :], bank[:, 0:T])
                ins.then_inc(ffn.drained[F_RANK % 4], 1)
                dve.wait_ge(*ffn.read(b, F_RANK))
                for t in range(T):
                    v.tensor_scalar(Pm[:, t, :], iota_r[:, :], rank[:, t:t + 1], None, ALU.is_equal
                                    ).then_inc(P_ready, 1)

            def ffn_pick(b):
                v.tensor_scalar(moff[:, :], boff[:, :], float((MB - 1) * L), None, ALU.min)
                dve.wait_ge(*ffn.full(b, F_IDX))
                bank = ffn.bank(F_IDX)
                ins = v.tensor_copy(self_[:, 0:1], bank[:, 0:1])
                ins.then_inc(ffn.drained[F_IDX % 4], 1)
                dve.wait_ge(*ffn.read(b, F_IDX))
                v.tensor_copy(xidx[:, :], self_[:, 0:1])
                v.tensor_scalar(gidx[:, :], self_[:, 0:1], boff[:, :], None, ALU.add)
                v.tensor_scalar(midx[:, :], self_[:, 0:1], moff[:, :], None, ALU.add).then_inc(gidx_ready, 1)
                dve.wait_ge(gidx_ready, at(gidx_ready, b, 1))
                chR(dve, b, v.tensor_scalar(boff[:, :], boff[:, :], float(L), None, ALU.add))

            def ffn_norm(b):
                dve.wait_ge(xs_loaded, at(xs_loaded, b, 16))
                chR(dve, b, v.bn_stats(st1[:, :], xs))
                take_waits()
                chR(dve, b, v.bn_aggr(sm[:, 8:10], st1[:, :]))
                v.tensor_scalar(sm[:, 0:1], sm[:, 9:10], EPS, None, ALU.add).then_inc(fv_ready, 1)
                dve.wait_ge(m_loaded, at(m_loaded, b, 16))
                v.tensor_scalar(mrows, mrows, -3e38, None, ALU.max).then_inc(mclamp_ready, 1)
                dve.wait_ge(fr_ready, at(fr_ready, b, 1))
                chR(dve, b, v.tensor_scalar(hs, xs, sm[:, 8:9], sm[:, 1:2], ALU.subtract, ALU.mult))
                chR(dve, b, v.tensor_tensor(hs, hs, modrow[:, 2, :], ALU.mult))
                chR(dve, b, v.tensor_tensor(hs, hs, modrow[:, 1, :], ALU.add))
                chR(dve, b, v.tensor_tensor_reduce(out=junk, in0=hs, in1=hs, scale=1.0, scalar=0.0, op0=ALU.mult,
                                                   op1=ALU.add, accum_out=sm[:, 10:11]))
                v.tensor_scalar(sm[:, 2:3], sm[:, 10:11], 1.0 / D, 1e-6, ALU.mult, ALU.add).then_inc(fs_ready, 1)
                chR(dve, b, v.tensor_tensor_reduce(out=junk, in0=hs, in1=rw_s[:, :], scale=1.0, scalar=0.0,
                                                   op0=ALU.mult, op1=ALU.add, accum_out=sm[:, 11:12]))
                chR(dve, b, v.tensor_scalar(sm[:, 11:12], sm[:, 11:12], rb_s[:, :], None, ALU.add))
                dve.wait_ge(frr_ready, at(frr_ready, b, 1))
                v.tensor_scalar(hn, hs, sm[:, 3:4], None, ALU.mult).then_inc(hn_ready, 1)
                chR(dve, b, v.tensor_scalar(junkt, wrow[:, :], sm[:, 11:12], None, ALU.is_ge, ALU.add,
                                            accum_out=sm[:, 12:13]))
                chR(dve, b, v.tensor_scalar(sm[:, 13:14], sm[:, 12:13], KSEL - 0.5, None, ALU.is_ge))
                dve.wait_ge(pos_loaded, at(pos_loaded, b, 16))
                chR(dve, b, v.tensor_copy(posf[:, :], posi[:, :]))
                chR(dve, b, v.tensor_scalar(ang[:, :, :], invf[:, :, :], posf[:, :], None, ALU.mult))
                chR(dve, b, v.scalar_tensor_tensor(trn[:, :, :], ang[:, :, :], 1.0 / (2 * PI), phase[:, 0, :, :],
                                                   ALU.mult, ALU.add))
                chR(dve, b, v.tensor_scalar(trn[:, :, :], trn[:, :, :], ROUND, None, ALU.add))
                chR(dve, b, v.tensor_scalar(trn[:, :, :], trn[:, :, :], -ROUND, None, ALU.add))
                for part in TWO_PI:
                    chR(dve, b, v.scalar_tensor_tensor(ang[:, :, :], trn[:, :, :], -part, ang[:, :, :],
                                                       ALU.mult, ALU.add))
                chR(dve, b, v.tensor_tensor(ang[:, :, :], ang[:, :, :], phase[:, 1, :, :], ALU.add))
                v.tensor_scalar(ang[:, :, :], ang[:, :, :], -3.1415925, 3.1415925, ALU.max, ALU.min
                                ).then_inc(ang_ready, 1)

            def ffn_rope(b):
                dve.wait_ge(*ffn.full(b, F_MSEL))
                bank = ffn.bank(F_MSEL)
                ins = v.tensor_copy(msel, bank[:, 0:P])
                ins.then_inc(ffn.drained[F_MSEL % 4], 1)
                dve.wait_ge(*ffn.read(b, F_MSEL))
                dve.wait_ge(*ffn.full(b, F_QK))
                bank = ffn.bank(F_QK)
                ins = v.tensor_copy(qk, bank[:, :])
                ins.then_inc(ffn.drained[F_QK % 4], 1)
                dve.wait_ge(*ffn.read(b, F_QK))
                dve.wait_ge(sin_ready, at(sin_ready, b, 1))
                dve.wait_ge(qkz_ready, at(qkz_ready, b, 1))
                q4 = qk.rearrange("p (h a n) -> p h a n", a=2, n=HD // 2)
                r4 = rt.rearrange("p (h a n) -> p h a n", a=2, n=HD // 2)
                sinb = sc_[:, 0:1, :].broadcast_to([P, 2 * FH, HD // 2])
                cosb = sc_[:, 1:2, :].broadcast_to([P, 2 * FH, HD // 2])
                v.scalar_tensor_tensor(r4[:, :, 0, :], q4[:, :, 1, :], -1.0, sinb, ALU.mult, ALU.mult)
                chR(dve, b, v.tensor_tensor(r4[:, :, 1, :], q4[:, :, 0, :], sinb, ALU.mult))
                v.tensor_tensor(q4[:, :, 0, :], q4[:, :, 0, :], cosb, ALU.mult)
                chR(dve, b, v.tensor_tensor(q4[:, :, 1, :], q4[:, :, 1, :], cosb, ALU.mult))
                v.tensor_tensor(qkr[:, :, :, 0:HD].rearrange("p s h n -> p (s h) n"),
                                qk.rearrange("p (h n) -> p h n", n=HD),
                                rt.rearrange("p (h n) -> p h n", n=HD), ALU.add).then_inc(rope_ready, 1)

            def ffn_scores(b):
                for r in range(4):
                    q = F_SC + r
                    dve.wait_ge(*ffn.full(b, q))
                    bank = ffn.bank(q)
                    ins = v.scalar_tensor_tensor(scr[:, 4 * r:4 * r + 4, 0:NSEL],
                                                 bank[:, :].rearrange("p (m n) -> p m n", m=4)[:, :, 0:NSEL],
                                                 float(HD) ** -0.5,
                                                 msel[:, 0:NSEL].unsqueeze(1).broadcast_to([P, 4, NSEL]),
                                                 ALU.mult, ALU.add)
                    ins.then_inc(ffn.drained[q % 4], 1)
                dve.wait_ge(*ffn.read(b, F_SC + 3))
                chR(dve, b, v.tensor_reduce(mx[:, :], scr[:, :, 0:NSEL], AX.X, ALU.max))
                v.tensor_scalar(mx[:, :], mx[:, :], -1.0, None, ALU.mult).then_inc(mx_ready, 1)

            def ffn_o(b):
                dve.wait_ge(prob_ready, at(prob_ready, b, FH))
                chR(dve, b, v.reciprocal(den[:, :], den[:, :]))
                q = F_AV
                dve.wait_ge(*ffn.full(b, q))
                bank = ffn.bank(q)
                ins = v.tensor_tensor(ob.rearrange("p (m r n) -> p r m n", m=4, r=4),
                                      bank[:, 0:D].rearrange("p (m r n) -> p r m n", m=4, r=4),
                                      den[:, :].rearrange("p (r m) -> p r m", r=4).unsqueeze(3)
                                      .broadcast_to([P, 4, 4, HD]), ALU.mult)
                ins.then_inc(ffn.drained[q % 4], 1)

            def ffn_x1(b):
                q = F_WO
                dve.wait_ge(*ffn.full(b, q))
                bank = ffn.bank(q)
                ins = v.tensor_tensor(x1s, hs, bank[:, 0:D], ALU.add)
                ins.then_inc(ffn.drained[q % 4], 1)
                dve.wait_ge(*ffn.read(b, q))
                chR(dve, b, v.tensor_tensor_reduce(out=junk, in0=x1s, in1=x1s, scale=1.0, scalar=0.0, op0=ALU.mult,
                                                   op1=ALU.add, accum_out=sm[:, 10:11]))
                v.tensor_scalar(sm[:, 4:5], sm[:, 10:11], 1.0 / D, 1e-6, ALU.mult, ALU.add).then_inc(fs2_ready, 1)
                dve.wait_ge(frr2_ready, at(frr2_ready, b, 1))
                v.tensor_scalar(hn, x1s, sm[:, 5:6], None, ALU.mult).then_inc(hnb_ready, 1)

            def ffn_end(b):
                q = F_W2
                dve.wait_ge(*ffn.full(b, q))
                bank = ffn.bank(q)
                ins = v.tensor_tensor(x1s, x1s, bank[:, 0:D], ALU.add)
                ins.then_inc(ffn.drained[q % 4], 1)
                dve.wait_ge(*ffn.read(b, q))
                chR(dve, b, v.tensor_scalar(x1s, x1s, sm[:, 11:12], None, ALU.mult))
                chR(dve, b, v.scalar_tensor_tensor(x1s, hs, sm[:, 13:14], x1s, ALU.mult, ALU.add))
                chR(dve, b, v.tensor_tensor(x1s, x1s, modrow[:, 3, :], ALU.mult))
                v.tensor_tensor(x1s, x1s, xs, ALU.add).then_inc(so_ready, 1)
                chR.end()

            def batch(b, f, last=False):
                if f is not None:
                    out_(f)
                conv_first_half(b)
                if f is not None:
                    ffn_rank(f)
                conv(b, 1, 0)
                if f is not None:
                    ffn_onehot(f)
                conv(b, 1, 1)
                chV.end()
                if f is not None:
                    ffn_pick(f)
                    ffn_norm(f)
                softplus_in(b)
                decay_rows(b)
                if f is not None:
                    ffn_rope(f)
                decay_operands(b)
                if f is not None:
                    ffn_scores(f)
                    ffn_o(f)
                dw_copy(b)
                if f is not None:
                    ffn_x1(f)
                    ffn_end(f)
                scan(b, last)

            ln_stats(0)
            ln_apply(0)
            batch(0, None)
            fold_ln()
            with dve.Fori(1, NB - 1) as b:
                batch(b, b - 1)
            batch(NB - 1, NB - 2, last=True)
            f = NB - 1
            out_(f)
            ffn_rank(f)
            ffn_onehot(f)
            ffn_pick(f)
            ffn_norm(f)
            ffn_rope(f)
            ffn_scores(f)
            ffn_o(f)
            ffn_x1(f)
            ffn_end(f)

        @block.tensor
        def _(pe):
            t_ = nc.tensor
            pe.wait_ge(mload, 32)
            pe.wait_ge(setup_act, 1)
            for j in range(3):
                for k in range(KD):
                    ins = t_.matmul(ps[j][0:NB, :], mcin[:, k, :], wmod_s[:, k, j * 512:(j + 1) * 512],
                                    start=k == 0, stop=k == KD - 1)
                ins.then_inc(setup_pe, 1)
            pe.wait_ge(setup_dve, SD_MOD)
            pe.wait_ge(setup_pool, SP_ALL)
            for j in range(4):
                ins = t_.transpose(ps[3][:, j * NB:(j + 1) * NB], mod8[:, j * P:(j + 1) * P], ident[0:NB, 0:NB])
            ins.then_inc(setup_pe, 1)
            pe.wait_ge(wload, 16 * len(mixer_loads))
            pe.wait_ge(setup_dve, SD_MIX)
            pe.wait_ge(setup_act, 5)

            def ln_in(b):
                for half in range(2):
                    for k in range(KD):
                        q = J_H + half * KD + k
                        if later(b):
                            pe.wait_ge(Mt_ready, at(Mt_ready, b - 1, 2 * T))
                        if q >= 4:
                            pe.wait_ge(*proj.read(b, q - 4))
                        bank = proj.bank(q)
                        pe.wait_ge(xn_ready, at(xn_ready, b, 4 * half + 4))
                        for i in range(4):
                            ins = t_.transpose(bank[:, i * P:(i + 1) * P],
                                               xin[:, 4 * half + i, k * P:(k + 1) * P], ident[:, :])
                        ins.then_inc(proj.filled[q % 4], 1)

            def project(b, q, w, m, rhs, nk, half):
                if q >= 4:
                    pe.wait_ge(*proj.read(b, q - 4))
                bank = proj.bank(q)
                for k in range(nk):
                    ins = t_.matmul(bank[:, :], w[:, k, m * P:(m + 1) * P],
                                    rhs[:, k, half * HALF:(half + 1) * HALF], start=k == 0, stop=k == nk - 1)
                ins.then_inc(proj.filled[q % 4], 1)

            def x_proj(b, half, ms):
                pe.wait_ge(*proj.read(b, J_H + (2 * half + 2) - 1))
                for m in ms:
                    project(b, J_X + half * KC + m, wx_s, m, hT, KD, half)

            def z_proj(b, half):
                for m in range(KC):
                    project(b, J_Z + half * KC + m, wz_s, m, hT, KD, half)

            def dt_proj(b):
                pe.wait_ge(xT_ready, at(xT_ready, b, 8))
                for half in range(2):
                    q = J_DT + half
                    if q >= 4:
                        pe.wait_ge(*proj.read(b, q - 4))
                    bank = proj.bank(q)
                    for k in range(KC):
                        ins = t_.matmul(bank[0:RW, :], wdt_s[:, k, :], xT[:, k, half * HALF:(half + 1) * HALF],
                                        start=k == 0, stop=k == KC - 1)
                    ins.then_inc(proj.filled[q % 4], 1)

            def bc_proj(b, half, ms):
                pe.wait_ge(xT_ready, at(xT_ready, b, 4 * half + 4))
                for m in ms:
                    project(b, J_BC[half][m], wb_s if m < KC else wc_s, m % KC, xT, KC, half)

            def decay_jobs(b):
                q = J_V
                if q >= 4:
                    pe.wait_ge(*proj.read(b, q - 4))
                bank = proj.bank(q)
                pe.wait_ge(v_ready, at(v_ready, b, 1))
                t_.matmul(bank[:, 0:1], identb[:, :], ones_b[:, :], start=True, stop=True)
                for t in range(T):
                    ins = t_.transpose(bank[:, t * RW:(t + 1) * RW], a48[:, t * P:(t + 1) * P], ident[0:RW, 0:RW])
                ins.then_inc(proj.filled[q % 4], 1)

            def carry_rows(b, half):
                pe.wait_ge(rows_ready, at(rows_ready, b, 1))
                for k in range(KC):
                    q = J_EC + half * KC + k
                    pe.wait_ge(*proj.read(b, q - 4))
                    t_.matmul(proj.bank(q)[:, :], selp[:, k, :], Lw[:, half * HALF:(half + 1) * HALF],
                              start=True, stop=True).then_inc(proj.filled[q % 4], 1)

            def scan(b):
                def turn(c):
                    if c or later(b):
                        pe.wait_ge(Xd_ready, at(Xd_ready, b, c))
                    for k in range(KC):
                        ins = t_.transpose(ps[6][:, k * P:(k + 1) * P], xT[:, k, c * P:(c + 1) * P], ident[:, :])
                    ins.then_inc(xt_filled, 1)
                    if c < T - 1:
                        if c or later(b):
                            pe.wait_ge(Bw_ready, at(Bw_ready, b, c))
                        for k in range(KC):
                            ins = t_.transpose(ps[7][:, k * P:(k + 1) * P], BT[:, c // 4, k, chunk(c)],
                                               ident[:, :])
                        ins.then_inc(bt_filled, 1)

                def cumdiff(c):
                    for s in range(2):
                        if c or later(b):
                            pe.wait_ge(Eg_ready, at(Eg_ready, b, 2 * (c - 1) + s + 1 if c else 0))
                        t_.matmul(ps[s][:, :], identb[:, :], causal[:, :, :].rearrange("p a n -> p (a n)"),
                                  start=True, stop=False)
                        t_.matmul(ps[s][:, :], Lw[:, c * P:(c + 1) * P], R8[:, 4 * s:4 * s + 4, c * P:(c + 1) * P],
                                  start=False, stop=True).then_inc(cd_filled, 1)

                def scores(c):
                    for s in range(2):
                        if c or later(b):
                            pe.wait_ge(Mt_ready, at(Mt_ready, b, 2 * (c - 1) + s + 1 if c else 0))
                        r = slice(64 * s, 64 * s + 64)
                        for k in range(KC):
                            ins = t_.matmul(ps[2 + s][:, k * P:(k + 1) * P], BT[r, c // 4, k, chunk(c)],
                                            CT[r, c // 4, k, chunk(c)], start=True, stop=True)
                        ins.then_inc(sc_filled, 1)

                def state(c):
                    pe.wait_ge(Bw_ready, at(Bw_ready, b, c + 1))
                    pe.wait_ge(Xd_ready, at(Xd_ready, b, c + 1))
                    if c or later(b):
                        pe.wait_ge(S_ready, at(S_ready, b, c))
                    for k in range(KC):
                        ins = t_.matmul(ps[5][:, k * P:(k + 1) * P], XB[:, c % 2, 1, k * P:(k + 1) * P],
                                        XB[:, c % 2, 0, k * P:(k + 1) * P], start=True, stop=True)
                    ins.then_inc(s_filled, 1)

                def output(c):
                    if c or later(b):
                        pe.wait_ge(y_ready, at(y_ready, b, c))
                    pe.wait_ge(Mt_ready, at(Mt_ready, b, 2 * c + 2))
                    if c:
                        if c or later(b):
                            pe.wait_ge(S_ready, at(S_ready, b, c))
                        pe.wait_ge(CE_ready, at(CE_ready, b, 4 * (c // 4) + 4))
                    for k in range(KC):
                        o = slice(k * P, (k + 1) * P)
                        for hh in range(2):
                            r = slice(64 * hh, 64 * hh + 64)
                            h = 2 * k + hh
                            ins = t_.matmul(ps[4][r, o], XB[:, c % 2, 0, h * 64:(h + 1) * 64],
                                            Mt[:, c % 2, hh * HALF + k * P:hh * HALF + (k + 1) * P],
                                            start=True, stop=True)
                        if c:
                            ins = t_.matmul(ps[4][:, o], Sbd[:, k, :], ECv[:, k, c * P:(c + 1) * P],
                                            start=False, stop=True, skip_group_check=True)
                    ins.then_inc(y_filled, 1)

                for i in range(4):
                    pe.wait_ge(proj.drained[i], at(proj.drained[i], b + 1, 0))
                if later(b):
                    for i in range(4):
                        pe.wait_ge(ffn.drained[i], at(ffn.drained[i], b - 1 + 1, 0))
                pe.wait_ge(*proj.read(b, J_BC[1][7]))
                turn(0)
                cumdiff(0)
                scores(0)
                for c in range(T):
                    if c + 1 < T:
                        turn(c + 1)
                        cumdiff(c + 1)
                    if c < T - 1:
                        state(c)
                    output(c)
                    if c + 1 < T:
                        scores(c + 1)

            def gn_stats(b):
                pe.wait_ge(pk_ready, at(pk_ready, b, 1))
                t_.matmul(ps[4][:, 0:2 * KC], halfmean[:, :], pk[:, 0:2, :].rearrange("p a n -> p (a n)"),
                          start=True, stop=True).then_inc(pk_filled, 1)

            def out_(b):
                pe.wait_ge(wog_ready, at(wog_ready, b, 1))
                for j in range(4):
                    pe.wait_ge(g_ready, at(g_ready, b, 2 * (j // 2) + 2))
                    pe.wait_ge(gd_ready, at(gd_ready, b, 2 * (j // 2) + 2))
                    for i in range(2):
                        t = 2 * j + i
                        for k in range(KC):
                            ins = t_.matmul(ps[4 + j][:, i * D:(i + 1) * D], xT[:, k, t * P:(t + 1) * P],
                                            wog_s[:, k, :], start=k == 0, stop=k == KC - 1)
                    ins.then_inc(out_filled, 1)

            def ffn_wrow(b):
                pe.wait_ge(wcol_ready, at(wcol_ready, b, 1))
                for j in range(2):
                    if F_WROW + j >= 4:
                        pe.wait_ge(*ffn.read(b, F_WROW + j - 4))
                    bank = ffn.bank(F_WROW + j)
                    for i in range(4):
                        ins = t_.transpose(bank[:, i * P:(i + 1) * P],
                                           wcol[:, 4 * j + i:4 * j + i + 1].broadcast_to([P, P]), ident[:, :])
                    ins.then_inc(ffn.filled[(F_WROW + j) % 4], 1)

            def ffn_rank(b):
                if F_RANK >= 4:
                    pe.wait_ge(*ffn.read(b, F_RANK - 4))
                bank = ffn.bank(F_RANK)
                pe.wait_ge(G_ready, at(G_ready, b, T))
                for s in range(T):
                    for t in range(T):
                        ins = t_.matmul(bank[:, s:s + 1], Gt[:, t, s * P:(s + 1) * P], ones_b[:, :],
                                        start=t == 0, stop=t == T - 1)
                ins.then_inc(ffn.filled[F_RANK % 4], 1)

            def ffn_idx(b):
                if F_IDX >= 4:
                    pe.wait_ge(*ffn.read(b, F_IDX - 4))
                bank = ffn.bank(F_IDX)
                pe.wait_ge(P_ready, at(P_ready, b, T))
                for t in range(T):
                    ins = t_.matmul(bank[:, 0:1], Pm[:, t, :], tok[:, t:t + 1], start=t == 0, stop=t == T - 1)
                ins.then_inc(ffn.filled[F_IDX % 4], 1)

            def ffn_turn(b, q, src):
                if q >= 4:
                    pe.wait_ge(*ffn.read(b, q - 4))
                bank = ffn.bank(q)
                for k in range(KD):
                    ins = t_.transpose(bank[:, k * P:(k + 1) * P], src[:, k * P:(k + 1) * P], ident[:, :])
                ins.then_inc(ffn.filled[q % 4], 1)

            def ffn_mask(b):
                pe.wait_ge(mclamp_ready, at(mclamp_ready, b, 1))
                for j in range(2):
                    if F_MT + j >= 4:
                        pe.wait_ge(*ffn.read(b, F_MT + j - 4))
                    bank = ffn.bank(F_MT + j)
                    for i in range(4):
                        t = 4 * j + i
                        ins = t_.transpose(bank[:, i * P:(i + 1) * P], mrows[:, t * P:(t + 1) * P], ident[:, :])
                    ins.then_inc(ffn.filled[(F_MT + j) % 4], 1)

            def ffn_msel(b):
                if F_MSEL >= 4:
                    pe.wait_ge(*ffn.read(b, F_MSEL - 4))
                bank = ffn.bank(F_MSEL)
                pe.wait_ge(*ffn.read(b, F_MT + 1))
                for t in range(T):
                    ins = t_.matmul(bank[:, 0:P], mT[:, t, :], Pm[:, t, :], start=t == 0, stop=t == T - 1)
                ins.then_inc(ffn.filled[F_MSEL % 4], 1)

            def ffn_qkv(b):
                pe.wait_ge(*ffn.read(b, F_HNT))
                for q, o, w in ((F_QK, 0, 2 * D), (F_V, 2 * D, D)):
                    if q >= 4:
                        pe.wait_ge(*ffn.read(b, q - 4))
                    bank = ffn.bank(q)
                    for k in range(KD):
                        ins = t_.matmul(bank[:, 0:w], hnT[:, k, :], wqkv_s[:, k, o:o + w],
                                        start=k == 0, stop=k == KD - 1)
                    ins.then_inc(ffn.filled[q % 4], 1)

            def ffn_qT(b):
                pe.wait_ge(rope_ready, at(rope_ready, b, 1))
                for s in range(2):
                    if F_QT + s >= 4:
                        pe.wait_ge(*ffn.read(b, F_QT + s - 4))
                    bank = ffn.bank(F_QT + s)
                    for m in range(4):
                        ins = t_.transpose(bank[:, m * P:(m + 1) * P],
                                           qkr[:, s, 4 * m:4 * m + 4, :].rearrange("p h n -> p (h n)"), ident[:, :])
                    ins.then_inc(ffn.filled[(F_QT + s) % 4], 1)

            def ffn_scores(b):
                pe.wait_ge(*ffn.read(b, F_KT))
                for r in range(4):
                    if F_SC + r >= 4:
                        pe.wait_ge(*ffn.read(b, F_SC + r - 4))
                    bank = ffn.bank(F_SC + r)
                    s = slice(32 * r, 32 * r + 32)
                    for m in range(4):
                        ins = t_.matmul(bank[:, m * P:m * P + NSEL], qT[s, m, :], kT[s, m, 0:NSEL],
                                        start=True, stop=True)
                    ins.then_inc(ffn.filled[(F_SC + r) % 4], 1)

            def ffn_AT(b):
                for r in range(4):
                    if F_AT + r >= 4:
                        pe.wait_ge(*ffn.read(b, F_AT + r - 4))
                    bank = ffn.bank(F_AT + r)
                    pe.wait_ge(prob_ready, at(prob_ready, b, 4 * r + 4))
                    for m in range(4):
                        ins = t_.transpose(bank[0:NSEL, m * P:(m + 1) * P], scr[:, 4 * r + m, 0:NSEL], ident[:, :])
                    ins.then_inc(ffn.filled[(F_AT + r) % 4], 1)

            def ffn_av(b):
                if F_AV >= 4:
                    pe.wait_ge(*ffn.read(b, F_AV - 4))
                bank = ffn.bank(F_AV)
                pe.wait_ge(*ffn.read(b, F_AT + 3))
                pe.wait_ge(*ffn.read(b, F_V))
                for r in range(4):
                    for m in range(4):
                        o = (4 * m + r) * HD
                        ins = t_.matmul(bank[:, o:o + HD], AT[0:NSEL, 4 * r + m, :], vs[0:NSEL, o:o + HD],
                                        start=True, stop=True)
                ins.then_inc(ffn.filled[F_AV % 4], 1)

            def ffn_wo(b):
                if F_WO >= 4:
                    pe.wait_ge(*ffn.read(b, F_WO - 4))
                bank = ffn.bank(F_WO)
                pe.wait_ge(*ffn.read(b, F_OT))
                for k in range(KD):
                    ins = t_.matmul(bank[:, 0:D], oT[:, k, :], fwo_s[:, k, :], start=k == 0, stop=k == KD - 1)
                ins.then_inc(ffn.filled[F_WO % 4], 1)

            def ffn_w1(b):
                pe.wait_ge(*ffn.read(b, F_HNBT))
                for j in range(2):
                    if F_W1 + j >= 4:
                        pe.wait_ge(*ffn.read(b, F_W1 + j - 4))
                    bank = ffn.bank(F_W1 + j)
                    for i in range(4):
                        f = 4 * j + i
                        for k in range(KD):
                            ins = t_.matmul(bank[:, i * P:(i + 1) * P], w1_s[:, k, f * P:(f + 1) * P], hnT[:, k, :],
                                            start=k == 0, stop=k == KD - 1)
                    ins.then_inc(ffn.filled[(F_W1 + j) % 4], 1)

            def ffn_w2(b):
                if F_W2 >= 4:
                    pe.wait_ge(*ffn.read(b, F_W2 - 4))
                bank = ffn.bank(F_W2)
                pe.wait_ge(*ffn.read(b, F_W1 + 1))
                for f in range(FT):
                    ins = t_.matmul(bank[:, 0:D], gT[:, f, :], w2_s[:, f, :], start=f == 0, stop=f == FT - 1)
                ins.then_inc(ffn.filled[F_W2 % 4], 1)

            def batch(b, f):
                ln_in(b)
                x_proj(b, 0, range(3))
                if f is not None:
                    gn_stats(f)
                x_proj(b, 0, (3,))
                x_proj(b, 1, range(4))
                if f is not None:
                    out_(f)
                z_proj(b, 0)
                if f is not None:
                    ffn_wrow(f)
                z_proj(b, 1)
                bc_proj(b, 0, (0, 1, 2))
                if f is not None:
                    ffn_rank(f)
                bc_proj(b, 0, (3, 4))
                if f is not None:
                    ffn_idx(f)
                bc_proj(b, 0, (5, 6, 7))
                dt_proj(b)
                if f is not None:
                    pe.wait_ge(hn_ready, at(hn_ready, f, 1))
                    ffn_turn(f, F_HNT, hn)
                    ffn_mask(f)
                bc_proj(b, 1, (0,))
                if f is not None:
                    ffn_msel(f)
                    ffn_qkv(f)
                bc_proj(b, 1, (1,))
                if f is not None:
                    ffn_qT(f)
                bc_proj(b, 1, (2,))
                if f is not None:
                    ffn_scores(f)
                bc_proj(b, 1, (3, 4))
                if f is not None:
                    ffn_AT(f)
                bc_proj(b, 1, (5,))
                if f is not None:
                    ffn_av(f)
                decay_jobs(b)
                if f is not None:
                    pe.wait_ge(*ffn.read(f, F_AV))
                    ffn_turn(f, F_OT, ob)
                bc_proj(b, 1, (6,))
                if f is not None:
                    ffn_wo(f)
                bc_proj(b, 1, (7,))
                if f is not None:
                    pe.wait_ge(hnb_ready, at(hnb_ready, f, 1))
                    ffn_turn(f, F_HNBT, hn)
                carry_rows(b, 0)
                if f is not None:
                    ffn_w1(f)
                carry_rows(b, 1)
                if f is not None:
                    ffn_w2(f)
                scan(b)

            batch(0, None)
            pe.wait_ge(fload, 16 * len(ffn_loads))
            pe.wait_ge(setup_dve, SD_ALL)
            with pe.Fori(1, NB) as b:
                batch(b, b - 1)
            f = NB - 1
            gn_stats(f)
            out_(f)
            ffn_wrow(f)
            ffn_rank(f)
            ffn_idx(f)
            pe.wait_ge(hn_ready, at(hn_ready, f, 1))
            ffn_turn(f, F_HNT, hn)
            ffn_mask(f)
            ffn_msel(f)
            ffn_qkv(f)
            ffn_qT(f)
            ffn_scores(f)
            ffn_AT(f)
            ffn_av(f)
            pe.wait_ge(*ffn.read(f, F_AV))
            ffn_turn(f, F_OT, ob)
            ffn_wo(f)
            pe.wait_ge(hnb_ready, at(hnb_ready, f, 1))
            ffn_turn(f, F_HNBT, hn)
            ffn_w1(f)
            ffn_w2(f)


def kernel(**inputs):
    import concourse.bacc as bacc
    import numpy as np
    from concourse.bass_utils import run_bass_kernel_spmd

    def arr(name):
        return np.asarray(inputs[name])

    def by_partition(w):
        return np.ascontiguousarray(w.reshape(-1, P, w.shape[-1]).transpose(1, 0, 2))

    rep = INNER // HEADS
    columns = np.concatenate([
        arr("L0_attn_conv_w")[:, 0, :], arr("L0_attn_conv_b")[:, None],
        np.repeat(arr("L0_attn_d_param"), rep)[:, None], arr("L0_attn_gn_w")[:, None],
        arr("L0_attn_gn_b")[:, None]], axis=1)
    lncols = np.stack([arr("L0_ffn_ln1").reshape(KD, P).T, arr("L0_ffn_ln2").reshape(KD, P).T], axis=1)
    arrays = {
        "x": arr("L0_attn_input_tensor"),
        "wxT": arr("L0_attn_Wx").T, "wzT": arr("L0_attn_Wz").T, "wbT": arr("L0_attn_Wb").T,
        "wcT": arr("L0_attn_Wc").T, "wdtT": np.tile(arr("L0_attn_Wdt").T, (1, G3)), "woT": arr("L0_attn_Wout").T,
        "cols": by_partition(columns),
        "rows48": np.tile(np.stack([arr("L0_attn_b_dt"), arr("L0_attn_log_a")], axis=1), (G3, 1)),
        "mask": arr("L0_ffn_attention_mask").reshape(MB * L, L),
        "pos": arr("L0_ffn_position_ids").reshape(MB * L, 1),
        "rw": arr("L0_ffn_router_w").reshape(D), "rb": arr("L0_ffn_router_b"),
        "wqkv": np.concatenate([arr("L0_ffn_wq"), arr("L0_ffn_wk"), arr("L0_ffn_wv")], axis=1),
        "wo": arr("L0_ffn_wo"), "w1": arr("L0_ffn_w1"), "w2": arr("L0_ffn_w2"), "lncols": lncols,
        "cT": arr("L0_c").T, "wmod": arr("L0_wmod"),
    }
    nc = bacc.Bacc("TRN2", target_bir_lowering=False, num_devices=1)
    aps = {}
    for name, a in arrays.items():
        arrays[name] = a = np.ascontiguousarray(a)
        aps[name] = nc.dram_tensor(name, a.shape, mybir.dt.from_np(a.dtype), kind="ExternalInput").ap()
    out = nc.dram_tensor("out", (NB * L, D), F32, kind="ExternalOutput").ap()
    adaln_block(nc, out=out, **aps)
    result = run_bass_kernel_spmd(nc, [arrays], core_ids=[0])
    return result.results[0]["out"].reshape(NB, L, D)
```

```python
from contextlib import ExitStack

import concourse.bass as bass
from concourse import mybir
from concourse.alu_op_type import AluOpType as ALU

F32 = mybir.dt.float32
BF16 = mybir.dt.bfloat16
I32 = mybir.dt.int32
U32 = mybir.dt.uint32
ACT = mybir.ActivationFunctionType
AX = mybir.AxisListType

P = 128
NB, L, D = 8, 1024, 256
MB = 4
INNER, HEADS, STATE, TAPS = 512, 8, 64, 4
T = L // P
KD, KC = D // P, INNER // P
HALF = L // 2
G3 = 6
RW = G3 * HEADS
FH, HD, F = 16, 16, 1024
KSEL = L // 8
NSEL = KSEL - 1
FT = F // P
EPS = 1e-5
MASKED = -1e30
ROPE_BASE = 10000.0
PI = 3.141592653589793
ROUND = 12582912.0
TWO_PI = (6.28125, 0.0019352436065673828, 6.35732715934e-08)
SD_MOD, SD_MIX, SD_ALL = 10, 14, 18
SP_ALL = 68
CHAINS = {"A": 2, "V": 9, "D": 14, "S": 3, "G": 17, "R": 33, "O": 8}


PER_BATCH = {}


def at(sem, b, k):
    return b * PER_BATCH[id(sem)] + k


def later(b):
    return not isinstance(b, int) or b > 0


class Chain:

    def __init__(self, sem, name):
        self.sem, self.name, self.k = sem, name, 0

    def __call__(self, eng, b, ins):
        ins.then_inc(self.sem, 1)
        self.k += 1
        eng.wait_ge(self.sem, at(self.sem, b, self.k))

    def end(self):
        assert self.k == CHAINS[self.name], (self.name, self.k)
        self.k = 0


class Ring:

    def __init__(self, banks, filled, drained):
        self.banks, self.filled, self.drained = banks, filled, drained

    def bank(self, q):
        return self.banks[q % 4]

    def full(self, b, q):
        return self.filled[q % 4], at(self.filled[q % 4], b, q // 4 + 1)

    def read(self, b, q):
        return self.drained[q % 4], at(self.drained[q % 4], b, q // 4 + 1)


def adaln_block(nc, x, wxT, wzT, wbT, wcT, wdtT, woT, cols, rows48, mask, pos, rw, rb,
                wqkv, wo, w1, w2, lncols, cT, wmod, out):
    ctx = ExitStack()
    with ctx:
        def sb(name, shape, dt=F32):
            return ctx.enter_context(nc.sbuf_tensor(name, shape, dt))

        def chunk(c):
            return slice((c % 4) * P, (c % 4) * P + P)

        def sig(name, per=1):
            sem = ctx.enter_context(nc.semaphore(name))
            PER_BATCH[id(sem)] = per
            return sem

        mod_d = nc.dram_tensor("mod_scratch", (NB, 6 * D), F32, kind="Internal").ap()
        x1_d = nc.dram_tensor("x1_scratch", (L, D), F32, kind="Internal").ap()

        wx_s = sb("wx_s", [P, KD, INNER])
        wz_s = sb("wz_s", [P, KD, INNER])
        wb_s = sb("wb_s", [P, KC, INNER])
        wc_s = sb("wc_s", [P, KC, INNER])
        wdt_s = sb("wdt_s", [P, KC, RW])
        wo_s = sb("wo_s", [P, KC, D])
        wqkv_s = sb("wqkv_s", [P, KD, 3 * D])
        fwo_s = sb("fwo_s", [P, KD, D])
        w1_s = sb("w1_s", [P, KD, F])
        w2_s = sb("w2_s", [P, FT, D])
        cols_s = sb("cols_s", [P, KC, 8])
        ln_s = sb("ln_s", [P, 2, KD])
        r48_s = sb("r48_s", [RW, 2])
        rw_s = sb("rw_s", [P, D])
        rb_s = sb("rb_s", [P, 1])
        ident = sb("ident", [P, P])
        identb = sb("identb", [P, P], BF16)
        causal = sb("causal", [P, 4, P], BF16)
        ones_b = sb("ones_b", [P, 1], BF16)
        tri = sb("tri", [P, P])
        halfmean = sb("halfmean", [P, P])
        iota_r = sb("iota_r", [P, P])
        tok = sb("tok", [P, T])
        ones4 = sb("ones4", [P, KC, T])
        spare = sb("spare", [P, 4])
        negone = sb("negone", [P, T])
        mhalf = sb("mhalf", [P, T])
        gmask = sb("gmask", [RW, 8])
        gneg = sb("gneg", [RW, 1])
        delta = sb("delta", [RW, HEADS])
        selp = sb("selp", [RW, 4, P], BF16)
        reset = sb("reset", [RW, T, P], BF16)
        zero48 = sb("zero48", [RW, 1])
        aneg = sb("aneg", [RW, 1])
        invf = sb("invf", [P, 2, HD // 2])
        phase = sb("phase", [P, 2, 2, HD // 2])
        mcol = sb("mcol", [P, 4, NB])
        mc = sb("mc", [P, 4])
        modrow = sb("modrow", [P, 4, D])
        xr = sb("xr", [P, T, D])
        hT = sb("hT", [P, KD, L])
        xc = sb("xc", [P, KC * (L + TAPS - 1) + 4])
        xT = sb("xT", [P, KC, L])
        zs = sb("zs", [P, KC, L])
        BT = sb("BT", [P, 2, KC, HALF])
        CT = sb("CT", [P, 2, KC, HALF])
        EC = sb("EC", [P, KC * L])
        Lw = sb("Lw", [RW, L], BF16)
        dw = sb("dw", [P, T, 2 * HEADS])
        dec = sb("dec", [P, KC, T])
        st6 = sb("st6", [P, T, 6])
        mv = sb("mv", [P, T, 2])
        rstd = sb("rstd", [P, T])
        mrs = sb("mrs", [P, T])
        Sbd = sb("Sbd", [P, KC, P])
        Sdc = sb("Sdc", [P, KC, P])
        Eg = sb("Eg", [P, 2 * HALF])
        Mt = sb("Mt", [P, 2, 2 * HALF])
        XB = sb("XB", [P, 2, 2, INNER])
        yst = sb("yst", [P, KC, 12])
        ymv = sb("ymv", [P, KC, 2])
        pk = sb("pk", [P, 4, KC])
        gab = sb("gab", [P, 6, KC])
        st6b = sb("st6b", [P, T, 6])
        mvb = sb("mvb", [P, T, 2])
        rstdb = sb("rstdb", [P, T])
        wcol = sb("wcol", [P, T])
        c0 = sb("c0", [P, 1])
        boff = sb("boff", [P, 1])
        moff = sb("moff", [P, 1])
        rank = sb("rank", [P, T])
        tokens_after = sb("tokens_after", [P, T])
        above = sb("above", [P, T])
        picked = sb("picked", [P, 2])
        xidx = sb("xidx", [P, 1], U32)
        gidx = sb("gidx", [P, 1], U32)
        midx = sb("midx", [P, 1], U32)
        posi = sb("posi", [P, 1], I32)
        posf = sb("posf", [P, 1])
        sm = sb("sm", [P, 16])
        st1 = sb("st1", [P, 6])
        ang = sb("ang", [P, 2, HD // 2])
        trn = sb("trn", [P, 2, HD // 2])
        sc_ = sb("sc_", [P, 2, HD // 2])
        mx = sb("mx", [P, FH])
        den = sb("den", [P, FH])

        xcv = xc[:, 0:KC * (L + TAPS - 1)].rearrange("p (k n) -> p k n", k=KC)
        R8 = xc[0:RW, 0:4 * L].bitcast(BF16).rearrange("p (h n) -> p h n", h=HEADS)
        ECv = EC[:, :].rearrange("p (k n) -> p k n", k=KC)
        v48, dt48 = xc[0:RW, 0:L], xc[0:RW, L:2 * L]
        lo = xc[0:RW, 2 * L:2 * L + HALF].bitcast(BF16)
        Rw = Sdc[0:RW, :, :].rearrange("p a b -> p (a b)").bitcast(BF16)
        xin = BT[:, 0, :, :].rearrange("p a n -> p (a n)").rearrange("p (t n) -> p t n", t=T)
        h2 = EC[:, 0:T * D].rearrange("p (t n) -> p t n", t=T)
        wog_s = CT[:, 0, 0:2, :].rearrange("p a n -> p (a n)").rearrange("p (k n) -> p k n", k=KC)
        rwc, cg, sg = CT[:, 1, 0, 0:D], CT[:, 1, 0, D:2 * D], CT[:, 1, 1, 0:D]
        a48 = hT[0:RW, 0, :]
        b48 = hT[0:RW, 1, :]
        hi = hT[0:RW, 1, 0:HALF].bitcast(BF16)
        mid = hT[0:RW, 1, HALF:L].bitcast(BF16)
        Gt = []
        for where, tiles in ((EC[:, 2048:4096].bitcast(BF16), range(0, 4)), (Mt[:, 1, :].bitcast(BF16), range(4, T))):
            o = 0
            for t in tiles:
                Gt.append(where[:, o:o + (T - t) * P])
                o += (T - t) * P
        scr = EC[:, 0:2048].rearrange("p (h n) -> p h n", h=FH)
        AT = EC[:, 2048:4096].rearrange("p (h n) -> p h n", h=FH)
        qk = EC[:, 0:512]
        rt = EC[:, 512:1024]
        qkr = EC[:, 2048:3072].rearrange("p (s h n) -> p s h n", s=2, h=FH)
        qT = EC[:, 3072:3584].rearrange("p (m n) -> p m n", m=4)
        kT = EC[:, 3584:4096].rearrange("p (m n) -> p m n", m=4)
        wrow = Eg
        Pm = Mt[:, 0, :].rearrange("p (t n) -> p t n", t=T)
        mrows = Mt[:, 1, :]
        mT = XB[:, 0, :, :].rearrange("p a b -> p (a b)").rearrange("p (t n) -> p t n", t=T)
        gT = XB[:, 1, :, :].rearrange("p a b -> p (a b)").rearrange("p (t n) -> p t n", t=FT)
        xs, hs, hn, vs, ob, x1s, hnT_, oT_ = (xr[:, i, :] for i in range(8))
        hnT = hnT_.rearrange("p (k n) -> p k n", k=KD)
        oT = oT_.rearrange("p (k n) -> p k n", k=KD)
        msel = Sbd[:, 0, :]
        junk = oT_
        junkt = XB[:, 1, :, :].rearrange("p a b -> p (a b)")
        junkd = Mt[:, 0, 0:2 * D].rearrange("p (a n) -> p a n", a=2)
        mcin_s = sb("mcin_s", [P, KD, NB])
        mcin = mcin_s[:, :, :]
        wmod_s = xT[:, 0:3, :].rearrange("p k n -> p (k n)")[:, 0:KD * 6 * D].rearrange("p (k n) -> p k n", k=KD)
        mod8 = CT[0:NB, 1, :, :].rearrange("p a n -> p (a n)")[:, 0:6 * D]
        sgn8, abs8 = EC[0:NB, L:L + D], EC[0:NB, L + D:L + 2 * D]
        dlt6 = EC[0:RW, 0:RW].rearrange("p (g h) -> p g h", g=G3)
        delt3 = sb("delt3", [RW, HEADS])

        ps = [ctx.enter_context(nc.psum_tensor(f"ps{i}", [P, 512], F32)) for i in range(8)]

        wload = ctx.enter_context(nc.semaphore("first_weights_loaded"))
        wload2 = ctx.enter_context(nc.semaphore("mixer_weights_loaded"))
        fload = ctx.enter_context(nc.semaphore("ffn_weights_loaded"))
        mload = ctx.enter_context(nc.semaphore("mod_inputs_loaded"))
        mload2 = ctx.enter_context(nc.semaphore("mod_rest_loaded"))
        setup_pool = ctx.enter_context(nc.semaphore("setup_pool"))
        setup_dve = ctx.enter_context(nc.semaphore("setup_dve"))
        setup_act = ctx.enter_context(nc.semaphore("setup_act"))
        setup_pe = ctx.enter_context(nc.semaphore("setup_pe"))
        mod_stored = ctx.enter_context(nc.semaphore("mod_stored"))
        x_loaded = sig("x_loaded", 16)
        xr_loaded = sig("xr_loaded", 16)
        modrow_loaded = sig("modrow_loaded", 16)
        mc_ready = sig("mc_ready")
        var_ready = sig("var_ready")
        rstd_ready = sig("rstd_ready", 3)
        xn_ready = sig("xn_ready", T)
        tap_ready = sig("conv_last_tap_ready", 8)
        conv_ready = sig("conv_ready", 8)
        xT_ready = sig("xT_ready", 8)
        u_ready = sig("dt_u_ready")
        l_ready = sig("dt_log_ready", 2)
        dif_ready = sig("dif_ready")
        wexp_ready = sig("wexp_ready")
        rows_ready = sig("decay_rows_ready", HEADS)
        v_ready = sig("v_ready")
        dec_ready = sig("dec_ready")
        CE_ready = sig("CE_ready", 8)
        cd_filled = sig("cumdiff_filled", 2 * T)
        Eg_ready = sig("decay_ready", 2 * T)
        sc_filled = sig("scores_filled", 2 * T)
        Mt_ready = sig("masked_scores_ready", 2 * T)
        xt_filled = sig("xt_filled", T)
        bt_filled = sig("bt_filled", T - 1)
        Xd_ready = sig("Xd_ready", T)
        Bw_ready = sig("Bw_ready", T - 1)
        y_filled = sig("y_filled", T)
        y_ready = sig("y_ready", T)
        s_filled = sig("s_filled", T - 1)
        S_ready = sig("state_ready", T - 1)
        Sdc_ready = sig("state_decayed", T - 2)
        pk_ready = sig("gn_stats_ready")
        pk_filled = sig("gn_stats_filled")
        gvar_ready = sig("gn_var_ready")
        grstd_ready = sig("gn_rstd_ready")
        wog_ready = sig("wog_ready")
        yn_ready = sig("yn_ready", 8)
        g_ready = sig("gated_ready", 4)
        out_filled = sig("out_filled", 4)
        x1_ready = sig("x1_ready", 4)
        var2_ready = sig("var2_ready", 4)
        rstd2_ready = sig("rstd2_ready", 4)
        hn2_ready = sig("hn2_ready", T)
        w_ready = sig("w_ready", T)
        rows2_ready = sig("folded_rows_ready")
        c0_ready = sig("router_constant_ready")
        gd_ready = sig("gated_by_dve_ready", 4)
        wcol_ready = sig("wcol_ready")
        base_ready = sig("base_ready", 4)
        x1_stored = sig("x1_stored", 64)
        base_stored = sig("base_stored", 64)
        G_ready = sig("compare_ready", T)
        P_ready = sig("onehot_ready", T)
        gidx_ready = sig("gidx_ready")
        xs_loaded = sig("xs_gathered", 16)
        m_loaded = sig("mask_gathered", 16)
        pos_loaded = sig("pos_gathered", 16)
        fv_ready = sig("ffn_var_ready")
        fr_ready = sig("ffn_rstd_ready")
        fs_ready = sig("ffn_rms1_ready")
        frr_ready = sig("ffn_rms1_inv")
        fs2_ready = sig("ffn_rms2_ready")
        frr2_ready = sig("ffn_rms2_inv")
        hn_ready = sig("ffn_hn_ready")
        mclamp_ready = sig("mask_clamped")
        qkz_ready = sig("rope_pad_zero")
        ang_ready = sig("angles_ready")
        sin_ready = sig("sin_ready")
        rope_ready = sig("rope_ready")
        mx_ready = sig("max_ready", 4)
        prob_ready = sig("prob_ready", FH)
        hnb_ready = sig("ffn_hn2_ready")
        so_ready = sig("proc_ready")
        scattered = sig("scattered", 16)

        def ring(name, banks, jobs):
            return Ring(banks, [sig(f"{name}_filled{i}", len(range(i, jobs, 4))) for i in range(4)],
                        [sig(f"{name}_drained{i}", len(range(i, jobs, 4))) for i in range(4)])

        proj = ring("proj", ps[0:4], 47)
        ffn = ring("ffn", ps[4:8], 27)
        J_H, J_X, J_Z, J_DT, J_V, J_EC = 0, 4, 12, 28, 36, 39
        J_BC = ((20, 21, 22, 23, 24, 25, 26, 27), (30, 31, 32, 33, 34, 35, 37, 38))
        (F_WROW, F_RANK, F_IDX, F_HNT, F_MT, F_MSEL, F_QK, F_V, F_QT, F_KT, F_SC, F_AT, F_AV, F_OT, F_WO,
         F_HNBT, F_W1, F_W2) = 0, 2, 3, 4, 5, 7, 8, 9, 10, 11, 12, 16, 20, 21, 22, 23, 24, 26

        chA, chV, chD, chS, chG, chR, chO = (Chain(sig("chain" + c, CHAINS[c]), c) for c in "AVDSGRO")

        block = ctx.enter_context(nc.Block())

        def kp(w):
            return w.rearrange("(k p) n -> p k n", p=P)

        first_loads = ((r48_s[:, :], rows48), (cols_s[:, :, :], cols), (wx_s[:, :, :], kp(wxT)),
                       (wz_s[:, :, :], kp(wzT)))
        mixer_loads = ((wdt_s[:, :, :], kp(wdtT)), (wb_s[:, :, :], kp(wbT)),
                       (wc_s[:, :, :], kp(wcT)), (wo_s[:, :, :], kp(woT)), (rw_s[:, :], rw.partition_broadcast(P)),
                       (rb_s[:, :], rb.partition_broadcast(P)))
        ffn_loads = ((wqkv_s[:, :, :], kp(wqkv)), (fwo_s[:, :, :], kp(wo)), (w1_s[:, :, :], kp(w1)),
                     (w2_s[:, :, :], kp(w2)), (ln_s[:, :, :], lncols))

        @block.sync
        def _(sp):

            sp.dma_start(mcin, cT.rearrange("(k p) n -> p k n", p=P)).then_inc(mload, 16)
            sp.dma_start(wmod_s[:, :, 0:2 * D], kp(wmod)[:, :, 0:2 * D]).then_inc(mload, 16)
            sp.dma_start(xin[:, :, :], x[0, :, :].rearrange("(t p) n -> p t n", p=P)).then_inc(x_loaded, 16)
            sp.dma_start(wmod_s[:, :, 2 * D:], kp(wmod)[:, :, 2 * D:]).then_inc(mload2, 16)
            for dst, src in first_loads:
                sp.dma_start(dst, src).then_inc(wload, 16)
            for dst, src in mixer_loads:
                sp.dma_start(dst, src).then_inc(wload2, 16)
            for dst, src in ffn_loads:
                sp.dma_start(dst, src).then_inc(fload, 16)
            sp.wait_ge(setup_dve, SD_MOD)
            sp.dma_start(mod_d[:, :], mod8).then_inc(mod_stored, 16)
            sp.wait_ge(mod_stored, 16)

            def loads(b):
                if later(b):
                    sp.wait_ge(so_ready, at(so_ready, b - 1, 1))
                if later(b):
                    sp.wait_ge(scattered, at(scattered, b - 1, 16))
                sp.dma_start(modrow[:, :, :].rearrange("p a n -> p (a n)"),
                             mod_d[bass.ds(b, 1), 2 * D:6 * D].rearrange("a n -> (a n)").partition_broadcast(P)
                             ).then_inc(modrow_loaded, 16)
                sp.dma_start(xr[:, :, :], x[bass.ds(b, 1), :, :].rearrange("a (t p) n -> p (a t) n", p=P)
                             ).then_inc(xr_loaded, 16)

            def prefetch(b):
                sp.wait_ge(sc_filled, at(sc_filled, b, 8))
                sp.wait_ge(bt_filled, at(bt_filled, b, 4))
                sp.dma_start(xin[:, :, :], x[bass.ds(b + 1, 1), :, :].rearrange("a (t p) n -> p (a t) n", p=P)
                             ).then_inc(x_loaded, 16)

            def stores(b):
                for j in range(4):
                    rows = slice(2 * j, 2 * j + 2)
                    sp.wait_ge(x1_ready, at(x1_ready, b, j + 1))
                    sp.dma_start(x1_d[2 * j * P:2 * (j + 1) * P, :].rearrange("(t p) n -> p t n", p=P),
                                 xr[:, rows, :]).then_inc(x1_stored, 16)
                    sp.wait_ge(base_ready, at(base_ready, b, j + 1))
                    sp.dma_start(out[bass.ds(b * L + 2 * j * P, 2 * P), :].rearrange("(t p) n -> p t n", p=P),
                                 h2[:, rows, :]).then_inc(base_stored, 16)

            loads(0)
            prefetch(0)
            stores(0)
            with sp.Fori(1, NB - 1) as b:
                loads(b)
                prefetch(b)
                stores(b)
            loads(NB - 1)
            stores(NB - 1)
            sp.wait_ge(x1_stored, at(x1_stored, NB - 1, 64))
            sp.wait_ge(base_stored, at(base_stored, NB - 1, 64))
            sp.wait_ge(scattered, at(scattered, NB - 1, 16))

        @block.gpsimd
        def _(pool):
            g = nc.gpsimd
            n = [0]

            def link(ins):
                ins.then_inc(setup_pool, 1)
                n[0] += 1
                pool.wait_ge(setup_pool, n[0])

            def ln_in(b):
                pool.wait_ge(var_ready, at(var_ready, b, 1))
                g.tensor_tensor(rstd[:, :], rstd[:, :], mhalf[:, :], ALU.pow).then_inc(rstd_ready, 1)
                pool.wait_ge(rstd_ready, at(rstd_ready, b, 1))
                g.tensor_tensor(mrs[:, :], mv[:, :, 0], rstd[:, :], ALU.mult).then_inc(rstd_ready, 1)
                pool.wait_ge(rstd_ready, at(rstd_ready, b, 2))
                g.tensor_tensor(mrs[:, :], mrs[:, :], negone[:, :], ALU.mult).then_inc(rstd_ready, 1)

            link(g.memset(ident[:, :], 0.0))
            link(g.affine_select(out=ident[:, :], in_=ident[:, :], compare_op=ALU.not_equal, fill=1.0,
                                 base=0, pattern=[[-1, P]], channel_multiplier=1))
            link(g.memset(mhalf[:, :], -0.5))
            link(g.memset(negone[:, :], -1.0))
            link(g.tensor_copy(identb[:, :], ident[:, :]))
            link(g.memset(tri[:, :], 1.0))
            link(g.affine_select(out=tri[:, :], in_=tri[:, :], compare_op=ALU.is_gt, fill=0.0,
                                 base=0, pattern=[[1, P]], channel_multiplier=-1))
            link(g.memset(causal[:, :, :], 0.0))
            link(g.affine_select(out=causal[:, :, :], in_=causal[:, :, :], compare_op=ALU.is_ge, fill=MASKED,
                                 base=0, pattern=[[0, 4], [1, P]], channel_multiplier=-1))
            link(g.memset(ones_b[:, :], 1.0))
            link(g.memset(halfmean[:, :], 0.0))
            link(g.memset(halfmean[0:64, 0:64], 1.0 / STATE))
            link(g.memset(halfmean[64:128, 64:128], 1.0 / STATE))
            link(g.iota(iota_r[:, :], pattern=[[1, P]], base=0, channel_multiplier=0,
                        allow_small_or_imprecise_dtypes=True))
            link(g.iota(tok[:, :], pattern=[[P, T]], base=0, channel_multiplier=1,
                        allow_small_or_imprecise_dtypes=True))
            link(g.iota(tokens_after[:, :], pattern=[[-P, T]], base=(T - 1) * P, channel_multiplier=0,
                        allow_small_or_imprecise_dtypes=True))
            link(g.memset(above[:, :], 0.0))
            link(g.memset(ones4[:, :, :], 1.0))
            for i in range(G3 + 2):
                first, last = (i, i) if i < G3 else ((0, 2) if i == G3 else (3, 5))
                link(g.memset(gmask[:, i:i + 1], 1.0))
                link(g.affine_select(out=gmask[:, i:i + 1], in_=gmask[:, i:i + 1], compare_op=ALU.is_ge,
                                     fill=0.0, base=-HEADS * first, pattern=[[0, 1]], channel_multiplier=1))
                link(g.affine_select(out=gmask[:, i:i + 1], in_=gmask[:, i:i + 1], compare_op=ALU.is_ge,
                                     fill=0.0, base=HEADS * last + HEADS - 1, pattern=[[0, 1]],
                                     channel_multiplier=-1))
            link(g.tensor_scalar(gneg[:, :], gmask[:, G3:G3 + 1], -1.0, None, ALU.mult))
            link(g.memset(dlt6, 0.0))
            link(g.affine_select(out=dlt6, in_=dlt6, compare_op=ALU.not_equal, fill=1.0, base=0,
                                 pattern=[[-HEADS, G3], [-1, HEADS]], channel_multiplier=1))
            for i in range(G3):
                link(g.tensor_copy(delta[:, :], dlt6[:, 0, :]) if i == 0 else
                     g.tensor_tensor(delta[:, :], delta[:, :], dlt6[:, i, :], ALU.add))
            link(g.memset(reset[:, :, :], 1.0))
            link(g.memset(reset[:, :, 0:1], 0.0))
            ln_in(0)
            for i in range(HD // 2):
                link(g.memset(invf[:, :, i:i + 1], 1.0 / ROPE_BASE ** (2.0 * i / HD)))
            link(g.memset(phase[:, :, 0, :], 0.0))
            link(g.memset(phase[:, 0, 1, :], 0.25))
            link(g.memset(phase[:, 1, 1, :], PI / 2))
            link(g.memset(Sbd[:, :, :], 0.0))
            link(g.memset(Sdc[:, :, :], 0.0))
            link(g.memset(boff[:, :], 0.0))
            link(g.memset(zero48[:, :], 0.0))
            assert n[0] == SP_ALL, n[0]

            def carry(b):
                pool.wait_ge(*proj.read(b, J_EC + 7))
                g.tensor_tensor(dec[:, :, :], ECv[:, :, P - 1::P], ones4[:, :, :], ALU.mult).then_inc(dec_ready, 1)
                pool.wait_ge(dec_ready, at(dec_ready, b, 1))
                pool.wait_ge(*proj.read(b, J_BC[1][7]))
                for half in range(2):
                    for k in range(KC):
                        s = ECv[:, k, half * HALF:(half + 1) * HALF]
                        g.tensor_tensor(s, s, CT[:, half, k, :], ALU.mult).then_inc(CE_ready, 1)

            def decays(b):
                for c in range(1, T - 1):
                    pool.wait_ge(S_ready, at(S_ready, b, c))
                    g.tensor_tensor(Sdc[:, :, :], Sbd[:, :, :], dec[:, :, c:c + 1].broadcast_to([P, KC, P]),
                                    ALU.mult).then_inc(Sdc_ready, 1)
                    if c == 5:
                        pool.wait_ge(modrow_loaded, at(modrow_loaded, b, 16))
                        pool.wait_ge(sc_filled, at(sc_filled, b, 8))
                        g.tensor_tensor(wog_s, wo_s[:, :, :], modrow[:, 0:1, :].broadcast_to([P, KC, D]),
                                        ALU.mult).then_inc(wog_ready, 1)

            def fold_rows(b):
                pool.wait_ge(sc_filled, at(sc_filled, b, 16))
                g.tensor_tensor(rwc, modrow[:, 2, :], rw_s[:, :], ALU.mult)
                g.tensor_tensor(cg, modrow[:, 2, :], modrow[:, 3, :], ALU.mult)
                g.tensor_tensor(sg, modrow[:, 1, :], modrow[:, 3, :], ALU.mult).then_inc(rows2_ready, 1)

            def out_(b):
                fold_rows(b)
                pool.wait_ge(gvar_ready, at(gvar_ready, b, 1))
                g.tensor_tensor(gab[:, 1, :], gab[:, 0, :], mhalf[:, 0:KC], ALU.pow).then_inc(grstd_ready, 1)
                for half in range(2):
                    for k in range(2):
                        s = slice(half * HALF, (half + 1) * HALF)
                        pool.wait_ge(yn_ready, at(yn_ready, b, half * KC + k + 1))
                        g.tensor_tensor(xT[:, k, s], xT[:, k, s], zs[:, k, s], ALU.mult).then_inc(g_ready, 1)
                for j in range(4):
                    pool.wait_ge(var2_ready, at(var2_ready, b, j + 1))
                    q = slice(2 * j, 2 * j + 2)
                    g.tensor_tensor(rstdb[:, q], rstdb[:, q], mhalf[:, q], ALU.pow).then_inc(rstd2_ready, 1)
                for j in range(4):
                    base(b, j)
                chO.end()

            def base(b, j):
                q = slice(2 * j, 2 * j + 2)
                pool.wait_ge(w_ready, at(w_ready, b, 2 * j + 2))
                for i, row in enumerate((cg, sg)):
                    chO(pool, b, g.tensor_tensor(h2[:, q, :], h2[:, q, :],
                                                 row.unsqueeze(1).broadcast_to([P, 2, D]),
                                                 ALU.add if i else ALU.mult))
                g.tensor_tensor(h2[:, q, :], h2[:, q, :], xr[:, q, :], ALU.add).then_inc(base_ready, 1)

            def take_waits():
                g.tensor_tensor(spare[:, 0:1], mhalf[:, 0:1], mhalf[:, 1:2], ALU.mult)

            def gather(b):
                pool.wait_ge(gidx_ready, at(gidx_ready, b, 1))
                pool.wait_ge(x1_stored, at(x1_stored, b, 64))
                take_waits()
                g.indirect_dma_start(xs, None, x1_d[:, :], bass.IndirectOffsetOnAxis(ap=xidx[:, 0:1], axis=0)
                                     ).then_inc(xs_loaded, 16)
                g.indirect_dma_start(mrows, None, mask, bass.IndirectOffsetOnAxis(ap=midx[:, 0:1], axis=0)
                                     ).then_inc(m_loaded, 16)
                g.indirect_dma_start(posi[:, :], None, pos, bass.IndirectOffsetOnAxis(ap=midx[:, 0:1], axis=0)
                                     ).then_inc(pos_loaded, 16)
                g.memset(qkr[:, :, :, HD:2 * HD], 0.0).then_inc(qkz_ready, 1)

            def small_pow(b, before, after, col):
                pool.wait_ge(before, at(before, b, 1))
                g.tensor_tensor(sm[:, col + 1:col + 2], sm[:, col:col + 1], mhalf[:, 0:1], ALU.pow
                                ).then_inc(after, 1)

            def scatter(b):
                pool.wait_ge(so_ready, at(so_ready, b, 1))
                pool.wait_ge(base_stored, at(base_stored, b, 64))
                take_waits()
                g.indirect_dma_start(out, bass.IndirectOffsetOnAxis(ap=gidx[0:NSEL, 0:1], axis=0),
                                     x1s[0:NSEL, :], None).then_inc(scattered, 16)

            def ffn_all(b):
                gather(b)
                small_pow(b, fv_ready, fr_ready, 0)
                small_pow(b, fs_ready, frr_ready, 2)
                small_pow(b, fs2_ready, frr2_ready, 4)
                scatter(b)

            def rest(b, last=False):
                carry(b)
                decays(b)
                if not last:
                    ln_in(b + 1)
                out_(b)

            rest(0)
            with pool.Fori(1, NB - 1) as b:
                ffn_all(b - 1)
                rest(b)
            ffn_all(NB - 2)
            rest(NB - 1, last=True)
            ffn_all(NB - 1)

        @block.scalar
        def _(act):
            a = nc.scalar
            act.wait_ge(mload, 16 * 2)
            a.activation(mcin, mcin, ACT.Silu).then_inc(setup_act, 1)
            act.wait_ge(setup_pe, 1)
            a.activation(mod8[:, 0:2 * D], ps[4][0:NB, :], ACT.Copy).then_inc(setup_act, 1)
            act.wait_ge(setup_pe, 2)
            a.activation(mcol[:, :, :], ps[7][:, 0:4 * NB].rearrange("p (a n) -> p a n", a=4), ACT.Copy
                         ).then_inc(setup_act, 1)
            for j in (1, 2):
                act.wait_ge(setup_pe, j + 2)
                a.activation(mod8[:, 2 * j * D:2 * (j + 1) * D], ps[4 + j][0:NB, :], ACT.Copy).then_inc(setup_act, 1)

            def ln_apply(b, half):
                act.wait_ge(rstd_ready, at(rstd_ready, b, 3))
                for t in range(4 * half, 4 * half + 4):
                    a.activation(xin[:, t, :], xin[:, t, :], ACT.Identity, bias=mrs[:, t:t + 1],
                                 scale=rstd[:, t:t + 1]).then_inc(xn_ready, 1)

            def ln_in(b):
                act.wait_ge(mc_ready, at(mc_ready, b, 1))
                for half in range(2):
                    for k in range(KD):
                        q = J_H + half * KD + k
                        act.wait_ge(*proj.full(b, q))
                        bank = proj.bank(q)
                        act_in = a.activation(hT[:, k, half * HALF:(half + 1) * HALF], bank[:, :], ACT.Identity,
                                              bias=mc[:, k:k + 1], scale=mc[:, 2 + k:3 + k])
                        act_in.then_inc(proj.drained[q % 4], 1)

            def x_copies(b):
                for half in range(2):
                    for m in range(KC):
                        q = J_X + half * KC + m
                        act.wait_ge(*proj.full(b, q))
                        bank = proj.bank(q)
                        o = TAPS - 1 + half * HALF
                        ins = a.activation(xcv[:, m, o:o + HALF], bank[:, :], ACT.Copy)
                        ins.then_inc(proj.drained[q % 4], 1)

            def last_tap(b, half):
                if later(b):
                    act.wait_ge(out_filled, at(out_filled, b - 1, 2 * half + 2))
                for m in range(KC):
                    act.wait_ge(*proj.read(b, J_X + half * KC + m))
                    o = TAPS - 1 + half * HALF
                    a.activation(xT[:, m, half * HALF:(half + 1) * HALF], xcv[:, m, o:o + HALF], ACT.Identity,
                                 bias=cols_s[:, m, 4:5], scale=cols_s[:, m, 3:4]).then_inc(tap_ready, 1)

            def x_silu(b, half, pair):
                for m in (2 * pair, 2 * pair + 1):
                    s = xT[:, m, half * HALF:(half + 1) * HALF]
                    act.wait_ge(conv_ready, at(conv_ready, b, half * KC + m + 1))
                    a.activation(s, s, ACT.Silu).then_inc(xT_ready, 1)

            def z_silu(b, half, pair):
                for m in (2 * pair, 2 * pair + 1):
                    q = J_Z + half * KC + m
                    act.wait_ge(*proj.full(b, q))
                    a.activation(zs[:, m, half * HALF:(half + 1) * HALF], proj.bank(q)[:, :], ACT.Silu
                                 ).then_inc(proj.drained[q % 4], 1)

            def softplus(b):
                act.wait_ge(u_ready, at(u_ready, b, 1))
                a.activation(a48, a48, ACT.Exp, scale=-1.0).then_inc(l_ready, 1)
                act.wait_ge(l_ready, at(l_ready, b, 1))
                a.activation(b48, a48, ACT.Ln, bias=1.0).then_inc(l_ready, 1)

            def bc_copies(b, half, ms):
                for m in ms:
                    q = J_BC[half][m]
                    act.wait_ge(*proj.full(b, q))
                    a.activation((BT if m < KC else CT)[:, half, m % KC, :], proj.bank(q)[:, :], ACT.Copy
                                 ).then_inc(proj.drained[q % 4], 1)

            def w_exp(b):
                act.wait_ge(dif_ready, at(dif_ready, b, 1))
                a.activation(a48, a48, ACT.Exp).then_inc(wexp_ready, 1)

            def right_rows(b, heads):
                act.wait_ge(v_ready, at(v_ready, b, 1))
                for i in heads:
                    h = 2 * (i % 4) + i // 4
                    a.activation(R8[:, i, :], Rw, ACT.Identity, bias=zero48[:, :], scale=delta[:, h:h + 1]
                                 ).then_inc(rows_ready, 1)

            def ec(b, half):
                for k in range(KC):
                    q = J_EC + half * KC + k
                    act.wait_ge(*proj.full(b, q))
                    a.activation(ECv[:, k, half * HALF:(half + 1) * HALF], proj.bank(q)[:, :], ACT.Exp
                                 ).then_inc(proj.drained[q % 4], 1)

            def scan(b, last):
                for c in range(T):
                    for s in range(2):
                        act.wait_ge(cd_filled, at(cd_filled, b, 2 * c + s + 1))
                        if c or later(b):
                            act.wait_ge(Mt_ready, at(Mt_ready, b, 2 * (c - 1) + s + 1 if c else 0))
                        a.activation(Eg[:, s * HALF:(s + 1) * HALF], ps[s][:, :], ACT.Exp
                                     ).then_inc(Eg_ready, 1)
                if not last:
                    ln_apply(b + 1, 0)
                    ln_apply(b + 1, 1)

            def ffn_wrow(b):
                for j in range(2):
                    act.wait_ge(*ffn.full(b, F_WROW + j))
                    bank = ffn.bank(F_WROW + j)
                    ins = a.activation(wrow[:, j * HALF:(j + 1) * HALF], bank[:, :], ACT.Copy)
                    ins.then_inc(ffn.drained[(F_WROW + j) % 4], 1)

            def ffn_hnT(b):
                act.wait_ge(*ffn.full(b, F_HNT))
                bank = ffn.bank(F_HNT)
                ins = a.activation(hnT_, bank[:, 0:D], ACT.Copy)
                ins.then_inc(ffn.drained[F_HNT % 4], 1)

            def ffn_v(b):
                act.wait_ge(*ffn.full(b, F_V))
                bank = ffn.bank(F_V)
                ins = a.activation(vs, bank[:, 0:D], ACT.Copy)
                ins.then_inc(ffn.drained[F_V % 4], 1)

            def ffn_sin(b):
                act.wait_ge(ang_ready, at(ang_ready, b, 1))
                a.activation(sc_[:, :, :], ang[:, :, :], ACT.Sin).then_inc(sin_ready, 1)

            def ffn_qT(b):
                for j, dst in ((F_QT, qT), (F_KT, kT)):
                    act.wait_ge(*ffn.full(b, j))
                    bank = ffn.bank(j)
                    ins = a.activation(dst.rearrange("p m n -> p (m n)"), bank[:, :], ACT.Copy)
                    ins.then_inc(ffn.drained[j % 4], 1)

            def ffn_softmax(b):
                for h in range(FH):
                    if h % 4 == 0:
                        act.wait_ge(mx_ready, at(mx_ready, b, h // 4 + 1))
                    a.activation(scr[:, h, 0:NSEL], scr[:, h, 0:NSEL], ACT.Exp, bias=mx[:, h:h + 1],
                                 accum_out=den[:, h:h + 1]).then_inc(prob_ready, 1)

            def ffn_AT(b):
                for j in range(4):
                    act.wait_ge(*ffn.full(b, F_AT + j))
                    bank = ffn.bank(F_AT + j)
                    ins = a.activation(AT[0:NSEL, 4 * j:4 * j + 4, :].rearrange("p t n -> p (t n)"),
                                       bank[0:NSEL, :], ACT.Copy)
                    ins.then_inc(ffn.drained[(F_AT + j) % 4], 1)

            def ffn_oT(b):
                act.wait_ge(*ffn.full(b, F_OT))
                bank = ffn.bank(F_OT)
                ins = a.activation(oT_, bank[:, 0:D], ACT.Copy)
                ins.then_inc(ffn.drained[F_OT % 4], 1)

            def ffn_hnbT(b):
                act.wait_ge(*ffn.full(b, F_HNBT))
                bank = ffn.bank(F_HNBT)
                ins = a.activation(hnT_, bank[:, 0:D], ACT.Copy)
                ins.then_inc(ffn.drained[F_HNBT % 4], 1)

            def ffn_gelu(b):
                for j in range(2):
                    act.wait_ge(*ffn.full(b, F_W1 + j))
                    bank = ffn.bank(F_W1 + j)
                    ins = a.activation(gT[:, 4 * j:4 * j + 4, :].rearrange("p t n -> p (t n)"), bank[:, :],
                                       ACT.Gelu_apprx_tanh)
                    ins.then_inc(ffn.drained[(F_W1 + j) % 4], 1)

            def batch(b, f, last=False):
                ln_in(b)
                x_copies(b)
                if f is None:
                    act.wait_ge(mod_stored, 16)
                    act.wait_ge(setup_pool, SP_ALL)
                last_tap(b, 0)
                z_silu(b, 0, 0)
                z_silu(b, 0, 1)
                last_tap(b, 1)
                if f is not None:
                    ffn_wrow(f)
                z_silu(b, 1, 0)
                x_silu(b, 0, 0)
                x_silu(b, 0, 1)
                z_silu(b, 1, 1)
                bc_copies(b, 0, (0, 1, 2, 3, 4))
                x_silu(b, 1, 0)
                bc_copies(b, 0, (5, 6))
                x_silu(b, 1, 1)
                bc_copies(b, 0, (7,))
                if f is not None:
                    ffn_hnT(f)
                    ffn_sin(f)
                softplus(b)
                bc_copies(b, 1, (0,))
                if f is not None:
                    ffn_v(f)
                bc_copies(b, 1, (1,))
                if f is not None:
                    ffn_qT(f)
                bc_copies(b, 1, (2,))
                w_exp(b)
                if f is not None:
                    ffn_softmax(f)
                bc_copies(b, 1, (3, 4))
                if f is not None:
                    ffn_AT(f)
                bc_copies(b, 1, (5,))
                right_rows(b, (0, 1, 2))
                if f is not None:
                    ffn_oT(f)
                right_rows(b, (3, 4, 5, 6))
                bc_copies(b, 1, (6,))
                right_rows(b, (7,))
                bc_copies(b, 1, (7,))
                if f is not None:
                    ffn_hnbT(f)
                ec(b, 0)
                if f is not None:
                    ffn_gelu(f)
                ec(b, 1)
                scan(b, last)

            ln_apply(0, 0)
            ln_apply(0, 1)
            act.wait_ge(wload, 16 * len(first_loads))
            a.activation(aneg[:, :], r48_s[:, 1:2], ACT.Exp).then_inc(setup_act, 1)
            batch(0, None)
            with act.Fori(1, NB - 1) as b:
                batch(b, b - 1)
            batch(NB - 1, NB - 2, last=True)
            f = NB - 1
            ffn_wrow(f)
            ffn_hnT(f)
            ffn_sin(f)
            ffn_v(f)
            ffn_qT(f)
            ffn_softmax(f)
            ffn_AT(f)
            ffn_oT(f)
            ffn_hnbT(f)
            ffn_gelu(f)

        @block.vector
        def _(dve):
            v = nc.vector
            n = [0]

            def link(ins):
                ins.then_inc(setup_dve, 1)
                n[0] += 1
                dve.wait_ge(setup_dve, n[0])

            def take_waits():
                v.tensor_copy(spare[:, 1:2], mhalf[:, 0:1])

            def ln_stats(b):
                dve.wait_ge(x_loaded, at(x_loaded, b, 16))
                for t in range(T):
                    ins = v.bn_stats(st6[:, t, :], xin[:, t, :])
                chA(dve, b, ins)

            def mod_column(b):
                if later(b):
                    dve.wait_ge(*proj.read(b - 1, J_H + 3))
                v.tensor_copy(mc[:, :], mcol[:, :, bass.ds(b, 1)].rearrange("p a n -> p (a n)")
                              ).then_inc(mc_ready, 1)

            def ln_var(b):
                take_waits()
                for t in range(T):
                    ins = v.bn_aggr(mv[:, t, :], st6[:, t, :])
                chA(dve, b, ins)
                v.tensor_scalar(rstd[:, :], mv[:, :, 1], EPS, None, ALU.add).then_inc(var_ready, 1)
                chA.end()

            dve.wait_ge(setup_act, 2)
            link(v.tensor_scalar(mod8[:, D:2 * D], mod8[:, D:2 * D], 1.0, None, ALU.add))
            ln_stats(0)
            dve.wait_ge(setup_pool, 4)
            ln_var(0)
            dve.wait_ge(setup_act, 3)
            mod_column(0)
            dve.wait_ge(setup_act, 5)
            link(v.tensor_scalar(mod8[:, 4 * D:5 * D], mod8[:, 4 * D:5 * D], 1.0, None, ALU.add))
            dve.wait_ge(setup_pool, SP_ALL)
            for i in (2, 5):
                s = mod8[:, i * D:(i + 1) * D]
                link(v.tensor_scalar(sgn8, s, 0.0, 2.0, ALU.is_ge, ALU.mult))
                link(v.scalar_tensor_tensor(abs8, s, -1.0, s, ALU.mult, ALU.max))
                link(v.tensor_scalar(abs8, abs8, 0.25, None, ALU.max))
                link(v.scalar_tensor_tensor(s, sgn8, -1.0, abs8, ALU.add, ALU.mult))
            assert n[0] == SD_MOD, n[0]
            dve.wait_ge(setup_act, 6)
            link(v.tensor_scalar(aneg[:, :], aneg[:, :], -1.0, None, ALU.mult))
            link(v.tensor_scalar(delt3[:, :], delta[:, :], gmask[:, G3:G3 + 1], None, ALU.mult))
            for hh in range(2):
                link(v.tensor_copy(selp[:, :, 64 * hh:64 * hh + 64],
                                   delt3[:, hh::2].unsqueeze(2).broadcast_to([RW, 4, 64])))
            assert n[0] == SD_MIX

            def fold_ln():
                dve.wait_ge(fload, 16 * len(ffn_loads))
                for k in range(KD):
                    link(v.tensor_scalar(wqkv_s[:, k, :], wqkv_s[:, k, :], ln_s[:, 0, k:k + 1], None, ALU.mult))
                    link(v.tensor_scalar(w1_s[:, k, :], w1_s[:, k, :], ln_s[:, 1, k:k + 1], None, ALU.mult))
                assert n[0] == SD_ALL

            def conv(b, half, m2):
                pair = (2 * m2, 2 * m2 + 1)
                for tap in range(TAPS - 1):
                    for m in pair:
                        dst = xT[:, m, half * HALF:(half + 1) * HALF]
                        if tap == 0:
                            dve.wait_ge(tap_ready, at(tap_ready, b, half * KC + m + 1))
                        ins = v.scalar_tensor_tensor(dst, xcv[:, m, half * HALF + tap:half * HALF + tap + HALF],
                                                     cols_s[:, m, tap:tap + 1], dst, ALU.mult, ALU.add)
                        if tap == TAPS - 2:
                            ins.then_inc(conv_ready, 1)
                        elif m == pair[1]:
                            chV(dve, b, ins)

            def conv_first_half(b):
                if later(b):
                    dve.wait_ge(out_filled, at(out_filled, b - 1, 4))
                    dve.wait_ge(cd_filled, at(cd_filled, b - 1, 2 * T))
                dve.wait_ge(*proj.read(b, J_X + 7))
                chV(dve, b, v.memset(xcv[:, :, 0:TAPS - 1], 0.0))
                conv(b, 0, 0)
                conv(b, 0, 1)

            def softplus_in(b):
                for half in range(2):
                    q = J_DT + half
                    dve.wait_ge(*proj.full(b, q))
                    bank = proj.bank(q)
                    s = slice(half * HALF, (half + 1) * HALF)
                    ins = v.tensor_scalar(v48[:, s], bank[64 * half:64 * half + RW, :], r48_s[:, 0:1], None, ALU.add)
                    ins.then_inc(proj.drained[q % 4], 1)
                for half in range(2):
                    dve.wait_ge(*proj.read(b, J_DT + half))
                v.scalar_tensor_tensor(a48, v48, -1.0, v48, ALU.mult, ALU.max).then_inc(u_ready, 1)

            def decay_rows(b):
                dve.wait_ge(l_ready, at(l_ready, b, 2))
                chD(dve, b, v.scalar_tensor_tensor(dt48, v48, 0.0, b48, ALU.max, ALU.add))
                chD(dve, b, v.tensor_scalar(a48, dt48, aneg[:, :], None, ALU.mult))
                chD(dve, b, v.tensor_tensor_scan(v48, reset[:, :, :].rearrange("p t n -> p (t n)"), a48, 0.0,
                                                 ALU.mult, ALU.add))
                chD(dve, b, v.tensor_copy(hi, v48))
                chD(dve, b, v.tensor_tensor(a48, v48, hi, ALU.subtract))
                chD(dve, b, v.tensor_copy(mid, a48))
                chD(dve, b, v.tensor_tensor(lo, a48, mid, ALU.subtract))
                cv = v48.rearrange("p (t n) -> p t n", t=T)
                v.tensor_tensor(a48.rearrange("p (t n) -> p t n", t=T), cv[:, :, P - 1:P].broadcast_to([RW, T, P]),
                                cv, ALU.subtract).then_inc(dif_ready, 1)

            def decay_operands(b):
                chD(dve, b, v.tensor_scalar(Lw[:, :], hi, gmask[:, 0:1], gmask[:, 7:8], ALU.mult, ALU.add))
                chD(dve, b, v.scalar_tensor_tensor(Lw[:, :], mid, gmask[:, 1:2], Lw[:, :], ALU.mult, ALU.add))
                chD(dve, b, v.scalar_tensor_tensor(Lw[:, :], lo, gmask[:, 2:3], Lw[:, :], ALU.mult, ALU.add))
                chD(dve, b, v.tensor_scalar(Rw, hi, gmask[:, 3:4], gneg[:, :], ALU.mult, ALU.add))
                chD(dve, b, v.scalar_tensor_tensor(Rw, mid, gmask[:, 4:5], Rw, ALU.mult, ALU.add))
                chD(dve, b, v.scalar_tensor_tensor(Rw, lo, gmask[:, 5:6], Rw, ALU.mult, ALU.add))
                chD(dve, b, v.tensor_scalar(v48, dt48, gmask[:, 0:1], None, ALU.mult))
                dve.wait_ge(wexp_ready, at(wexp_ready, b, 1))
                v.scalar_tensor_tensor(a48, a48, gmask[:, 1:2], v48, ALU.mult, ALU.add).then_inc(v_ready, 1)
                chD.end()

            def dw_copy(b):
                dve.wait_ge(*proj.full(b, J_V))
                bank = proj.bank(J_V)
                ins = v.tensor_copy(dw[:, :, :],
                                    bank[:, 0:T * RW].rearrange("p (t n) -> p t n", t=T)[:, :, 0:2 * HEADS])
                ins.then_inc(proj.drained[J_V % 4], 1)

            def scan(b, last):
                def weigh(c):
                    dve.wait_ge(*proj.read(b, J_V))
                    if c == 0:
                        if later(b):
                            dve.wait_ge(so_ready, at(so_ready, b - 1, 1))
                    dve.wait_ge(xt_filled, at(xt_filled, b, c + 1))
                    if c >= 2:
                        dve.wait_ge(y_filled, at(y_filled, b, c - 1))
                    if c >= 2:
                        dve.wait_ge(s_filled, at(s_filled, b, c - 1))
                    v.tensor_tensor(XB[:, c % 2, 0, :].rearrange("p (h n) -> p h n", h=HEADS),
                                    ps[6][:, :].rearrange("p (h n) -> p h n", h=HEADS),
                                    dw[:, c, 0:HEADS].unsqueeze(2).broadcast_to([P, HEADS, STATE]), ALU.mult
                                    ).then_inc(Xd_ready, 1)
                    if c < T - 1:
                        dve.wait_ge(bt_filled, at(bt_filled, b, c + 1))
                        v.tensor_tensor(XB[:, c % 2, 1, :].rearrange("p (h n) -> p h n", h=HEADS),
                                        ps[7][:, :].rearrange("p (h n) -> p h n", h=HEADS),
                                        dw[:, c, HEADS:2 * HEADS].unsqueeze(2).broadcast_to([P, HEADS, STATE]),
                                        ALU.mult).then_inc(Bw_ready, 1)

                def masked(c):
                    for s in range(2):
                        dve.wait_ge(sc_filled, at(sc_filled, b, 2 * c + s + 1))
                        dve.wait_ge(Eg_ready, at(Eg_ready, b, 2 * c + s + 1))
                        v.tensor_tensor(Mt[:, c % 2, s * HALF:(s + 1) * HALF], ps[2 + s][:, :],
                                        Eg[:, s * HALF:(s + 1) * HALF], ALU.mult).then_inc(Mt_ready, 1)

                def state(c):
                    dve.wait_ge(s_filled, at(s_filled, b, c + 1))
                    if c:
                        dve.wait_ge(Sdc_ready, at(Sdc_ready, b, c))
                        dve.wait_ge(y_filled, at(y_filled, b, c + 1))
                    for hh in range(2):
                        q = slice(64 * hh, 64 * hh + 64)
                        src = ps[5][q, :].rearrange("p (k n) -> p k n", k=KC)[:, :, q]
                        if c:
                            ins = v.tensor_tensor(Sbd[q, :, q], src, Sdc[q, :, q], ALU.add)
                        else:
                            ins = v.tensor_copy(Sbd[q, :, q], src)
                    ins.then_inc(S_ready, 1)

                def skip(c):
                    dve.wait_ge(y_filled, at(y_filled, b, c + 1))
                    for k in range(KC):
                        s = xT[:, k, c * P:(c + 1) * P]
                        ins = v.scalar_tensor_tensor(s, s, cols_s[:, k, 5:6], ps[4][:, k * P:(k + 1) * P],
                                                     ALU.mult, ALU.add)
                    ins.then_inc(y_ready, 1)

                def y_stats(half):
                    dve.wait_ge(y_ready, at(y_ready, b, 4 * half + 4))
                    for k in range(KC):
                        ins = v.bn_stats(yst[:, k, 6 * half:6 * half + 6], xT[:, k, half * HALF:(half + 1) * HALF])
                    chS(dve, b, ins)

                if later(b):
                    dve.wait_ge(so_ready, at(so_ready, b - 1, 1))
                v.memset(Sbd[0:64, 0, 64:128], 0.0)
                chS(dve, b, v.memset(Sbd[64:128, 0, 0:64], 0.0))
                weigh(0)
                masked(0)
                for c in range(T):
                    if c + 1 < T:
                        weigh(c + 1)
                    if c == 5 and not last:
                        ln_var(b + 1)
                    if c < T - 1:
                        state(c)
                    else:
                        y_stats(0)
                    skip(c)
                    if c + 1 < T:
                        masked(c + 1)
                    if c == 4 and not last:
                        mod_column(b + 1)
                        ln_stats(b + 1)
                y_stats(1)
                chS.end()

            def out_(b):
                take_waits()
                for k in range(KC):
                    ins = v.bn_aggr(ymv[:, k, :], yst[:, k, :])
                chG(dve, b, ins)
                v.tensor_copy(pk[:, 0, :], ymv[:, :, 0])
                chG(dve, b, v.tensor_tensor(pk[:, 1, :], ymv[:, :, 0], ymv[:, :, 0], ALU.mult))
                v.tensor_tensor(pk[:, 1, :], pk[:, 1, :], ymv[:, :, 1], ALU.add).then_inc(pk_ready, 1)
                dve.wait_ge(pk_filled, at(pk_filled, b, 1))
                chG(dve, b, v.tensor_copy(pk[:, 2:4, :], ps[4][:, 0:2 * KC].rearrange("p (a n) -> p a n", a=2)))
                chG(dve, b, v.tensor_tensor(gab[:, 0, :], pk[:, 2, :], pk[:, 2, :], ALU.mult))
                chG(dve, b, v.tensor_tensor(gab[:, 0, :], pk[:, 3, :], gab[:, 0, :], ALU.subtract))
                v.tensor_scalar(gab[:, 0, :], gab[:, 0, :], EPS, None, ALU.add).then_inc(gvar_ready, 1)
                dve.wait_ge(grstd_ready, at(grstd_ready, b, 1))
                chG(dve, b, v.tensor_tensor(gab[:, 2, :], gab[:, 1, :], cols_s[:, :, 6], ALU.mult))
                chG(dve, b, v.tensor_tensor(gab[:, 3, :], pk[:, 2, :], gab[:, 2, :], ALU.mult))
                chG(dve, b, v.tensor_tensor(gab[:, 3, :], cols_s[:, :, 7], gab[:, 3, :], ALU.subtract))
                for half in range(2):
                    for k in range(KC):
                        s = xT[:, k, half * HALF:(half + 1) * HALF]
                        v.tensor_scalar(s, s, gab[:, 2, k:k + 1], gab[:, 3, k:k + 1], ALU.mult, ALU.add
                                        ).then_inc(yn_ready, 1)
                    for k in (2, 3):
                        s = xT[:, k, half * HALF:(half + 1) * HALF]
                        dve.wait_ge(yn_ready, at(yn_ready, b, half * KC + k + 1))
                        v.tensor_tensor(s, s, zs[:, k, half * HALF:(half + 1) * HALF], ALU.mult
                                        ).then_inc(gd_ready, 1)
                dve.wait_ge(modrow_loaded, at(modrow_loaded, b, 16))
                chG(dve, b, v.tensor_tensor_reduce(out=junkd[:, 0, :], in0=modrow[:, 1, :], in1=rw_s[:, :], scale=1.0,
                                                   scalar=0.0, op0=ALU.mult, op1=ALU.add, accum_out=c0[:, :]))
                v.tensor_scalar(c0[:, :], c0[:, :], rb_s[:, :], None, ALU.add).then_inc(c0_ready, 1)
                dve.wait_ge(xr_loaded, at(xr_loaded, b, 16))
                dve.wait_ge(rows2_ready, at(rows2_ready, b, 1))
                for step in range(6):
                    if step < 4:
                        residual(b, step)
                    if 1 <= step < 5:
                        second_norm(b, step - 1)
                    if step >= 2:
                        router(b, step - 2)
                dve.wait_ge(w_ready, at(w_ready, b, T))
                dve.wait_ge(c0_ready, at(c0_ready, b, 1))
                v.tensor_scalar(wcol[:, :], wcol[:, :], c0[:, :], None, ALU.add).then_inc(wcol_ready, 1)
                chG.end()

            def residual(b, j):
                q = slice(2 * j, 2 * j + 2)
                dve.wait_ge(out_filled, at(out_filled, b, j + 1))
                v.tensor_tensor(xr[:, q, :], xr[:, q, :], ps[4 + j][:, :].rearrange("p (t n) -> p t n", t=2),
                                ALU.add).then_inc(x1_ready, 1)
                dve.wait_ge(x1_ready, at(x1_ready, b, j + 1))
                for t in (2 * j, 2 * j + 1):
                    ins = v.bn_stats(st6b[:, t, :], xr[:, t, :])
                chG(dve, b, ins)
                take_waits()
                for t in (2 * j, 2 * j + 1):
                    ins = v.bn_aggr(mvb[:, t, :], st6b[:, t, :])
                chG(dve, b, ins)
                v.tensor_scalar(rstdb[:, q], mvb[:, q, 1], EPS, None, ALU.add).then_inc(var2_ready, 1)

            def second_norm(b, j):
                dve.wait_ge(rstd2_ready, at(rstd2_ready, b, j + 1))
                for t in (2 * j, 2 * j + 1):
                    v.tensor_scalar(h2[:, t, :], xr[:, t, :], mvb[:, t, 0:1], rstdb[:, t:t + 1],
                                    ALU.subtract, ALU.mult).then_inc(hn2_ready, 1)

            def router(b, j):
                dve.wait_ge(hn2_ready, at(hn2_ready, b, 2 * j + 2))
                if j:
                    dve.wait_ge(w_ready, at(w_ready, b, 2 * j))
                for t in (2 * j, 2 * j + 1):
                    v.tensor_tensor_reduce(out=junkd[:, t % 2, :], in0=h2[:, t, :], in1=rwc, scale=1.0,
                                           scalar=0.0, op0=ALU.mult, op1=ALU.add,
                                           accum_out=wcol[:, t:t + 1]).then_inc(w_ready, 1)

            def ffn_rank(b):
                dve.wait_ge(*ffn.read(b, F_WROW + 1))
                for t in range(T):
                    ins = v.scalar_tensor_tensor(Pm[:, t, :], wrow[:, t * P:(t + 1) * P], wcol[:, t:t + 1],
                                                 tri[:, :], ALU.is_equal, ALU.mult)
                chR(dve, b, ins)
                for t in range(T):
                    hi_ = (t + 1) * P
                    wj = wcol[:, t:t + 1]
                    if t < T - 1:
                        v.tensor_scalar(Gt[t][:, P:], wrow[:, hi_:L], wj, None, ALU.is_le, ALU.add,
                                        accum_out=above[:, t:t + 1])
                    v.scalar_tensor_tensor(Gt[t][:, 0:P], wrow[:, t * P:hi_], wj, Pm[:, t, :],
                                           ALU.is_lt, ALU.add).then_inc(G_ready, 1)

            def ffn_onehot(b):
                dve.wait_ge(G_ready, at(G_ready, b, T))
                chR(dve, b, v.tensor_tensor(rank[:, :], tokens_after[:, :], above[:, :], ALU.subtract))
                dve.wait_ge(*ffn.full(b, F_RANK))
                v.tensor_tensor(rank[:, :], rank[:, :], ffn.bank(F_RANK)[:, 0:T], ALU.add
                                ).then_inc(ffn.drained[F_RANK % 4], 1)
                dve.wait_ge(*ffn.read(b, F_RANK))
                for t in range(T):
                    v.tensor_scalar(Pm[:, t, :], iota_r[:, :], rank[:, t:t + 1], None, ALU.is_equal
                                    ).then_inc(P_ready, 1)

            def ffn_pick(b):
                v.tensor_scalar(moff[:, :], boff[:, :], float((MB - 1) * L), None, ALU.min)
                dve.wait_ge(*ffn.full(b, F_IDX))
                bank = ffn.bank(F_IDX)
                ins = v.tensor_copy(picked[:, 0:1], bank[:, 0:1])
                ins.then_inc(ffn.drained[F_IDX % 4], 1)
                dve.wait_ge(*ffn.read(b, F_IDX))
                v.tensor_copy(xidx[:, :], picked[:, 0:1])
                v.tensor_scalar(gidx[:, :], picked[:, 0:1], boff[:, :], None, ALU.add)
                v.tensor_scalar(midx[:, :], picked[:, 0:1], moff[:, :], None, ALU.add).then_inc(gidx_ready, 1)
                dve.wait_ge(gidx_ready, at(gidx_ready, b, 1))
                chR(dve, b, v.tensor_scalar(boff[:, :], boff[:, :], float(L), None, ALU.add))

            def ffn_norm(b):
                dve.wait_ge(xs_loaded, at(xs_loaded, b, 16))
                chR(dve, b, v.bn_stats(st1[:, :], xs))
                take_waits()
                chR(dve, b, v.bn_aggr(sm[:, 8:10], st1[:, :]))
                v.tensor_scalar(sm[:, 0:1], sm[:, 9:10], EPS, None, ALU.add).then_inc(fv_ready, 1)
                dve.wait_ge(m_loaded, at(m_loaded, b, 16))
                v.tensor_scalar(mrows, mrows, -3e38, None, ALU.max).then_inc(mclamp_ready, 1)
                dve.wait_ge(fr_ready, at(fr_ready, b, 1))
                chR(dve, b, v.tensor_scalar(hs, xs, sm[:, 8:9], sm[:, 1:2], ALU.subtract, ALU.mult))
                chR(dve, b, v.tensor_tensor(hs, hs, modrow[:, 2, :], ALU.mult))
                chR(dve, b, v.tensor_tensor(hs, hs, modrow[:, 1, :], ALU.add))
                chR(dve, b, v.tensor_tensor_reduce(out=junk, in0=hs, in1=hs, scale=1.0, scalar=0.0, op0=ALU.mult,
                                                   op1=ALU.add, accum_out=sm[:, 10:11]))
                v.tensor_scalar(sm[:, 2:3], sm[:, 10:11], 1.0 / D, 1e-6, ALU.mult, ALU.add).then_inc(fs_ready, 1)
                chR(dve, b, v.tensor_tensor_reduce(out=junk, in0=hs, in1=rw_s[:, :], scale=1.0, scalar=0.0,
                                                   op0=ALU.mult, op1=ALU.add, accum_out=sm[:, 11:12]))
                chR(dve, b, v.tensor_scalar(sm[:, 11:12], sm[:, 11:12], rb_s[:, :], None, ALU.add))
                dve.wait_ge(frr_ready, at(frr_ready, b, 1))
                v.tensor_scalar(hn, hs, sm[:, 3:4], None, ALU.mult).then_inc(hn_ready, 1)
                chR(dve, b, v.tensor_scalar(junkt, wrow[:, :], sm[:, 11:12], None, ALU.is_ge, ALU.add,
                                            accum_out=sm[:, 12:13]))
                chR(dve, b, v.tensor_scalar(sm[:, 13:14], sm[:, 12:13], KSEL - 0.5, None, ALU.is_ge))
                dve.wait_ge(pos_loaded, at(pos_loaded, b, 16))
                chR(dve, b, v.tensor_copy(posf[:, :], posi[:, :]))
                chR(dve, b, v.tensor_scalar(ang[:, :, :], invf[:, :, :], posf[:, :], None, ALU.mult))
                chR(dve, b, v.scalar_tensor_tensor(trn[:, :, :], ang[:, :, :], 1.0 / (2 * PI), phase[:, 0, :, :],
                                                   ALU.mult, ALU.add))
                chR(dve, b, v.tensor_scalar(trn[:, :, :], trn[:, :, :], ROUND, None, ALU.add))
                chR(dve, b, v.tensor_scalar(trn[:, :, :], trn[:, :, :], -ROUND, None, ALU.add))
                for part in TWO_PI:
                    chR(dve, b, v.scalar_tensor_tensor(ang[:, :, :], trn[:, :, :], -part, ang[:, :, :],
                                                       ALU.mult, ALU.add))
                chR(dve, b, v.tensor_tensor(ang[:, :, :], ang[:, :, :], phase[:, 1, :, :], ALU.add))
                v.tensor_scalar(ang[:, :, :], ang[:, :, :], -3.1415925, 3.1415925, ALU.max, ALU.min
                                ).then_inc(ang_ready, 1)

            def ffn_maskT(b):
                for j in range(2):
                    dve.wait_ge(*ffn.full(b, F_MT + j))
                    v.tensor_copy(mT[:, 4 * j:4 * j + 4, :].rearrange("p t n -> p (t n)"), ffn.bank(F_MT + j)[:, :]
                                  ).then_inc(ffn.drained[(F_MT + j) % 4], 1)

            def ffn_rope(b):
                dve.wait_ge(base_stored, at(base_stored, b, 64))
                dve.wait_ge(*ffn.full(b, F_QK))
                bank = ffn.bank(F_QK)
                ins = v.tensor_copy(qk, bank[:, :])
                ins.then_inc(ffn.drained[F_QK % 4], 1)
                dve.wait_ge(*ffn.read(b, F_QK))
                dve.wait_ge(sin_ready, at(sin_ready, b, 1))
                dve.wait_ge(qkz_ready, at(qkz_ready, b, 1))
                q4 = qk.rearrange("p (h a n) -> p h a n", a=2, n=HD // 2)
                r4 = rt.rearrange("p (h a n) -> p h a n", a=2, n=HD // 2)
                sinb = sc_[:, 0:1, :].broadcast_to([P, 2 * FH, HD // 2])
                cosb = sc_[:, 1:2, :].broadcast_to([P, 2 * FH, HD // 2])
                v.scalar_tensor_tensor(r4[:, :, 0, :], q4[:, :, 1, :], -1.0, sinb, ALU.mult, ALU.mult)
                chR(dve, b, v.tensor_tensor(r4[:, :, 1, :], q4[:, :, 0, :], sinb, ALU.mult))
                v.tensor_tensor(q4[:, :, 0, :], q4[:, :, 0, :], cosb, ALU.mult)
                chR(dve, b, v.tensor_tensor(q4[:, :, 1, :], q4[:, :, 1, :], cosb, ALU.mult))
                v.tensor_tensor(qkr[:, :, :, 0:HD].rearrange("p s h n -> p (s h) n"),
                                qk.rearrange("p (h n) -> p h n", n=HD),
                                rt.rearrange("p (h n) -> p h n", n=HD), ALU.add).then_inc(rope_ready, 1)
                dve.wait_ge(*ffn.full(b, F_MSEL))
                v.tensor_copy(msel, ffn.bank(F_MSEL)[:, 0:P]).then_inc(ffn.drained[F_MSEL % 4], 1)

            def ffn_scores(b):
                dve.wait_ge(*ffn.read(b, F_MSEL))
                for r in range(4):
                    q, h = F_SC + r, slice(4 * r, 4 * r + 4)
                    dve.wait_ge(*ffn.full(b, q))
                    v.scalar_tensor_tensor(scr[:, h, 0:NSEL],
                                           ffn.bank(q)[:, :].rearrange("p (m n) -> p m n", m=4)[:, :, 0:NSEL],
                                           float(HD) ** -0.5, msel[:, 0:NSEL].unsqueeze(1).broadcast_to([P, 4, NSEL]),
                                           ALU.mult, ALU.add).then_inc(ffn.drained[q % 4], 1)
                    dve.wait_ge(*ffn.read(b, q))
                    chR(dve, b, v.tensor_reduce(mx[:, h], scr[:, h, 0:NSEL], AX.X, ALU.max))
                    v.tensor_scalar(mx[:, h], mx[:, h], -1.0, None, ALU.mult).then_inc(mx_ready, 1)

            def ffn_o(b):
                dve.wait_ge(prob_ready, at(prob_ready, b, FH))
                chR(dve, b, v.reciprocal(den[:, :], den[:, :]))
                q = F_AV
                dve.wait_ge(*ffn.full(b, q))
                bank = ffn.bank(q)
                ins = v.tensor_tensor(ob.rearrange("p (m r n) -> p r m n", m=4, r=4),
                                      bank[:, 0:D].rearrange("p (m r n) -> p r m n", m=4, r=4),
                                      den[:, :].rearrange("p (r m) -> p r m", r=4).unsqueeze(3)
                                      .broadcast_to([P, 4, 4, HD]), ALU.mult)
                ins.then_inc(ffn.drained[q % 4], 1)

            def ffn_x1(b):
                q = F_WO
                dve.wait_ge(*ffn.full(b, q))
                bank = ffn.bank(q)
                ins = v.tensor_tensor(x1s, hs, bank[:, 0:D], ALU.add)
                ins.then_inc(ffn.drained[q % 4], 1)
                dve.wait_ge(*ffn.read(b, q))
                chR(dve, b, v.tensor_tensor_reduce(out=junk, in0=x1s, in1=x1s, scale=1.0, scalar=0.0, op0=ALU.mult,
                                                   op1=ALU.add, accum_out=sm[:, 10:11]))
                v.tensor_scalar(sm[:, 4:5], sm[:, 10:11], 1.0 / D, 1e-6, ALU.mult, ALU.add).then_inc(fs2_ready, 1)
                dve.wait_ge(frr2_ready, at(frr2_ready, b, 1))
                v.tensor_scalar(hn, x1s, sm[:, 5:6], None, ALU.mult).then_inc(hnb_ready, 1)

            def ffn_end(b):
                q = F_W2
                dve.wait_ge(*ffn.full(b, q))
                bank = ffn.bank(q)
                ins = v.tensor_tensor(x1s, x1s, bank[:, 0:D], ALU.add)
                ins.then_inc(ffn.drained[q % 4], 1)
                dve.wait_ge(*ffn.read(b, q))
                chR(dve, b, v.tensor_scalar(x1s, x1s, sm[:, 11:12], None, ALU.mult))
                chR(dve, b, v.scalar_tensor_tensor(x1s, hs, sm[:, 13:14], x1s, ALU.mult, ALU.add))
                chR(dve, b, v.tensor_tensor(x1s, x1s, modrow[:, 3, :], ALU.mult))
                v.tensor_tensor(x1s, x1s, xs, ALU.add).then_inc(so_ready, 1)
                chR.end()

            def batch(b, f, last=False):
                if f is not None:
                    out_(f)
                conv_first_half(b)
                if f is not None:
                    ffn_rank(f)
                conv(b, 1, 0)
                if f is not None:
                    ffn_onehot(f)
                conv(b, 1, 1)
                chV.end()
                if f is not None:
                    ffn_pick(f)
                    ffn_norm(f)
                if f is not None:
                    ffn_maskT(f)
                softplus_in(b)
                if f is not None:
                    ffn_rope(f)
                decay_rows(b)
                if f is not None:
                    ffn_scores(f)
                decay_operands(b)
                if f is not None:
                    ffn_o(f)
                dw_copy(b)
                if f is not None:
                    ffn_x1(f)
                    ffn_end(f)
                else:
                    fold_ln()
                scan(b, last)

            batch(0, None)
            with dve.Fori(1, NB - 1) as b:
                batch(b, b - 1)
            batch(NB - 1, NB - 2, last=True)
            f = NB - 1
            out_(f)
            ffn_rank(f)
            ffn_onehot(f)
            ffn_pick(f)
            ffn_norm(f)
            ffn_maskT(f)
            ffn_rope(f)
            ffn_scores(f)
            ffn_o(f)
            ffn_x1(f)
            ffn_end(f)

        @block.tensor
        def _(pe):
            t_ = nc.tensor
            def modulation(j):
                for k in range(KD):
                    ins = t_.matmul(ps[4 + j][0:NB, :], mcin[:, k, :], wmod_s[:, k, j * 512:(j + 1) * 512],
                                    start=k == 0, stop=k == KD - 1)
                ins.then_inc(setup_pe, 1)

            pe.wait_ge(mload, 32)
            pe.wait_ge(setup_act, 1)
            modulation(0)
            pe.wait_ge(setup_dve, 1)
            pe.wait_ge(setup_pool, 2)
            for j in range(4):
                ins = t_.transpose(ps[7][:, j * NB:(j + 1) * NB], mod8[:, j * P:(j + 1) * P], ident[0:NB, 0:NB])
            ins.then_inc(setup_pe, 1)
            pe.wait_ge(mload2, 16)
            modulation(1)
            modulation(2)

            def ln_in(b, half):
                if later(b):
                    if half == 0:
                        pe.wait_ge(Eg_ready, at(Eg_ready, b - 1, 2 * T))
                    else:
                        pe.wait_ge(Mt_ready, at(Mt_ready, b - 1, 2 * T))
                pe.wait_ge(xn_ready, at(xn_ready, b, 4 * half + 4))
                for k in range(KD):
                    q = J_H + half * KD + k
                    for i in range(4):
                        ins = t_.transpose(proj.bank(q)[:, i * P:(i + 1) * P],
                                           xin[:, 4 * half + i, k * P:(k + 1) * P], ident[:, :])
                    ins.then_inc(proj.filled[q % 4], 1)

            def project(b, q, w, m, rhs, nk, half, first=False):
                if q >= 4:
                    pe.wait_ge(*proj.read(b, q - 4))
                bank = proj.bank(q)
                for k in range(nk):
                    if first and k % 2 == 0:
                        pe.wait_ge(xT_ready, at(xT_ready, b, 4 * half + k + 2))
                    ins = t_.matmul(bank[:, :], w[:, k, m * P:(m + 1) * P],
                                    rhs[:, k, half * HALF:(half + 1) * HALF], start=k == 0, stop=k == nk - 1)
                ins.then_inc(proj.filled[q % 4], 1)

            def x_proj(b, half, ms):
                pe.wait_ge(*proj.read(b, J_H + (2 * half + 2) - 1))
                for m in ms:
                    project(b, J_X + half * KC + m, wx_s, m, hT, KD, half)

            def z_proj(b, half, ms):
                for m in ms:
                    project(b, J_Z + half * KC + m, wz_s, m, hT, KD, half)

            def dt_proj(b):
                pe.wait_ge(xT_ready, at(xT_ready, b, 8))
                for half in range(2):
                    pe.wait_ge(*proj.read(b, J_DT + half - 4))
                for k in range(KC):
                    for half in range(2):
                        q = J_DT + half
                        ins = t_.matmul(proj.bank(q)[64 * half:64 * half + RW, :], wdt_s[:, k, :],
                                        xT[:, k, half * HALF:(half + 1) * HALF], start=k == 0, stop=k == KC - 1)
                        if k == KC - 1:
                            ins.then_inc(proj.filled[q % 4], 1)

            def bc_proj(b, half, ms):
                for m in ms:
                    project(b, J_BC[half][m], wb_s if m < KC else wc_s, m % KC, xT, KC, half, first=m == 0)

            def decay_jobs(b):
                q = J_V
                if q >= 4:
                    pe.wait_ge(*proj.read(b, q - 4))
                bank = proj.bank(q)
                pe.wait_ge(v_ready, at(v_ready, b, 1))
                t_.matmul(bank[:, 0:1], identb[:, :], ones_b[:, :], start=True, stop=True)
                for t in range(T):
                    ins = t_.transpose(bank[:, t * RW:(t + 1) * RW], a48[:, t * P:(t + 1) * P], ident[0:RW, 0:RW])
                ins.then_inc(proj.filled[q % 4], 1)

            def carry_rows(b, half):
                pe.wait_ge(v_ready, at(v_ready, b, 1))
                for k in range(KC):
                    q = J_EC + half * KC + k
                    pe.wait_ge(*proj.read(b, q - 4))
                    t_.matmul(proj.bank(q)[:, :], selp[:, k, :], Lw[:, half * HALF:(half + 1) * HALF],
                              start=True, stop=True).then_inc(proj.filled[q % 4], 1)

            def output(b, c):
                if c or later(b):
                    pe.wait_ge(y_ready, at(y_ready, b, c))
                if c:
                    pe.wait_ge(S_ready, at(S_ready, b, c))
                    pe.wait_ge(CE_ready, at(CE_ready, b, 4 * (c // 4) + 4))
                    for k in range(KC):
                        t_.matmul(ps[4][:, k * P:(k + 1) * P], Sbd[:, k, :], ECv[:, k, c * P:(c + 1) * P],
                                  start=k == 0, stop=True, skip_group_check=k > 0)
                pe.wait_ge(Mt_ready, at(Mt_ready, b, 2 * c + 2))
                for h in range(HEADS):
                    k, hh = h // 2, h % 2
                    ins = t_.matmul(ps[4][64 * hh:64 * hh + 64, k * P:(k + 1) * P],
                                    XB[:, c % 2, 0, h * STATE:(h + 1) * STATE],
                                    Mt[:, c % 2, hh * HALF + k * P:hh * HALF + (k + 1) * P],
                                    start=c == 0, stop=True, skip_group_check=c > 0)
                ins.then_inc(y_filled, 1)

            def scan(b):
                def turn(c):
                    if c or later(b):
                        pe.wait_ge(Xd_ready, at(Xd_ready, b, c))
                    for k in range(KC):
                        ins = t_.transpose(ps[6][:, k * P:(k + 1) * P], xT[:, k, c * P:(c + 1) * P], ident[:, :])
                    ins.then_inc(xt_filled, 1)
                    if c < T - 1:
                        if c or later(b):
                            pe.wait_ge(Bw_ready, at(Bw_ready, b, c))
                        for k in range(KC):
                            ins = t_.transpose(ps[7][:, k * P:(k + 1) * P], BT[:, c // 4, k, chunk(c)],
                                               ident[:, :])
                        ins.then_inc(bt_filled, 1)

                def cumdiff(c):
                    for s in range(2):
                        if c or later(b):
                            pe.wait_ge(Eg_ready, at(Eg_ready, b, 2 * (c - 1) + s + 1 if c else 0))
                        t_.matmul(ps[s][:, :], identb[:, :], causal[:, :, :].rearrange("p a n -> p (a n)"),
                                  start=True, stop=False)
                        t_.matmul(ps[s][:, :], Lw[:, c * P:(c + 1) * P], R8[:, 4 * s:4 * s + 4, c * P:(c + 1) * P],
                                  start=False, stop=True).then_inc(cd_filled, 1)

                def scores(c):
                    if c or later(b):
                        pe.wait_ge(Mt_ready, at(Mt_ready, b, 2 * c))
                    for k in range(KC):
                        for s in range(2):
                            r = slice(64 * s, 64 * s + 64)
                            ins = t_.matmul(ps[2 + s][:, k * P:(k + 1) * P], BT[r, c // 4, k, chunk(c)],
                                            CT[r, c // 4, k, chunk(c)], start=True, stop=True)
                            if k == KC - 1:
                                ins.then_inc(sc_filled, 1)

                def state(c):
                    pe.wait_ge(Bw_ready, at(Bw_ready, b, c + 1))
                    pe.wait_ge(Xd_ready, at(Xd_ready, b, c + 1))
                    if c or later(b):
                        pe.wait_ge(S_ready, at(S_ready, b, c))
                    for h in range(HEADS):
                        r, o = slice(64 * (h % 2), 64 * (h % 2) + 64), slice(h * 64, h * 64 + 64)
                        ins = t_.matmul(ps[5][r, o], XB[:, c % 2, 1, o], XB[:, c % 2, 0, o], start=True, stop=True)
                    ins.then_inc(s_filled, 1)

                for i in range(4):
                    pe.wait_ge(proj.drained[i], at(proj.drained[i], b + 1, 0))
                pe.wait_ge(*proj.read(b, J_BC[1][7]))
                scores(0)
                pe.wait_ge(rows_ready, at(rows_ready, b, HEADS))
                cumdiff(0)
                if later(b):
                    for i in range(4):
                        pe.wait_ge(ffn.drained[i], at(ffn.drained[i], b - 1 + 1, 0))
                turn(0)
                for c in range(T - 1):
                    turn(c + 1)
                    cumdiff(c + 1)
                    state(c)
                    output(b, c)
                    scores(c + 1)

            def gn_stats(b):
                pe.wait_ge(pk_ready, at(pk_ready, b, 1))
                t_.matmul(ps[4][:, 0:2 * KC], halfmean[:, :], pk[:, 0:2, :].rearrange("p a n -> p (a n)"),
                          start=True, stop=True).then_inc(pk_filled, 1)

            def out_(b):
                pe.wait_ge(wog_ready, at(wog_ready, b, 1))
                for j in range(4):
                    pe.wait_ge(g_ready, at(g_ready, b, 2 * (j // 2) + 2))
                    pe.wait_ge(gd_ready, at(gd_ready, b, 2 * (j // 2) + 2))
                    for i in range(2):
                        t = 2 * j + i
                        for k in range(KC):
                            ins = t_.matmul(ps[4 + j][:, i * D:(i + 1) * D], xT[:, k, t * P:(t + 1) * P],
                                            wog_s[:, k, :], start=k == 0, stop=k == KC - 1)
                    ins.then_inc(out_filled, 1)

            def ffn_wrow(b):
                pe.wait_ge(wcol_ready, at(wcol_ready, b, 1))
                for j in range(2):
                    if F_WROW + j >= 4:
                        pe.wait_ge(*ffn.read(b, F_WROW + j - 4))
                    bank = ffn.bank(F_WROW + j)
                    for i in range(4):
                        ins = t_.transpose(bank[:, i * P:(i + 1) * P],
                                           wcol[:, 4 * j + i:4 * j + i + 1].broadcast_to([P, P]), ident[:, :])
                    ins.then_inc(ffn.filled[(F_WROW + j) % 4], 1)

            def ffn_rank(b):
                if F_RANK >= 4:
                    pe.wait_ge(*ffn.read(b, F_RANK - 4))
                bank = ffn.bank(F_RANK)
                pe.wait_ge(G_ready, at(G_ready, b, T))
                for s in range(T):
                    for t in range(s + 1):
                        ins = t_.matmul(bank[:, s:s + 1], Gt[t][:, (s - t) * P:(s - t + 1) * P], ones_b[:, :],
                                        start=t == 0, stop=t == s)
                ins.then_inc(ffn.filled[F_RANK % 4], 1)

            def ffn_idx(b):
                if F_IDX >= 4:
                    pe.wait_ge(*ffn.read(b, F_IDX - 4))
                bank = ffn.bank(F_IDX)
                pe.wait_ge(P_ready, at(P_ready, b, T))
                for t in range(T):
                    ins = t_.matmul(bank[:, 0:1], Pm[:, t, :], tok[:, t:t + 1], start=t == 0, stop=t == T - 1)
                ins.then_inc(ffn.filled[F_IDX % 4], 1)

            def ffn_turn(b, q, src):
                if q >= 4:
                    pe.wait_ge(*ffn.read(b, q - 4))
                bank = ffn.bank(q)
                for k in range(KD):
                    ins = t_.transpose(bank[:, k * P:(k + 1) * P], src[:, k * P:(k + 1) * P], ident[:, :])
                ins.then_inc(ffn.filled[q % 4], 1)

            def ffn_mask(b):
                pe.wait_ge(mclamp_ready, at(mclamp_ready, b, 1))
                for j in range(2):
                    if F_MT + j >= 4:
                        pe.wait_ge(*ffn.read(b, F_MT + j - 4))
                    bank = ffn.bank(F_MT + j)
                    for i in range(4):
                        t = 4 * j + i
                        ins = t_.transpose(bank[:, i * P:(i + 1) * P], mrows[:, t * P:(t + 1) * P], ident[:, :])
                    ins.then_inc(ffn.filled[(F_MT + j) % 4], 1)

            def ffn_msel(b):
                if F_MSEL >= 4:
                    pe.wait_ge(*ffn.read(b, F_MSEL - 4))
                bank = ffn.bank(F_MSEL)
                pe.wait_ge(*ffn.read(b, F_MT + 1))
                for t in range(T):
                    ins = t_.matmul(bank[:, 0:P], mT[:, t, :], Pm[:, t, :], start=t == 0, stop=t == T - 1)
                ins.then_inc(ffn.filled[F_MSEL % 4], 1)

            def ffn_qkv(b):
                pe.wait_ge(*ffn.read(b, F_HNT))
                for q, o, w in ((F_QK, 0, 2 * D), (F_V, 2 * D, D)):
                    if q >= 4:
                        pe.wait_ge(*ffn.read(b, q - 4))
                    bank = ffn.bank(q)
                    for k in range(KD):
                        ins = t_.matmul(bank[:, 0:w], hnT[:, k, :], wqkv_s[:, k, o:o + w],
                                        start=k == 0, stop=k == KD - 1)
                    ins.then_inc(ffn.filled[q % 4], 1)

            def ffn_qT(b):
                pe.wait_ge(rope_ready, at(rope_ready, b, 1))
                for s in range(2):
                    if F_QT + s >= 4:
                        pe.wait_ge(*ffn.read(b, F_QT + s - 4))
                    bank = ffn.bank(F_QT + s)
                    for m in range(4):
                        ins = t_.transpose(bank[:, m * P:(m + 1) * P],
                                           qkr[:, s, 4 * m:4 * m + 4, :].rearrange("p h n -> p (h n)"), ident[:, :])
                    ins.then_inc(ffn.filled[(F_QT + s) % 4], 1)

            def ffn_scores(b):
                pe.wait_ge(*ffn.read(b, F_KT))
                for r in range(4):
                    pe.wait_ge(*ffn.read(b, F_SC + r - 4))
                    q = slice(32 * r, 32 * r + 32)
                    for m in range(4):
                        ins = t_.matmul(ffn.bank(F_SC + r)[:, m * P:m * P + NSEL], qT[q, m, :], kT[q, m, 0:NSEL],
                                        start=True, stop=True)
                    ins.then_inc(ffn.filled[(F_SC + r) % 4], 1)

            def ffn_AT(b):
                for r in range(4):
                    if F_AT + r >= 4:
                        pe.wait_ge(*ffn.read(b, F_AT + r - 4))
                    bank = ffn.bank(F_AT + r)
                    pe.wait_ge(prob_ready, at(prob_ready, b, 4 * r + 4))
                    for m in range(4):
                        ins = t_.transpose(bank[0:NSEL, m * P:(m + 1) * P], scr[:, 4 * r + m, 0:NSEL], ident[:, :])
                    ins.then_inc(ffn.filled[(F_AT + r) % 4], 1)

            def ffn_av(b):
                if F_AV >= 4:
                    pe.wait_ge(*ffn.read(b, F_AV - 4))
                bank = ffn.bank(F_AV)
                pe.wait_ge(*ffn.read(b, F_V))
                for r in range(4):
                    pe.wait_ge(*ffn.read(b, F_AT + r))
                    for m in range(4):
                        o = (4 * m + r) * HD
                        ins = t_.matmul(bank[:, o:o + HD], AT[0:NSEL, 4 * r + m, :], vs[0:NSEL, o:o + HD],
                                        start=True, stop=True)
                ins.then_inc(ffn.filled[F_AV % 4], 1)

            def ffn_wo(b):
                if F_WO >= 4:
                    pe.wait_ge(*ffn.read(b, F_WO - 4))
                bank = ffn.bank(F_WO)
                pe.wait_ge(*ffn.read(b, F_OT))
                for k in range(KD):
                    ins = t_.matmul(bank[:, 0:D], oT[:, k, :], fwo_s[:, k, :], start=k == 0, stop=k == KD - 1)
                ins.then_inc(ffn.filled[F_WO % 4], 1)

            def ffn_w1(b):
                pe.wait_ge(*ffn.read(b, F_HNBT))
                for j in range(2):
                    if F_W1 + j >= 4:
                        pe.wait_ge(*ffn.read(b, F_W1 + j - 4))
                    bank = ffn.bank(F_W1 + j)
                    for i in range(4):
                        f = 4 * j + i
                        for k in range(KD):
                            ins = t_.matmul(bank[:, i * P:(i + 1) * P], w1_s[:, k, f * P:(f + 1) * P], hnT[:, k, :],
                                            start=k == 0, stop=k == KD - 1)
                    ins.then_inc(ffn.filled[(F_W1 + j) % 4], 1)

            def ffn_w2(b):
                if F_W2 >= 4:
                    pe.wait_ge(*ffn.read(b, F_W2 - 4))
                bank = ffn.bank(F_W2)
                pe.wait_ge(*ffn.read(b, F_W1 + 1))
                for f in range(FT):
                    ins = t_.matmul(bank[:, 0:D], gT[:, f, :], w2_s[:, f, :], start=f == 0, stop=f == FT - 1)
                ins.then_inc(ffn.filled[F_W2 % 4], 1)

            def batch(b, f):
                ln_in(b, 0)
                if f is not None:
                    output(f, T - 1)
                ln_in(b, 1)
                if f is None:
                    pe.wait_ge(wload, 16 * len(first_loads))
                x_proj(b, 0, range(3))
                if f is not None:
                    gn_stats(f)
                x_proj(b, 0, (3,))
                x_proj(b, 1, range(4))
                if f is not None:
                    out_(f)
                z_proj(b, 0, range(4))
                if f is not None:
                    ffn_wrow(f)
                z_proj(b, 1, range(4))
                if f is None:
                    pe.wait_ge(wload2, 16 * len(mixer_loads))
                    pe.wait_ge(setup_dve, SD_MIX)
                    pe.wait_ge(setup_pool, SP_ALL)
                    pe.wait_ge(setup_act, 6)
                bc_proj(b, 0, (0, 1, 2))
                if f is not None:
                    ffn_rank(f)
                bc_proj(b, 0, (3, 4, 5))
                if f is not None:
                    ffn_idx(f)
                bc_proj(b, 0, (6, 7))
                dt_proj(b)
                if f is not None:
                    pe.wait_ge(hn_ready, at(hn_ready, f, 1))
                    ffn_turn(f, F_HNT, hn)
                    ffn_mask(f)
                bc_proj(b, 1, (0,))
                if f is not None:
                    ffn_qkv(f)
                    ffn_msel(f)
                bc_proj(b, 1, (1,))
                if f is not None:
                    ffn_qT(f)
                bc_proj(b, 1, (2,))
                if f is not None:
                    ffn_scores(f)
                bc_proj(b, 1, (3, 4))
                if f is not None:
                    ffn_AT(f)
                bc_proj(b, 1, (5,))
                if f is not None:
                    ffn_av(f)
                decay_jobs(b)
                if f is not None:
                    pe.wait_ge(*ffn.read(f, F_AV))
                    ffn_turn(f, F_OT, ob)
                bc_proj(b, 1, (6,))
                if f is not None:
                    ffn_wo(f)
                bc_proj(b, 1, (7,))
                if f is not None:
                    pe.wait_ge(hnb_ready, at(hnb_ready, f, 1))
                    ffn_turn(f, F_HNBT, hn)
                carry_rows(b, 0)
                if f is not None:
                    ffn_w1(f)
                carry_rows(b, 1)
                if f is not None:
                    ffn_w2(f)
                scan(b)

            batch(0, None)
            pe.wait_ge(fload, 16 * len(ffn_loads))
            pe.wait_ge(setup_dve, SD_ALL)
            with pe.Fori(1, NB) as b:
                batch(b, b - 1)
            f = NB - 1
            output(f, T - 1)
            gn_stats(f)
            out_(f)
            ffn_wrow(f)
            ffn_rank(f)
            ffn_idx(f)
            pe.wait_ge(hn_ready, at(hn_ready, f, 1))
            ffn_turn(f, F_HNT, hn)
            ffn_mask(f)
            ffn_qkv(f)
            ffn_msel(f)
            ffn_qT(f)
            ffn_scores(f)
            ffn_AT(f)
            ffn_av(f)
            pe.wait_ge(*ffn.read(f, F_AV))
            ffn_turn(f, F_OT, ob)
            ffn_wo(f)
            pe.wait_ge(hnb_ready, at(hnb_ready, f, 1))
            ffn_turn(f, F_HNBT, hn)
            ffn_w1(f)
            ffn_w2(f)


def kernel(**inputs):
    import concourse.bacc as bacc
    import numpy as np
    from concourse.bass_utils import run_bass_kernel_spmd

    def arr(name):
        return np.asarray(inputs[name])

    def by_partition(w):
        return np.ascontiguousarray(w.reshape(-1, P, w.shape[-1]).transpose(1, 0, 2))

    rep = INNER // HEADS
    columns = np.concatenate([
        arr("L0_attn_conv_w")[:, 0, :], arr("L0_attn_conv_b")[:, None],
        np.repeat(arr("L0_attn_d_param"), rep)[:, None], arr("L0_attn_gn_w")[:, None],
        arr("L0_attn_gn_b")[:, None]], axis=1)
    lncols = np.stack([arr("L0_ffn_ln1").reshape(KD, P).T, arr("L0_ffn_ln2").reshape(KD, P).T], axis=1)
    arrays = {
        "x": arr("L0_attn_input_tensor"),
        "wxT": arr("L0_attn_Wx").T, "wzT": arr("L0_attn_Wz").T, "wbT": arr("L0_attn_Wb").T,
        "wcT": arr("L0_attn_Wc").T, "wdtT": np.tile(arr("L0_attn_Wdt").T, (1, G3)), "woT": arr("L0_attn_Wout").T,
        "cols": by_partition(columns),
        "rows48": np.tile(np.stack([arr("L0_attn_b_dt"), arr("L0_attn_log_a")], axis=1), (G3, 1)),
        "mask": arr("L0_ffn_attention_mask").reshape(MB * L, L),
        "pos": arr("L0_ffn_position_ids").reshape(MB * L, 1),
        "rw": arr("L0_ffn_router_w").reshape(D), "rb": arr("L0_ffn_router_b"),
        "wqkv": np.concatenate([arr("L0_ffn_wq"), arr("L0_ffn_wk"), arr("L0_ffn_wv")], axis=1),
        "wo": arr("L0_ffn_wo"), "w1": arr("L0_ffn_w1"), "w2": arr("L0_ffn_w2"), "lncols": lncols,
        "cT": arr("L0_c").T, "wmod": arr("L0_wmod"),
    }
    nc = bacc.Bacc("TRN2", target_bir_lowering=False, num_devices=1)
    aps = {}
    for name, a in arrays.items():
        arrays[name] = a = np.ascontiguousarray(a)
        aps[name] = nc.dram_tensor(name, a.shape, mybir.dt.from_np(a.dtype), kind="ExternalInput").ap()
    out = nc.dram_tensor("out", (NB * L, D), F32, kind="ExternalOutput").ap()
    adaln_block(nc, out=out, **aps)
    result = run_bass_kernel_spmd(nc, [arrays], core_ids=[0])
    return result.results[0]["out"].reshape(NB, L, D)
```
